# Optimizing a Trainium2 kernel written in Bass

```python
import numpy as np
import jax
import jax.numpy as jnp

def _softmax(x, axis=-1):
    return jax.nn.softmax(x, axis=axis)

def _gelu(x):
    return jax.nn.gelu(x, approximate=True)

def _silu(x):
    return jax.nn.silu(x)

def _sigmoid(x):
    return jax.nn.sigmoid(x)

def _layernorm(x, axis=-1, eps=1e-05):
    m = jnp.mean(x, axis=axis, keepdims=True)
    v = jnp.var(x, axis=axis, keepdims=True)
    return (x - m) / jnp.sqrt(v + eps)

def _scatter_add(tgt, idx, src, axis=0):
    return tgt.at[idx].add(src)

def _segment_sum(src, seg, n):
    return jax.ops.segment_sum(src, seg, n)
kernel_name = 'mk_seq_postln_d1_jaxref_r4_c586da'

def setup_inputs(seed: int=0):
    np.random.seed(seed)
    _w = jnp.asarray

    def _L0_attn_setup():
        import jax, jax.numpy as jnp
        import numpy as np
        D_MODEL = 256
        N_HEADS = 16
        HEAD_DIM = D_MODEL // N_HEADS
        key = jax.random.key(seed)
        k1, k2, k3 = jax.random.split(key, 3)
        B, S = (4, 512)
        x = jax.random.normal(k1, (B, S, D_MODEL), dtype=jnp.float32)
        w_qkv = jax.random.normal(k2, (D_MODEL, 3 * D_MODEL), dtype=jnp.float32) / np.sqrt(D_MODEL)
        b_qkv = jnp.zeros((3 * D_MODEL,), dtype=jnp.float32)
        w_out = jax.random.normal(k3, (D_MODEL, D_MODEL), dtype=jnp.float32) / np.sqrt(D_MODEL)
        b_out = jnp.zeros((D_MODEL,), dtype=jnp.float32)
        return {'x': x, 'w_qkv': w_qkv, 'b_qkv': b_qkv, 'w_out': w_out, 'b_out': b_out}
    _L0_attn_in = _L0_attn_setup()

    def _L0_ffn_setup():
        import jax, jax.numpy as jnp
        import numpy as np
        DIM = 256
        DEPTH = 2
        HEADS = 8
        DIM_HEAD = 64
        WINDOW = 128
        INNER = HEADS * DIM_HEAD
        HID = int(DIM * 4 * 2 / 3)
        B, N = (2, 2048)
        QK_SCALE = 8.0

        def shift_token(t):
            t1, t2 = jnp.split(t, 2, axis=-1)
            t2 = jnp.pad(t2, ((0, 0), (1, 0), (0, 0)))[:, :-1]
            return jnp.concatenate([t1, t2], axis=-1)

        def l2norm(t):
            return t / jnp.clip(jnp.linalg.norm(t, axis=-1, keepdims=True), 1e-12)

        def rotate_half(x):
            x1, x2 = jnp.split(x, 2, axis=-1)
            return jnp.concatenate([-x2, x1], axis=-1)

        def rotary_xpos(q, k):
            n = q.shape[-2]
            half_idx = jnp.arange(0, DIM_HEAD, 2, dtype=jnp.float32)
            inv_freq = 1.0 / 10000.0 ** (half_idx / DIM_HEAD)
            t = jnp.arange(n, dtype=jnp.float32)
            freqs = t[:, None] * inv_freq[None, :]
            freqs = jnp.concatenate([freqs, freqs], axis=-1)
            base = (half_idx + 0.4 * DIM_HEAD) / (1.4 * DIM_HEAD)
            power = (t - n // 2) / float(WINDOW // 2)
            scale = base[None, :] ** power[:, None]
            scale = jnp.concatenate([scale, scale], axis=-1)
            cos, sin = (jnp.cos(freqs), jnp.sin(freqs))
            q = q * cos * scale + rotate_half(q) * sin * scale
            k = k * cos / scale + rotate_half(k) * sin / scale
            return (q, k)

        def local_attention(q, k, v):
            b, h, n, d = q.shape
            w = n // WINDOW
            bq = q.reshape(b, h, w, WINDOW, d) * QK_SCALE
            bk = k.reshape(b, h, w, WINDOW, d)
            bv = v.reshape(b, h, w, WINDOW, d)

            def look_around(t):
                p = jnp.pad(t, ((0, 0), (0, 0), (1, 0), (0, 0), (0, 0)))
                return jnp.concatenate([p[:, :, :w], p[:, :, 1:]], axis=3)
            bk, bv = (look_around(bk), look_around(bv))
            bt = jnp.arange(n).reshape(w, WINDOW)
            btp = jnp.pad(bt, ((1, 0), (0, 0)), constant_values=-1)
            btk = jnp.concatenate([btp[:w], btp[1:]], axis=1)
            sim = jnp.einsum('bhwid,bhwjd->bhwij', bq, bk)
            i = bt[:, :, None]
            j = btk[:, None, :]
            mask = (i < j) | (i > j + WINDOW) | (j == -1)
            sim = jnp.where(mask, -jnp.finfo(sim.dtype).max, sim)
            attn = jax.nn.softmax(sim, axis=-1)
            out = jnp.einsum('bhwij,bhwjd->bhwid', attn, bv)
            return out.reshape(b, h, n, d)

        def _layer(x, wqkv, qs, ksc, wo, lg, lb, w1, b1, w2, b2):
            b, n, _ = x.shape
            h = shift_token(x)
            qkv = h @ wqkv
            q, k, v = jnp.split(qkv, 3, axis=-1)
            to_heads = lambda t: t.reshape(b, n, HEADS, DIM_HEAD).transpose(0, 2, 1, 3)
            q, k, v = (to_heads(q), to_heads(k), to_heads(v))
            q = l2norm(q) * qs
            k = l2norm(k) * ksc
            q, k = rotary_xpos(q, k)
            o = local_attention(q, k, v)
            o = o.transpose(0, 2, 1, 3).reshape(b, n, INNER)
            x = x + o @ wo
            h = shift_token(x)
            mu = h.mean(-1, keepdims=True)
            var = h.var(-1, keepdims=True)
            h = (h - mu) / jnp.sqrt(var + 1e-05) * lg + lb
            h = h @ w1 + b1
            a, g = jnp.split(h, 2, axis=-1)
            h = a * jax.nn.gelu(g, approximate=False)
            x = x + h @ w2 + b2
            return x
        key = jax.random.key(seed)
        ks = jax.random.split(key, 6)
        return {'x': jax.random.normal(ks[0], (B, N, DIM), jnp.float32), 'wqkv': jax.random.normal(ks[1], (DEPTH, DIM, 3 * INNER), jnp.float32) * 0.02, 'q_scale': jnp.ones((DEPTH, DIM_HEAD), jnp.float32), 'k_scale': jnp.ones((DEPTH, DIM_HEAD), jnp.float32), 'wo': jax.random.normal(ks[2], (DEPTH, INNER, DIM), jnp.float32) * 0.02, 'ln_g': jnp.ones((DEPTH, DIM), jnp.float32), 'ln_b': jnp.zeros((DEPTH, DIM), jnp.float32), 'w1': jax.random.normal(ks[3], (DEPTH, DIM, 2 * HID), jnp.float32) * 0.02, 'b1': jnp.zeros((DEPTH, 2 * HID), jnp.float32), 'w2': jax.random.normal(ks[4], (DEPTH, HID, DIM), jnp.float32) * 0.02, 'b2': jnp.zeros((DEPTH, DIM), jnp.float32)}
    _L0_ffn_in = _L0_ffn_setup()
    _d = {'L0_attn_x': _L0_attn_in['x'], 'L0_attn_w_qkv': _L0_attn_in['w_qkv'], 'L0_attn_b_qkv': _L0_attn_in['b_qkv'], 'L0_attn_w_out': _L0_attn_in['w_out'], 'L0_attn_b_out': _L0_attn_in['b_out'], 'L0_ffn_wqkv': _L0_ffn_in['wqkv'], 'L0_ffn_q_scale': _L0_ffn_in['q_scale'], 'L0_ffn_k_scale': _L0_ffn_in['k_scale'], 'L0_ffn_wo': _L0_ffn_in['wo'], 'L0_ffn_ln_g': _L0_ffn_in['ln_g'], 'L0_ffn_ln_b': _L0_ffn_in['ln_b'], 'L0_ffn_w1': _L0_ffn_in['w1'], 'L0_ffn_b1': _L0_ffn_in['b1'], 'L0_ffn_w2': _L0_ffn_in['w2'], 'L0_ffn_b2': _L0_ffn_in['b2']}
    _x0 = _d['L0_attn_x']
    _d['L0_attn_x'] = jax.random.normal(jax.random.fold_in(jax.random.key(seed), 1), (8, 512, 256), dtype=_x0.dtype)
    del _x0
    return _d

def reference(L0_attn_x, L0_attn_w_qkv, L0_attn_b_qkv, L0_attn_w_out, L0_attn_b_out, L0_ffn_wqkv, L0_ffn_q_scale, L0_ffn_k_scale, L0_ffn_wo, L0_ffn_ln_g, L0_ffn_ln_b, L0_ffn_w1, L0_ffn_b1, L0_ffn_w2, L0_ffn_b2):

    def _L0_attn_ref(x, w_qkv, b_qkv, w_out, b_out):
        import jax, jax.numpy as jnp
        import numpy as np
        D_MODEL = 256
        N_HEADS = 16
        HEAD_DIM = D_MODEL // N_HEADS
        B, S, D = x.shape
        qkv = x @ w_qkv + b_qkv
        q, k, v = jnp.split(qkv, 3, axis=-1)

        def split_heads(t):
            return t.reshape(B, S, N_HEADS, HEAD_DIM).transpose(0, 2, 1, 3)
        q, k, v = (split_heads(q), split_heads(k), split_heads(v))
        a = jnp.einsum('bhsd,bhtd->bhst', q, k)
        causal_mask = jnp.triu(jnp.full((S, S), -jnp.inf, dtype=a.dtype), k=1)
        a = (a + causal_mask) / np.sqrt(HEAD_DIM)
        a = jax.nn.softmax(a, axis=-1)
        z = jnp.einsum('bhst,bhtd->bhsd', a, v)
        z = z.transpose(0, 2, 1, 3).reshape(B, S, D)
        return z @ w_out + b_out

    def _L0_ffn_ref(x, wqkv, q_scale, k_scale, wo, ln_g, ln_b, w1, b1, w2, b2):
        import jax, jax.numpy as jnp
        import numpy as np
        DIM = 256
        DEPTH = 2
        HEADS = 8
        DIM_HEAD = 64
        WINDOW = 128
        INNER = HEADS * DIM_HEAD
        HID = int(DIM * 4 * 2 / 3)
        B, N = (2, 2048)
        QK_SCALE = 8.0

        def shift_token(t):
            t1, t2 = jnp.split(t, 2, axis=-1)
            t2 = jnp.pad(t2, ((0, 0), (1, 0), (0, 0)))[:, :-1]
            return jnp.concatenate([t1, t2], axis=-1)

        def l2norm(t):
            return t / jnp.clip(jnp.linalg.norm(t, axis=-1, keepdims=True), 1e-12)

        def rotate_half(x):
            x1, x2 = jnp.split(x, 2, axis=-1)
            return jnp.concatenate([-x2, x1], axis=-1)

        def rotary_xpos(q, k):
            n = q.shape[-2]
            half_idx = jnp.arange(0, DIM_HEAD, 2, dtype=jnp.float32)
            inv_freq = 1.0 / 10000.0 ** (half_idx / DIM_HEAD)
            t = jnp.arange(n, dtype=jnp.float32)
            freqs = t[:, None] * inv_freq[None, :]
            freqs = jnp.concatenate([freqs, freqs], axis=-1)
            base = (half_idx + 0.4 * DIM_HEAD) / (1.4 * DIM_HEAD)
            power = (t - n // 2) / float(WINDOW // 2)
            scale = base[None, :] ** power[:, None]
            scale = jnp.concatenate([scale, scale], axis=-1)
            cos, sin = (jnp.cos(freqs), jnp.sin(freqs))
            q = q * cos * scale + rotate_half(q) * sin * scale
            k = k * cos / scale + rotate_half(k) * sin / scale
            return (q, k)

        def local_attention(q, k, v):
            b, h, n, d = q.shape
            w = n // WINDOW
            bq = q.reshape(b, h, w, WINDOW, d) * QK_SCALE
            bk = k.reshape(b, h, w, WINDOW, d)
            bv = v.reshape(b, h, w, WINDOW, d)

            def look_around(t):
                p = jnp.pad(t, ((0, 0), (0, 0), (1, 0), (0, 0), (0, 0)))
                return jnp.concatenate([p[:, :, :w], p[:, :, 1:]], axis=3)
            bk, bv = (look_around(bk), look_around(bv))
            bt = jnp.arange(n).reshape(w, WINDOW)
            btp = jnp.pad(bt, ((1, 0), (0, 0)), constant_values=-1)
            btk = jnp.concatenate([btp[:w], btp[1:]], axis=1)
            sim = jnp.einsum('bhwid,bhwjd->bhwij', bq, bk)
            i = bt[:, :, None]
            j = btk[:, None, :]
            mask = (i < j) | (i > j + WINDOW) | (j == -1)
            sim = jnp.where(mask, -jnp.finfo(sim.dtype).max, sim)
            attn = jax.nn.softmax(sim, axis=-1)
            out = jnp.einsum('bhwij,bhwjd->bhwid', attn, bv)
            return out.reshape(b, h, n, d)

        def _layer(x, wqkv, qs, ksc, wo, lg, lb, w1, b1, w2, b2):
            b, n, _ = x.shape
            h = shift_token(x)
            qkv = h @ wqkv
            q, k, v = jnp.split(qkv, 3, axis=-1)
            to_heads = lambda t: t.reshape(b, n, HEADS, DIM_HEAD).transpose(0, 2, 1, 3)
            q, k, v = (to_heads(q), to_heads(k), to_heads(v))
            q = l2norm(q) * qs
            k = l2norm(k) * ksc
            q, k = rotary_xpos(q, k)
            o = local_attention(q, k, v)
            o = o.transpose(0, 2, 1, 3).reshape(b, n, INNER)
            x = x + o @ wo
            h = shift_token(x)
            mu = h.mean(-1, keepdims=True)
            var = h.var(-1, keepdims=True)
            h = (h - mu) / jnp.sqrt(var + 1e-05) * lg + lb
            h = h @ w1 + b1
            a, g = jnp.split(h, 2, axis=-1)
            h = a * jax.nn.gelu(g, approximate=False)
            x = x + h @ w2 + b2
            return x
        for l in range(DEPTH):
            x = _layer(x, wqkv[l], q_scale[l], k_scale[l], wo[l], ln_g[l], ln_b[l], w1[l], b1[l], w2[l], b2[l])
        return x
    x = L0_attn_x
    x = _layernorm(x + _L0_attn_ref(x, L0_attn_w_qkv, L0_attn_b_qkv, L0_attn_w_out, L0_attn_b_out), axis=-1)
    x = _layernorm(x + _L0_ffn_ref(x, L0_ffn_wqkv, L0_ffn_q_scale, L0_ffn_k_scale, L0_ffn_wo, L0_ffn_ln_g, L0_ffn_ln_b, L0_ffn_w1, L0_ffn_b1, L0_ffn_w2, L0_ffn_b2), axis=-1)
    return x

_drawn_inputs = setup_inputs


def setup_inputs(seed=0):
    import zlib

    import numpy as np

    out = dict(_drawn_inputs(seed))
    spreads = {'L0_attn_b_qkv': (0.0, 0.1),
     'L0_attn_b_out': (0.0, 0.1),
     'L0_ffn_q_scale': (1.0, 0.6),
     'L0_ffn_k_scale': (1.0, 0.6),
     'L0_ffn_ln_g': (1.0, 0.6),
     'L0_ffn_ln_b': (0.0, 0.8),
     'L0_ffn_b1': (0.0, 0.8),
     'L0_ffn_b2': (0.0, 0.1)}
    factors = {}
    for name, (base, spread) in spreads.items():
        noise = np.random.default_rng([zlib.crc32(name.encode()), seed]).standard_normal(out[name].shape)
        drawn = base * np.exp(spread * noise) if base else spread * noise
        out[name] = jnp.asarray(drawn.astype(out[name].dtype))
    for name, factor in factors.items():
        out[name] = (out[name] * factor).astype(out[name].dtype)
    return out
```

```python
from contextlib import ExitStack

import numpy as np

import concourse.bass as bass
from concourse import mybir

F32 = mybir.dt.float32
F32R = mybir.dt.float32r
BF16 = mybir.dt.bfloat16
ALU = mybir.AluOpType
ACT = mybir.ActivationFunctionType
AX = mybir.AxisListType

P = 128
NEG = -1.0e30
MADE = 15
LN_EPS = 1e-5

NB, S, DM = 8, 512, 256
TB = S // P
KT = DM // P
AH, AD = 16, 16
HP = 4
AG = AH // HP
FH, FD = 8, 64
INNER = FH * FD
HID = 682
NT = 6
HT = 114
DEPTH = 2


def tile_rows(n):
    return min(HT, HID - n * HT)


class Uses:

    def __init__(self, consumers, depth):
        self.c, self.depth = consumers, depth

    def filled(self, b, n):
        return b * len(self.c) + n + 1

    def emptied(self, b, n):
        eng = self.c[n]
        return eng, b * self.c.count(eng) + self.c[:n + 1].count(eng)

    def before(self, b, n):
        if n >= self.depth:
            return [self.emptied(b, n - self.depth)]
        if isinstance(b, int) and b == 0:
            return []
        return [(e, b * self.c.count(e)) for e in sorted(set(self.c))]


def wait_apart(eng, K, sem, value):
    if not isinstance(value, int):
        value = eng.snap(eng.to_reg(value))
        eng.wait_ge(K["made"], MADE)
    eng.wait_ge(sem, value)


def constants(nc, ctx):
    sb = lambda name, shape, dt: ctx.enter_context(nc.sbuf_tensor(name, shape, dt))
    k = {
        "ident": sb("ident", [P, P], F32),
        "identb": sb("identb", [P, P], BF16),
        "causal": sb("causal", [P, P], BF16),
        "window": sb("window", [P, 2, P], BF16),
        "window0": sb("window0", [P, 2, P], BF16),
        "window_t": sb("window_t", [P, 2, P], BF16),
    }
    made = k["made"] = ctx.enter_context(nc.semaphore("const_made"))
    with nc.Block() as block:
        @block.gpsimd
        def _(pool):
            pool.memset(k["ident"][:, :], 0.0).then_inc(made, 1)
            pool.memset(k["identb"][:, :], 0.0).then_inc(made, 1)
            pool.memset(k["causal"][:, :], 0.0).then_inc(made, 1)
            pool.memset(k["window"][:, :, :], 0.0).then_inc(made, 1)
            pool.memset(k["window0"][:, 0, :], 0.0).then_inc(made, 1)
            pool.memset(k["window0"][:, 1, :], NEG).then_inc(made, 1)
            pool.memset(k["window_t"][:, :, :], 0.0).then_inc(made, 1)
            pool.wait_ge(made, 7)
            for m in (k["ident"], k["identb"]):
                pool.affine_select(out=m[:, :], in_=m[:, :], compare_op=ALU.not_equal, fill=1.0, base=0,
                                   pattern=[[-1, P]], channel_multiplier=1).then_inc(made, 1)
            for m in (k["causal"][:, :], k["window"][:, 1, :], k["window0"][:, 0, :]):
                pool.affine_select(out=m, in_=m, compare_op=ALU.is_ge, fill=NEG, base=0,
                                   pattern=[[-1, P]], channel_multiplier=1).then_inc(made, 1)
            pool.affine_select(out=k["window"][:, 0, :], in_=k["window"][:, 0, :], compare_op=ALU.is_ge,
                               fill=NEG, base=0, pattern=[[1, P]], channel_multiplier=-1).then_inc(made, 1)
            pool.affine_select(out=k["window_t"][:, 0, :], in_=k["window_t"][:, 0, :], compare_op=ALU.is_ge,
                               fill=NEG, base=0, pattern=[[1, P]], channel_multiplier=-1).then_inc(made, 1)
            pool.affine_select(out=k["window_t"][:, 1, :], in_=k["window_t"][:, 1, :], compare_op=ALU.is_ge,
                               fill=NEG, base=0, pattern=[[-1, P]], channel_multiplier=1).then_inc(made, 1)
            pool.wait_ge(made, MADE)
    return k


def first_attention(nc, K, scr, x, w_qkv, b_qkv, w_out, b_out, dst):
    with ExitStack() as ctx:
        sb = lambda name, shape, dt=F32: ctx.enter_context(nc.sbuf_tensor("a_" + name, shape, dt))
        ps = lambda name, shape: ctx.enter_context(nc.psum_tensor("a_" + name, shape, F32))
        sem = lambda name: ctx.enter_context(nc.semaphore("a_" + name))

        w_hi, w_lo = sb("w_hi", [P, KT, 3 * DM], F32R), sb("w_lo", [P, KT, 3 * DM], F32R)
        w_raw = sb("w_raw", [P, KT, 3 * DM])
        wo = sb("wo", [P, AG, DM])
        bqk = sb("bqk", [P, 4])
        bv, bo = sb("bv", [P, DM]), sb("bo", [P, DM])
        xin = sb("xin", [P, TB, DM])
        xt_hi, xt_lo = sb("xt_hi", [P, KT, S], F32R), sb("xt_lo", [P, KT, S], F32R)
        qk_hi, qk_lo = sb("qk_hi", [P, 4, S], F32R), sb("qk_lo", [P, 4, S], F32R)
        MROW = 96
        Q, Kk = sb("Q", [P, AH, S], F32R), sb("K", [P, AH, S], F32R)
        V = sb("V", [P, TB, AH, 32])
        negm = sb("negm", [P, TB, AH])
        mrow = sb("mrow", [HP, AG, S], F32R)
        QOFF = [0, 512, 896, 1152]
        PT = sb("PT", [P, 2, HP, 1280])
        ot, on = sb("ot", [P, S]), sb("on", [P, S])
        rc = sb("rc", [P, S // 32])
        zt = sb("zt", [P, AG, S])
        xr = sb("xr", [P, TB, DM])
        y, out = sb("y", [P, TB, DM]), sb("out", [P, TB, DM])
        st, mv = sb("st", [P, TB, 6]), sb("mv", [P, TB, 2])
        ve, rs, half = sb("ve", [P, TB]), sb("rs", [P, TB]), sb("half", [P, TB])

        FB = [ps("f0", [P, S]), ps("f1", [P, S])]
        RB = [ps("r0", [P, 2, S]), ps("r1", [P, 2, S])]
        OB, MB = ps("o", [P, S]), ps("m", [P, S])

        w_loaded, w_split = sem("w_loaded"), sem("w_split")
        wo_zeroed, stacks_set, on_zeroed = sem("wo_zeroed"), sem("stacks_set"), sem("on_zeroed")
        x_in, front_full, front_free = sem("x_in"), sem("front_full"), sem("front_free")
        hi_done = sem("hi_done")
        parts_out = sem("parts_out")
        stacked = [sem(f"stacked{g}") for g in range(AG)]
        ring_full = sem("ring_full")
        ring_free = {"dve": sem("max_done"), "act": sem("exp_done")}
        mt_full, mrow_done = sem("mt_full"), sem("mrow_done")
        m_in = [sem(f"m_in{g}") for g in range(AG)]
        o_full, o_free, z_done = sem("o_full"), sem("o_free"), sem("z_done")
        xr_in, xb_ready = sem("xr_in"), sem("xb_ready")
        stats, var_done, rstd_a, rstd_done = sem("stats"), sem("var_done"), sem("rstd_a"), sem("rstd_done")
        norm = sem("norm")
        out_done, stored = sem("out_done"), sem("stored")

        NF = 10
        ring = Uses(sum([["dve"] * 8, ["dve"] * 8, ["act"] * 8, ["dve"] * 8, ["act"] * 8, ["dve"] * 8,
                         ["act"] * 8, ["act"] * 8, ["dve"] * 4], []), 2)
        SM_AT = [0, 8, 24, 40]
        ST_AT = [16, 32, 48, 56]
        OUT_AT = 64

        STEPS = [("xr", 0), ("sm", 0), ("f_x", 0), ("mt", 0), ("sm", 1), ("f_qk", 0), ("st", 0), ("mt", 1),
                 ("f_qk", 1), ("sm", 2), ("pv", 0), ("st", 1), ("f_load", 0), ("mt", 2), ("f_qk", 2),
                 ("sm", 3), ("pv", 1), ("st", 2), ("mt", 3), ("f_qk", 3), ("pv", 2), ("st", 3),
                 ("f_load", 1), ("pv", 3), ("f_v", 0), ("out", 0)]

        def steps(eng, do):
            for name, i in STEPS:
                if name[0] == "f":
                    do(name, i, 0)
            with eng.Fori(0, NB - 1) as it:
                for name, i in STEPS:
                    do(name, i, it + 1 if name[0] == "f" else it)
            for name, i in STEPS:
                if name[0] != "f":
                    do(name, i, NB - 1)

        with nc.Block() as block:
            @block.sync
            def _(sp):
                sp.dma_start(w_raw[:, :, :], w_qkv.rearrange("(k p) n -> p k n", p=P)).then_inc(w_loaded, 16)
                for m, c in enumerate((0, DM, P, DM + P)):
                    sp.dma_start(bqk[:, m:m + 1], b_qkv[c:c + P].unsqueeze(1),
                                 allow_slow_non_contiguous=True).then_inc(w_loaded, 16)
                sp.dma_start(bv[:, :], b_qkv[2 * DM:].partition_broadcast(P)).then_inc(w_loaded, 16)
                sp.dma_start(bo[:, :], b_out.partition_broadcast(P)).then_inc(w_loaded, 16)
                sp.wait_ge(wo_zeroed, 1)
                wo_rows = w_out.rearrange("(g j d) n -> j d g n", j=HP, d=AD)
                for j in range(HP):
                    sp.dma_start(wo[32 * j:32 * j + AD, :, :], wo_rows[j]).then_inc(w_loaded, 16)

                def do(name, i, b):
                    if name == "f_x":
                        if not isinstance(b, int):
                            sp.wait_ge(front_full, (b - 1) * NF + 2)
                        sp.dma_start(xin[:, :, :], x[b].rearrange("(t p) d -> p t d", p=P)).then_inc(x_in, 16)
                    elif name == "f_qk":
                        sp.wait_ge(hi_done, b * 6 + 3 + i)
                        sp.dma_start(scr[b, 0, P * i:P * i + P], qk_hi[:, i, :].bitcast(F32)).then_inc(parts_out, 16)
                        sp.wait_ge(front_free, b * NF + 3 + i)
                        sp.dma_start(scr[b, 1, P * i:P * i + P], qk_lo[:, i, :].bitcast(F32)).then_inc(parts_out, 16)
                    elif name == "f_load":
                        wait_apart(sp, K, parts_out, b * 128 + 64 * (i + 1))
                        if i == 0 and isinstance(b, int):
                            sp.wait_ge(stacks_set, 3)
                        for g in (2 * i, 2 * i + 1):
                            if not isinstance(b, int):
                                sp.wait_ge(ring_full, ring.filled(b - 1, ST_AT[g] + 7))
                            r0 = 64 * (g % 2)
                            for t, dst_t, order in ((2 * i, Q, (0, 0, 1)), (2 * i + 1, Kk, (0, 1, 0))):
                                for slot, part in enumerate(order):
                                    sp.dma_start(
                                        dst_t[AD * slot:AD * slot + AD, HP * g:HP * g + HP, :].bitcast(F32),
                                        scr[b, part, P * t + r0:P * t + r0 + 64]
                                        .rearrange("(h d) n -> d h n", d=AD)).then_inc(stacked[g], 16)
                    elif name == "xr":
                        sp.wait_ge(ring_free["dve"], b * ring.c.count("dve"))
                        sp.dma_start(xr[:, :, :], x[b].rearrange("(t p) d -> p t d", p=P)).then_inc(xr_in, 16)
                    elif name == "mt":
                        sp.wait_ge(mrow_done, b * AG + i + 1)
                        for j in range(HP):
                            sp.dma_start(Q[MROW:MROW + 1, HP * i + j, :].bitcast(F32),
                                         mrow[j:j + 1, i, :].bitcast(F32)).then_inc(m_in[i], 16)
                    elif name == "out":
                        sp.wait_ge(out_done, b * TB + TB)
                        sp.dma_start(dst[b, 1:1 + S].rearrange("(t p) d -> p t d", p=P),
                                     out[:, :, :]).then_inc(stored, 16)

                steps(sp, do)
                sp.wait_ge(stored, 16 * NB)

            @block.gpsimd
            def _(pool):
                pool.memset(wo[:, :, :], 0.0).then_inc(wo_zeroed, 1)
                pool.memset(half[:, :], -0.5).then_inc(rstd_a, 1)
                pool.memset(on[:, :], 0.0).then_inc(on_zeroed, 1)
                pool.memset(Kk[:, :, :].bitcast(F32), 0.0).then_inc(stacks_set, 1)
                pool.wait_ge(stacks_set, 2)
                pool.memset(Kk[MROW:MROW + 1, :, :].bitcast(F32), 1.0).then_inc(stacks_set, 1)

                def do(name, i, b):
                    if name == "xr":
                        pool.wait_ge(xr_in, b * 16 + 16)
                        pool.wait_ge(w_loaded, 176)
                        pool.tensor_tensor(xr[:, :, :], xr[:, :, :],
                                           bo[:, :].unsqueeze(1).to_broadcast([P, TB, DM]), ALU.add)\
                            .then_inc(xb_ready, 1)
                    elif name == "out":
                        wait_apart(pool, K, var_done, b + 1)
                        pool.tensor_scalar(ve[:, :], mv[:, :, 1], LN_EPS, None, ALU.add).then_inc(rstd_a, 1)
                        pool.wait_ge(rstd_a, b + 2)
                        pool.tensor_tensor(rs[:, :], ve[:, :], half[:, :], ALU.pow).then_inc(rstd_done, 1)

                steps(pool, do)

            @block.scalar
            def _(act):
                act.wait_ge(w_loaded, 176)
                for kt in range(KT):
                    nc.scalar.activation(w_hi[:, kt, :], w_raw[:, kt, :], ACT.Copy).then_inc(w_split, 1)

                def do(name, i, b):
                    if name == "f_x":
                        for h in range(KT):
                            act.wait_ge(front_full, b * NF + h + 1)
                            nc.scalar.activation(xt_hi[:, h, :], FB[h][:, :], ACT.Identity).then_inc(hi_done, 1)
                    elif name == "f_qk":
                        act.wait_ge(front_full, b * NF + 3 + i)
                        act.wait_ge(parts_out, b * 128)
                        nc.scalar.activation(qk_hi[:, i, :], FB[i % 2][:, :], ACT.Identity,
                                             bias=bqk[:, i:i + 1]).then_inc(hi_done, 1)
                    elif name == "mt":
                        act.wait_ge(mt_full, b * AG + i + 1)
                        act.wait_ge(m_in[i], b * 64)
                        nc.scalar.activation(mrow[:, i, :], MB[0:HP, :], ACT.Identity).then_inc(mrow_done, 1)
                    elif name == "st":
                        for pr in range(2):
                            for j in range(TB):
                                n = ST_AT[i] + TB * pr + j
                                act.wait_ge(ring_full, ring.filled(b, n))
                                q0 = max(P * j - S // 2, 0)
                                nq = S - P * j
                                nc.scalar.activation(
                                    PT[:, i % 2, 2 * pr:2 * pr + 2, QOFF[j]:QOFF[j] + nq],
                                    RB[n % 2][:, :, q0:q0 + nq],
                                    ACT.Exp, scale=AD ** -0.5).then_inc(ring_free["act"], 1)

                steps(act, do)

            @block.vector
            def _(dve):
                dve.memset(Q[:, :, :].bitcast(F32), 0.0).then_inc(stacks_set, 1)
                dve.memset(V[:, :, :, :], 0.0).then_inc(w_split, 1)
                dve.wait_ge(w_split, 3)
                for kt in range(KT):
                    dve.tensor_tensor(w_lo[:, kt, :], w_raw[:, kt, :], w_hi[:, kt, :], ALU.subtract)\
                        .then_inc(w_split, 1)
                dve.memset(V[:, :, :, AD:AD + 1], 1.0).then_inc(w_split, 1)

                def do(name, i, b):
                    if name == "f_x":
                        for h in range(KT):
                            dve.wait_ge(hi_done, b * 6 + h + 1)
                            dve.tensor_tensor(xt_lo[:, h, :], FB[h][:, :], xt_hi[:, h, :], ALU.subtract)\
                                .then_inc(front_free, 1)
                    elif name == "f_qk":
                        dve.wait_ge(hi_done, b * 6 + 3 + i)
                        dve.scalar_tensor_tensor(out=qk_lo[:, i, :], in0=FB[i % 2][:, :], scalar=bqk[:, i:i + 1],
                                                 in1=qk_hi[:, i, :], op0=ALU.add, op1=ALU.subtract)\
                            .then_inc(front_free, 1)
                    elif name == "f_v":
                        for t in range(TB):
                            dve.wait_ge(front_full, b * NF + 7 + t)
                            dve.tensor_tensor(V[:, t, :, 0:AD],
                                              FB[t % 2][:, 0:DM].rearrange("p (h d) -> p h d", d=AD),
                                              bv[:, :].rearrange("p (h d) -> p h d", d=AD), ALU.add)\
                                .then_inc(front_free, 1)
                    elif name == "sm":
                        for pr in range(2):
                            for q in range(TB):
                                n = SM_AT[i] + TB * pr + q
                                h = HP * i + 2 * pr
                                dve.wait_ge(ring_full, ring.filled(b, n))
                                dve.tensor_reduce(negm[:, q, h:h + 2], RB[n % 2][:, :, 0:P * (q + 1)], AX.X,
                                                  ALU.max, negate=True).then_inc(ring_free["dve"], 1)
                    elif name == "pv":
                        dve.wait_ge(o_full, b * AG + i + 1)
                        dve.wait_ge(on_zeroed, 1)
                        dve.transpose(ot[:, :], OB[:, :]).then_inc(o_free, 1)
                        dve.wait_ge(o_free, b * AG + i + 1)
                        ov = ot[:, :].rearrange("p (c r) -> p c r", r=32)
                        dve.reciprocal(rc[:, :], ov[:, :, AD]).then_inc(norm, 1)
                        dve.wait_ge(norm, b * 8 + 2 * i + 1)
                        dve.wait_ge(z_done, b * AG + i)
                        dve.tensor_tensor(on[:, :].rearrange("p (c r) -> p c r", r=32)[:, :, 0:AD],
                                          ov[:, :, 0:AD], rc[:, :].unsqueeze(2).to_broadcast([P, S // 32, AD]),
                                          ALU.mult).then_inc(norm, 1)
                        dve.wait_ge(norm, b * 8 + 2 * i + 2)
                        dve.transpose(zt[:, i, :], on[:, :]).then_inc(z_done, 1)
                    elif name == "out":
                        dve.wait_ge(xb_ready, b + 1)
                        dve.wait_ge(out_done, b * TB)
                        for t in range(TB):
                            n = OUT_AT + t
                            dve.wait_ge(ring_full, ring.filled(b, n))
                            dve.tensor_tensor(y[:, t, :], RB[n % 2][:, 0, 0:DM], xr[:, t, :], ALU.add)\
                                .then_inc(ring_free["dve"], 1)
                            dve.wait_ge(ring_free["dve"], ring.emptied(b, n)[1])
                            dve.bn_stats(st[:, t, :], y[:, t, :]).then_inc(stats, 1)
                        for t in range(TB):
                            wait_apart(dve, K, stats, b * TB + t + 1)
                            m = dve.bn_aggr(mv[:, t, :], st[:, t, :])
                        m.then_inc(var_done, 1)
                        dve.wait_ge(rstd_done, b + 1)
                        dve.wait_ge(stored, b * 16)
                        for t in range(TB):
                            dve.tensor_scalar(out[:, t, :], y[:, t, :], mv[:, t, 0:1], rs[:, t:t + 1],
                                              ALU.subtract, ALU.mult).then_inc(out_done, 1)

                steps(dve, do)

            @block.tensor
            def _(pe):
                def split_mm(o, a_hi, a_lo, r_hi, r_lo, first, last):
                    pe.matmul(o, a_hi, r_hi, start=first, stop=False)
                    pe.matmul(o, a_lo, r_hi, start=False, stop=False)
                    return pe.matmul(o, a_hi, r_lo, start=False, stop=last)

                def ring_wait(b, n):
                    for e, v in ring.before(b, n):
                        pe.wait_ge(ring_free[e], v)

                pe.wait_ge(w_split, 6)

                def do(name, i, b):
                    if name == "f_x":
                        pe.wait_ge(x_in, b * 16 + 16)
                        for h in range(KT):
                            if not isinstance(b, int):
                                pe.wait_ge(front_free, b * NF + h - 1)
                            for t in range(TB):
                                m = pe.transpose(FB[h][:, P * t:P * t + P], xin[:, t, P * h:P * h + P],
                                                 K["ident"][:, :])
                            m.then_inc(front_full, 1)
                    elif name == "f_qk":
                        col = (0, DM, P, DM + P)[i]
                        pe.wait_ge(front_free, b * NF + max(1 + i, 2))
                        for h in range(KT):
                            m = split_mm(FB[i % 2][:, :], w_hi[:, h, col:col + P], w_lo[:, h, col:col + P],
                                         xt_hi[:, h, :], xt_lo[:, h, :], h == 0, h == KT - 1)
                        m.then_inc(front_full, 1)
                    elif name == "f_v":
                        for t in range(TB):
                            pe.wait_ge(front_free, b * NF + 5 + t)
                            for h in range(KT):
                                tok = slice(P * t, P * t + P)
                                m = split_mm(FB[t % 2][:, 0:DM], xt_hi[:, h, tok], xt_lo[:, h, tok],
                                             w_hi[:, h, 2 * DM:], w_lo[:, h, 2 * DM:], h == 0, h == KT - 1)
                            m.then_inc(front_full, 1)
                    elif name == "sm":
                        pe.wait_ge(stacked[i], b * 96 + 96)
                        for pr in range(2):
                            for q in range(TB):
                                n = SM_AT[i] + TB * pr + q
                                ring_wait(b, n)
                                r = RB[n % 2]
                                for hh in range(2):
                                    h = HP * i + 2 * pr + hh
                                    pe.matmul(r[:, hh, 0:max(P * (q + 1), 256)], Q[0:MROW, h, P * q:P * q + P],
                                              Kk[0:MROW, h, 0:max(P * (q + 1), 256)], start=True, stop=True)
                                    m = pe.matmul(r[:, hh, P * q:P * q + P], K["identb"][:, :],
                                                  K["causal"][:, :], start=False, stop=True,
                                                  skip_group_check=True)
                                m.then_inc(ring_full, 1)
                    elif name == "mt":
                        pe.wait_ge(ring_free["dve"], ring.emptied(b, SM_AT[i] + 7)[1])
                        pe.wait_ge(mrow_done, b * AG + i)
                        for q in range(TB):
                            m = pe.transpose(MB[0:HP, P * q:P * q + P], negm[:, q, HP * i:HP * i + HP],
                                             K["ident"][:, :])
                        m.then_inc(mt_full, 1)
                    elif name == "st":
                        pe.wait_ge(m_in[i], b * 64 + 64)
                        for pr in range(2):
                            for j in range(TB):
                                n = ST_AT[i] + TB * pr + j
                                ring_wait(b, n)
                                q0 = min(P * j, S // 2)
                                for hh in range(2):
                                    h = HP * i + 2 * pr + hh
                                    pe.matmul(RB[n % 2][:, hh, 0:S - q0], Kk[0:MROW + 1, h, P * j:P * j + P],
                                              Q[0:MROW + 1, h, q0:S], start=True, stop=True)
                                    m = pe.matmul(RB[n % 2][:, hh, P * j - q0:P * j - q0 + P], K["identb"][:, :],
                                                  K["window_t"][:, 0, :], start=False, stop=True,
                                                  skip_group_check=True)
                                m.then_inc(ring_full, 1)
                    elif name == "pv":
                        pe.wait_ge(ring_free["act"], ring.emptied(b, ST_AT[i] + 7)[1])
                        pe.wait_ge(o_free, b * AG + i)
                        pe.wait_ge(front_free, b * NF + NF)
                        for j in range(TB):
                            for hh in range(HP):
                                m = pe.matmul(OB[32 * hh:32 * hh + 32, P * j:S], V[:, j, HP * i + hh, :],
                                              PT[:, i % 2, hh, QOFF[j]:QOFF[j] + S - P * j],
                                              start=(j == 0), stop=(j == TB - 1), skip_group_check=True)
                        m.then_inc(o_full, 1)
                    elif name == "out":
                        pe.wait_ge(z_done, b * AG + AG)
                        for t in range(TB):
                            n = OUT_AT + t
                            ring_wait(b, n)
                            for g in range(AG):
                                m = pe.matmul(RB[n % 2][:, 0, 0:DM], zt[:, g, P * t:P * t + P], wo[:, g, :],
                                              start=(g == 0), stop=(g == AG - 1))
                            m.then_inc(ring_full, 1)

                steps(pe, do)


def local_attention(nc, K, lay, x, wqkv, q_scale, k_scale, wo_w, rot, dst):
    with ExitStack() as ctx:
        sb = lambda name, shape, dt=F32: ctx.enter_context(nc.sbuf_tensor(f"l{lay}_" + name, shape, dt))
        ps = lambda name, shape: ctx.enter_context(nc.psum_tensor(f"l{lay}_" + name, shape, F32))
        sem = lambda name: ctx.enter_context(nc.semaphore(f"l{lay}_" + name))

        w_hi, w_lo = sb("w_hi", [P, KT, 3 * INNER], F32R), sb("w_lo", [P, KT, 3 * INNER], F32R)
        wo = sb("wo", [P, INNER // P, DM])
        scales = sb("scales", [P, 2, FD])
        rots = sb("rots", [P, 2, 2, TB, FD])
        xin = sb("xin", [P, TB, DM])
        xt_hi, xt_lo = sb("xt_hi", [P, KT, S + 1], F32R), sb("xt_lo", [P, KT, S + 1], F32R)
        sq, t1, t2 = sb("sq", [P, 2, INNER]), sb("t1", [P, 2, INNER]), sb("t2", [P, 2, INNER])
        ss, inv, half = sb("ss", [P, 2 * FH]), sb("inv", [P, 2 * FH]), sb("half", [P, 2 * FH])
        qk = sb("qk", [P, TB, 2, INNER])
        q_hi, q_lo = sb("q_hi", [P, FH // 2, S], F32R), sb("q_lo", [P, FH // 2, S], F32R)
        k_hi, k_lo = sb("k_hi", [P, FH, S], F32R), sb("k_lo", [P, FH, S], F32R)
        V = sb("V", [P, TB, INNER])
        ones = sb("ones", [P, FD])
        LOW, MK = 32, 96
        negm, mrow = sb("negm", [P, TB, FH]), sb("mrow", [P, S], F32R)
        pick_f, pick = sb("pick_f", [P, FH, P]), sb("pick", [P, FH, P], F32R)
        PT = sb("PT", [P, 2, TB, 2, 2 * P])
        lns, rsum = sb("lns", [P, S]), sb("rsum", [P, S])
        zt = sb("zt", [P, INNER // P, S])
        xr, out = sb("xr", [P, TB, DM]), sb("out", [P, TB, DM])

        FB = [ps("f0", [P, S]), ps("f1", [P, S])]
        RB = [ps(f"r{i}", [P, S]) for i in range(4)]
        OB, SB = ps("o", [P, S]), ps("s", [P, S])

        w_loaded, w_hi_done, w_lo_done, small = sem("w_loaded"), sem("w_hi_done"), sem("w_lo_done"), sem("small")
        rots_in, rots_done = sem("rots_in"), sem("rots_done")
        x_in, front_full, hi_done = sem("x_in"), sem("front_full"), sem("hi_done")
        front_free = {"dve": sem("front_free_dve"), "act": sem("v_done")}
        sq_done, ss_raw, ss_done, inv_done = sem("sq_done"), sem("ss_raw"), sem("ss_done"), sem("inv_done")
        summed, rotated = sem("summed"), sem("rotated")
        ring_full = sem("ring_full")
        ring_free = {"dve": sem("ring_free_dve"), "act": sem("exp_done")}
        mt_full, mhi_done, mrow_done = sem("mt_full"), sem("mhi_done"), sem("mrow_done")
        picked = sem("picked")
        o_full, rsum_done, ln_done, z_done = (
            sem("o_full"), sem("rsum_done"), sem("ln_done"), sem("z_done"))
        xr_in, stored = sem("xr_in"), sem("stored")

        front = Uses(["dve"] * 10 + ["act"] * 4 + ["dve"] * 8, 2)
        QK_AT, V_AT, T_AT = 2, 10, 14
        ring = Uses(["dve"] * 16 + ["act"] * 16 + ["dve"] * 4, 4)
        ST_AT, OUT_AT = 16, 32

        STEPS = [("xr", 0), ("sm", 0), ("sm", 1), ("f_x", 0), ("sm", 2), ("sm", 3), ("f_qk", 0), ("mt", 0),
                 ("f_qk", 1), ("st", 0), ("f_qk", 2), ("st", 1), ("pv", 0), ("f_qk", 3), ("st", 2), ("pv", 1),
                 ("st", 3), ("pv", 2), ("f_v", 0), ("pv", 3), ("f_v", 1), ("out", 0), ("f_t", 0)]
        STEPS = [s for s in STEPS if s[0] != "f_v"]
        STEPS.insert(STEPS.index(("out", 0)), ("f_v", 0))

        def steps(eng, do):
            for name, i in STEPS:
                if name[0] == "f":
                    do(name, i, 0)
            with eng.Fori(0, NB - 1) as it:
                for name, i in STEPS:
                    do(name, i, it + 1 if name[0] == "f" else it)
            for name, i in STEPS:
                if name[0] != "f":
                    do(name, i, NB - 1)

        raw = qk[:, 0:3, :, :].rearrange("p t w n -> p (t w n)").rearrange("p (k n) -> p k n", k=KT)

        with nc.Block() as block:
            @block.sync
            def _(sp):
                sp.dma_start(raw, wqkv.rearrange("(k p) n -> p k n", p=P)).then_inc(w_loaded, 16)
                sp.dma_start(wo[:, :, :], wo_w.rearrange("(k p) n -> p k n", p=P)).then_inc(w_loaded, 16)
                sp.dma_start(scales[:, 0, :], q_scale.partition_broadcast(P)).then_inc(rots_in, 16)
                sp.dma_start(scales[:, 1, :], k_scale.partition_broadcast(P)).then_inc(rots_in, 16)
                for w in range(2):
                    for c in range(2):
                        sp.dma_start(rots[:, w, c, :, :], rot[w, c].rearrange("(t p) d -> p t d", p=P))\
                            .then_inc(rots_in, 16)

                def do(name, i, b):
                    if name == "f_x":
                        if not isinstance(b, int):
                            sp.wait_ge(front_full, front.filled(b - 1, 1))
                        sp.dma_start(xin[:, :, :], x[b].rearrange("(t p) d -> p t d", p=P)).then_inc(x_in, 16)
                    elif name == "xr":
                        sp.wait_ge(ring_free["dve"], b * ring.c.count("dve"))
                        sp.dma_start(xr[:, :, :], x[b].rearrange("(t p) d -> p t d", p=P)).then_inc(xr_in, 16)
                    elif name == "out":
                        sp.wait_ge(ring_free["dve"], ring.emptied(b, OUT_AT + TB - 1)[1])
                        sp.dma_start(dst[b, 1:1 + S].rearrange("(t p) d -> p t d", p=P),
                                     out[:, :, :]).then_inc(stored, 16)

                steps(sp, do)
                sp.wait_ge(stored, 16 * NB)

            @block.gpsimd
            def _(pool):
                pool.memset(half[:, :], -0.5).then_inc(small, 1)
                pool.memset(ones[:, :], 1.0).then_inc(small, 1)
                pool.memset(k_hi[:, :, :].bitcast(F32), 0.0).then_inc(small, 1)
                pool.memset(xt_hi[:, 1, 0:1].bitcast(F32), 0.0).then_inc(small, 1)
                pool.memset(xt_lo[:, 1, 0:1].bitcast(F32), 0.0).then_inc(small, 1)
                pool.memset(pick_f[:, :, :], 0.0).then_inc(small, 1)
                pool.memset(mrow[:, :].bitcast(F32), 0.0).then_inc(small, 1)
                pool.wait_ge(small, 8)
                for n, low in enumerate((0, LOW)):
                    pool.affine_select(out=pick_f[:, :, :], in_=pick_f[:, :, :], compare_op=ALU.not_equal,
                                       fill=1.0, base=-low, pattern=[[-1, FH], [0, P]],
                                       channel_multiplier=1).then_inc(picked, 1)
                    pool.wait_ge(picked, n + 1)
                pool.tensor_copy(pick[:, :, :], pick_f[:, :, :]).then_inc(picked, 1)

                def do(name, i, b):
                    if name == "f_qk":
                        n = b * TB + i
                        pool.wait_ge(ss_done, n + 1)
                        pool.tensor_tensor(inv[:, :], ss[:, :], half[:, :], ALU.pow).then_inc(inv_done, 1)
                        for w in range(2):
                            pool.wait_ge(front_free["dve"], front.emptied(b, QK_AT + 2 * i + w)[1])
                            pool.tensor_tensor(t1[:, w, :], t1[:, w, :], t2[:, w, :], ALU.add)\
                                .then_inc(summed, 1)
                            if w == 0:
                                pool.wait_ge(inv_done, n + 1)
                            pool.wait_ge(summed, 2 * n + w + 1)
                            pool.tensor_tensor(qk[:, i, w, :].rearrange("p (h d) -> p h d", d=FD),
                                               t1[:, w, :].rearrange("p (h d) -> p h d", d=FD),
                                               inv[:, FH * w:FH * w + FH].unsqueeze(2)
                                               .to_broadcast([P, FH, FD]), ALU.mult).then_inc(rotated, 1)

                steps(pool, do)

            @block.scalar
            def _(act):
                act.wait_ge(w_loaded, 32)
                for kt in range(KT):
                    nc.scalar.activation(w_hi[:, kt, :], raw[:, kt, :], ACT.Copy).then_inc(w_hi_done, 1)

                def do(name, i, b):
                    if name == "f_x":
                        for h in range(KT):
                            act.wait_ge(front_full, front.filled(b, h))
                            nc.scalar.activation(xt_hi[:, h, h:S + h], FB[h][:, :], ACT.Identity)\
                                .then_inc(hi_done, 1)
                    elif name == "f_qk":
                        n = b * TB + i
                        for w in range(2):
                            act.wait_ge(front_full, front.filled(b, QK_AT + 2 * i + w))
                            act.wait_ge(ss_done, n)
                            nc.scalar.activation(sq[:, w, :], FB[w][:, :], ACT.Square).then_inc(sq_done, 1)
                    elif name == "f_v":
                        for t in range(TB):
                            act.wait_ge(front_full, front.filled(b, V_AT + t))
                            nc.scalar.activation(V[:, t, :], FB[t % 2][:, :], ACT.Identity)\
                                .then_inc(front_free["act"], 1)
                    elif name == "f_t":
                        act.wait_ge(small, 8)
                        for p in range(FH // 2):
                            act.wait_ge(front_full, front.filled(b, T_AT + 2 * p))
                            nc.scalar.activation(q_hi[:, p, :], FB[0][:, :], ACT.Identity).then_inc(hi_done, 1)
                            act.wait_ge(front_full, front.filled(b, T_AT + 2 * p + 1))
                            for hh in range(2):
                                rows = slice(FD * hh, FD * hh + FD)
                                m = nc.scalar.activation(k_hi[rows, 2 * p + hh, :], FB[1][rows, :], ACT.Identity)
                            m.then_inc(hi_done, 1)
                    elif name == "mt":
                        act.wait_ge(mt_full, b + 1)
                        nc.scalar.activation(mrow[0:FH, :], SB[0:FH, :], ACT.Identity).then_inc(mhi_done, 1)
                    elif name == "st":
                        for j in range(TB):
                            n = ST_AT + TB * i + j
                            act.wait_ge(ring_full, ring.filled(b, n))
                            nq = P if j == TB - 1 else 2 * P
                            src = RB[n % 4][:, :].rearrange("p (h q) -> p h q", h=2)
                            nc.scalar.activation(PT[:, i % 2, j, :, 0:nq], src[:, :, 2 * P - nq:2 * P], ACT.Exp,
                                                 scale=8.0).then_inc(ring_free["act"], 1)
                    elif name == "pv":
                        act.wait_ge(o_full, b * TB + i + 1)
                        nc.scalar.activation(lns[:, :], SB[:, :], ACT.Ln).then_inc(ln_done, 1)
                        act.wait_ge(ln_done, b * TB + i + 1)
                        act.wait_ge(z_done, b * TB + i)
                        nc.scalar.activation(rsum[:, :], lns[:, :], ACT.Exp, scale=-1.0).then_inc(rsum_done, 1)

                steps(act, do)

            @block.vector
            def _(dve):
                dve.memset(k_lo[:, :, :].bitcast(F32), 0.0).then_inc(small, 1)
                for kt in range(KT):
                    dve.wait_ge(w_hi_done, kt + 1)
                    dve.tensor_tensor(w_lo[:, kt, :], raw[:, kt, :], w_hi[:, kt, :], ALU.subtract)\
                        .then_inc(w_lo_done, 1)
                dve.wait_ge(rots_in, 96)
                H2 = FD // 2
                for w in range(2):
                    sc = scales[:, w:w + 1, :].to_broadcast([P, TB, FD])
                    dve.tensor_tensor(rots[:, w, 0, :, :], rots[:, w, 0, :, :], sc, ALU.mult)\
                        .then_inc(rots_done, 1)
                    dve.scalar_tensor_tensor(out=rots[:, w, 1, :, 0:H2], in0=rots[:, w, 1, :, 0:H2], scalar=-1.0,
                                             in1=sc[:, :, H2:FD], op0=ALU.mult, op1=ALU.mult)\
                        .then_inc(rots_done, 1)
                    dve.tensor_tensor(rots[:, w, 1, :, H2:FD], rots[:, w, 1, :, H2:FD], sc[:, :, 0:H2],
                                      ALU.mult).then_inc(rots_done, 1)
                dve.wait_ge(rots_done, 6)

                def do(name, i, b):
                    if name == "f_x":
                        for h in range(KT):
                            dve.wait_ge(hi_done, b * 10 + h + 1)
                            dve.tensor_tensor(xt_lo[:, h, h:S + h], FB[h][:, :], xt_hi[:, h, h:S + h],
                                              ALU.subtract).then_inc(front_free["dve"], 1)
                    elif name == "f_qk":
                        n = b * TB + i
                        dve.wait_ge(rotated, 2 * n)
                        for w in range(2):
                            f = FB[w][:, :].rearrange("p (h d) -> p h d", d=FD)
                            a = t1[:, w, :].rearrange("p (h d) -> p h d", d=FD)
                            c = t2[:, w, :].rearrange("p (h d) -> p h d", d=FD)
                            cs = lambda k, lo, hi: rots[:, w, k, i, lo:hi].unsqueeze(1)\
                                .to_broadcast([P, FH, hi - lo])
                            dve.wait_ge(sq_done, 2 * n + w + 1)
                            m = dve.tensor_reduce(ss[:, FH * w:FH * w + FH],
                                                  sq[:, w, :].rearrange("p (h d) -> p h d", d=FD), AX.X, ALU.add)
                            m.then_inc(ss_raw, 1)
                            dve.tensor_tensor(a, f, cs(0, 0, FD), ALU.mult)
                            dve.tensor_tensor(c[:, :, 0:H2], f[:, :, H2:FD], cs(1, 0, H2), ALU.mult)
                            dve.tensor_tensor(c[:, :, H2:FD], f[:, :, 0:H2], cs(1, H2, FD), ALU.mult)\
                                .then_inc(front_free["dve"], 1)
                        dve.wait_ge(ss_raw, 2 * n + 2)
                        dve.tensor_scalar(ss[:, :], ss[:, :], 1e-24, None, ALU.max).then_inc(ss_done, 1)
                    elif name == "f_t":
                        for p in range(FH // 2):
                            dve.wait_ge(hi_done, b * 10 + 3 + 2 * p)
                            dve.tensor_tensor(q_lo[:, p, :], FB[0][:, :], q_hi[:, p, :], ALU.subtract)\
                                .then_inc(front_free["dve"], 1)
                            dve.wait_ge(hi_done, b * 10 + 4 + 2 * p)
                            for hh in range(2):
                                r = slice(FD * hh, FD * hh + FD)
                                m = dve.tensor_tensor(k_lo[r, 2 * p + hh, :], FB[1][r, :], k_hi[r, 2 * p + hh, :],
                                                      ALU.subtract)
                            m.then_inc(front_free["dve"], 1)
                    elif name == "sm":
                        for q in range(TB):
                            n = TB * i + q
                            dve.wait_ge(ring_full, ring.filled(b, n))
                            dve.tensor_reduce(negm[:, q, 2 * i:2 * i + 2],
                                              RB[n % 4][:, :].rearrange("p (h k) -> p h k", h=2), AX.X,
                                              ALU.max, negate=True).then_inc(ring_free["dve"], 1)
                    elif name == "mt":
                        dve.wait_ge(mhi_done, b + 1)
                        dve.tensor_tensor(mrow[LOW:LOW + FH, :], SB[0:FH, :], mrow[0:FH, :], ALU.subtract)\
                            .then_inc(mrow_done, 1)
                    elif name == "pv":
                        dve.wait_ge(rsum_done, b * TB + i + 1)
                        dve.tensor_tensor(zt[:, i, :], OB[:, :], rsum[:, :], ALU.mult).then_inc(z_done, 1)
                    elif name == "out":
                        dve.wait_ge(xr_in, b * 16 + 16)
                        dve.wait_ge(stored, b * 16)
                        for t in range(TB):
                            n = OUT_AT + t
                            dve.wait_ge(ring_full, ring.filled(b, n))
                            dve.tensor_tensor(out[:, t, :], RB[n % 4][:, 0:DM], xr[:, t, :], ALU.add)\
                                .then_inc(ring_free["dve"], 1)

                steps(dve, do)

            @block.tensor
            def _(pe):
                def split_mm(o, a_hi, a_lo, r_hi, r_lo, first, last):
                    pe.matmul(o, a_hi, r_hi, start=first, stop=False)
                    pe.matmul(o, a_lo, r_hi, start=False, stop=False)
                    return pe.matmul(o, a_hi, r_lo, start=False, stop=last)

                def turn_wait(uses, free, b, n):
                    for e, v in uses.before(b, n):
                        pe.wait_ge(free[e], v)

                pe.wait_ge(w_lo_done, 2)
                pe.wait_ge(small, 8)
                pe.wait_ge(picked, 3)

                def do(name, i, b):
                    if name == "f_x":
                        pe.wait_ge(x_in, b * 16 + 16)
                        for h in range(KT):
                            turn_wait(front, front_free, b, h)
                            for t in range(TB):
                                m = pe.transpose(FB[h][:, P * t:P * t + P], xin[:, t, P * h:P * h + P],
                                                 K["ident"][:, :])
                            m.then_inc(front_full, 1)
                    elif name == "f_qk":
                        tok = slice(P * i, P * i + P)
                        for w in range(2):
                            turn_wait(front, front_free, b, QK_AT + 2 * i + w)
                            if i == 0 and w == 0:
                                pe.wait_ge(front_free["dve"], front.emptied(b, 1)[1])
                            for h in range(KT):
                                col = slice(INNER * w, INNER * w + INNER)
                                m = split_mm(FB[w][:, :], xt_hi[:, h, tok], xt_lo[:, h, tok], w_hi[:, h, col],
                                             w_lo[:, h, col], h == 0, h == KT - 1)
                            m.then_inc(front_full, 1)
                    elif name == "f_v":
                        for t in range(TB):
                            turn_wait(front, front_free, b, V_AT + t)
                            tok = slice(P * t, P * t + P)
                            for h in range(KT):
                                m = split_mm(FB[t % 2][:, :], xt_hi[:, h, tok], xt_lo[:, h, tok],
                                             w_hi[:, h, 2 * INNER:], w_lo[:, h, 2 * INNER:], h == 0, h == KT - 1)
                            m.then_inc(front_full, 1)
                    elif name == "f_t":
                        pe.wait_ge(rotated, b * 8 + 8)
                        for p in range(FH // 2):
                            for w in range(2):
                                turn_wait(front, front_free, b, T_AT + 2 * p + w)
                                for t in range(TB):
                                    m = pe.transpose(FB[w][:, P * t:P * t + P], qk[:, t, w, P * p:P * p + P],
                                                     K["ident"][:, :])
                                m.then_inc(front_full, 1)
                    elif name == "sm":
                        if i == 0:
                            pe.wait_ge(front_free["dve"], front.emptied(b, T_AT + 7)[1])
                        for q in range(TB):
                            n = TB * i + q
                            turn_wait(ring, ring_free, b, n)
                            k0 = P * max(q - 1, 0)
                            r = RB[n % 4][:, :].rearrange("p (h k) -> p h k", h=2)
                            for hh in range(2):
                                pe.matmul(r[:, hh, :], q_hi[:, i, P * q:P * q + P],
                                          k_hi[:, 2 * i + hh, k0:k0 + 2 * P], start=(hh == 0), stop=True,
                                          skip_group_check=True)
                            mask = K["window"] if q else K["window0"]
                            pe.matmul(r, K["identb"][:, :],
                                      mask[:, :, :].rearrange("p b k -> p (b k)").unsqueeze(1)
                                      .to_broadcast([P, 2, 2 * P]), start=False, stop=True,
                                      skip_group_check=True).then_inc(ring_full, 1)
                    elif name == "mt":
                        pe.wait_ge(ring_free["dve"], ring.emptied(b, 15)[1])
                        pe.wait_ge(rsum_done, b * TB)
                        for q in range(TB):
                            m = pe.transpose(SB[0:FH, P * q:P * q + P], negm[:, q, :], K["ident"][:, :])
                        m.then_inc(mt_full, 1)
                    elif name == "st":
                        if i == 0:
                            pe.wait_ge(mrow_done, b + 1)
                        for j in range(TB):
                            n = ST_AT + TB * i + j
                            turn_wait(ring, ring_free, b, n)
                            q0 = P * min(j, TB - 2)
                            for hh in range(2):
                                h = 2 * i + hh
                                o = RB[n % 4][:, 2 * P * hh:2 * P * hh + 2 * P]
                                key, qry = slice(P * j, P * j + P), slice(q0, q0 + 2 * P)
                                pe.matmul(o, k_hi[:, h, key], q_hi[:, i, qry], start=(hh == 0), stop=False,
                                          skip_group_check=True)
                                pe.matmul(o, k_hi[:, h, key], q_lo[:, i, qry], start=False, stop=False,
                                          skip_group_check=True)
                                pe.matmul(o, k_lo[:, h, key], q_hi[:, i, qry], start=False, stop=False,
                                          skip_group_check=True)
                                pe.matmul(o, pick[0:MK, h, :], mrow[0:MK, qry], start=False, stop=True,
                                          skip_group_check=True)
                            o = RB[n % 4][:, :].rearrange("p (h q) -> p h q", h=2)
                            if j < TB - 1:
                                mask = K["window_t"][:, :, :].rearrange("p b q -> p (b q)")
                            else:
                                o, mask = o[:, :, P:2 * P], K["window_t"][:, 0, :]
                            pe.matmul(o, K["identb"][:, :], mask.unsqueeze(1).to_broadcast([P, 2, mask.shape[1]]),
                                      start=False, stop=True, skip_group_check=True).then_inc(ring_full, 1)
                    elif name == "pv":
                        pe.wait_ge(ring_free["act"], ring.emptied(b, ST_AT + TB * i + TB - 1)[1])
                        pe.wait_ge(mrow_done, b + 1)
                        pe.wait_ge(z_done, b * TB + i)
                        pe.wait_ge(ln_done, b * TB + i)
                        pe.wait_ge(front_free["act"], b * TB + TB)
                        for j in range(TB):
                            nq = P if j == TB - 1 else 2 * P
                            for hh in range(2):
                                h, rows = 2 * i + hh, slice(FD * hh, FD * hh + FD)
                                pe.matmul(OB[rows, P * j:P * j + nq], V[:, j, FD * h:FD * h + FD],
                                          PT[:, i % 2, j, hh, 0:nq], start=(j == 0), stop=(j == TB - 1),
                                          skip_group_check=True)
                            for hh in range(2):
                                rows = slice(FD * hh, FD * hh + FD)
                                m = pe.matmul(SB[rows, P * j:P * j + nq], ones[:, :], PT[:, i % 2, j, hh, 0:nq],
                                              start=(j == 0), stop=(j == TB - 1), skip_group_check=True)
                        m.then_inc(o_full, 1)
                    elif name == "out":
                        pe.wait_ge(z_done, b * TB + TB)
                        for t in range(TB):
                            n = OUT_AT + t
                            turn_wait(ring, ring_free, b, n)
                            for p in range(INNER // P):
                                m = pe.matmul(RB[n % 4][:, 0:DM], zt[:, p, P * t:P * t + P], wo[:, p, :],
                                              start=(p == 0), stop=(p == INNER // P - 1))
                            m.then_inc(ring_full, 1)

                steps(pe, do)


def feed_forward(nc, K, lay, x, ln_g, ln_b, w1_w, b1_w, w2_w, b2_w, residual, dst):
    with ExitStack() as ctx:
        sb = lambda name, shape, dt=F32: ctx.enter_context(nc.sbuf_tensor(f"m{lay}_" + name, shape, dt))
        ps = lambda name, shape: ctx.enter_context(nc.psum_tensor(f"m{lay}_" + name, shape, F32))
        sem = lambda name: ctx.enter_context(nc.semaphore(f"m{lay}_" + name))
        last = residual is not None
        loads = 3 + 3 * NT

        w_raw = sb("w_raw", [P, KT, 2 * HID])
        w_hi, w_lo = sb("w_hi", [P, KT, 2 * HID], F32R), sb("w_lo", [P, KT, 2 * HID], F32R)
        w2 = sb("w2", [HT, NT, DM])
        b1 = sb("b1", [HT, 2, NT])
        gam, bet = sb("gam", [P, KT]), sb("bet", [P, KT])
        b2 = sb("b2", [P, DM])
        h = sb("h", [P, TB, DM])
        hn = sb("hn", [P, TB, DM])
        st, mv = sb("st", [P, TB, 6]), sb("mv", [P, TB, 2])
        ve, rs, half = sb("ve", [P, TB]), sb("rs", [P, TB]), sb("half", [P, TB])
        ht = sb("ht", [P, KT, S])
        ht_hi, ht_lo = sb("ht_hi", [P, KT, S], F32R), sb("ht_lo", [P, KT, S], F32R)
        gate = sb("gate", [HT, 2, S])
        hid = sb("hid", [HT, NT, S])
        xr = sb("xr", [P, TB, DM])
        res = sb("res", [P, TB, DM])
        y, out = sb("y", [P, TB, DM]), sb("out", [P, TB, DM])
        st2, mv2 = sb("st2", [P, TB, 6]), sb("mv2", [P, TB, 2])
        ve2, rs2 = sb("ve2", [P, TB]), sb("rs2", [P, TB])

        FB = [ps("f0", [P, S]), ps("f1", [P, S])]
        AB = [[ps(f"a{i}", [P, S]), ps(f"g{i}", [P, S])] for i in range(2)]
        WB = [ps("w0", [P, S]), ps("w1", [P, S])]

        w_loaded, loaded, w_hi_done, w_lo_done = sem("w_loaded"), sem("loaded"), sem("w_hi_done"), sem("w_lo_done")
        half_set = sem("half_set")
        h_in, stats, var_done, ve_done, rstd_done = (
            sem("h_in"), sem("stats"), sem("var_done"), sem("ve_done"), sem("rstd_done"))
        normed, turned, scaled, hi_done, lo_done = (
            sem("normed"), sem("turned"), sem("scaled"), sem("hi_done"), sem("lo_done"))
        ag_full, gate_done, hid_done = sem("ag_full"), sem("gate_done"), sem("hid_done")
        w2_full, y_done, xr_in, res_in, xb_done, stored = (
            sem("w2_full"), sem("y_done"), sem("xr_in"), sem("res_in"), sem("xb_done"), sem("stored"))
        stats2, var2_done, ve2_done, rstd2_done, out_done = (
            sem("stats2"), sem("var2_done"), sem("ve2_done"), sem("rstd2_done"), sem("out_done"))

        STEPS = [("xr", 0)] + [("w1", n) for n in range(3)] + [("f_n", 0)] + [("w1", n) for n in range(3, NT)] \
            + [("f_t", 0), ("w2", 0)]

        def steps(eng, do):
            for name, i in STEPS:
                if name[0] == "f":
                    do(name, i, 0)
            with eng.Fori(0, NB - 1) as it:
                for name, i in STEPS:
                    do(name, i, it + 1 if name[0] == "f" else it)
            for name, i in STEPS:
                if name[0] != "f":
                    do(name, i, NB - 1)

        with nc.Block() as block:
            @block.sync
            def _(sp):
                sp.dma_start(w_raw[:, :, :], w1_w.rearrange("(k p) n -> p k n", p=P)).then_inc(w_loaded, 16)
                sp.dma_start(gam[:, :], ln_g.rearrange("(k p) -> p k", p=P),
                             allow_slow_non_contiguous=True).then_inc(loaded, 16)
                sp.dma_start(bet[:, :], ln_b.rearrange("(k p) -> p k", p=P),
                             allow_slow_non_contiguous=True).then_inc(loaded, 16)
                for n in range(NT):
                    rows = tile_rows(n)
                    for k in range(2):
                        sp.dma_start(b1[0:rows, k, n:n + 1],
                                     b1_w[HID * k + HT * n:HID * k + HT * n + rows].unsqueeze(1),
                                     allow_slow_non_contiguous=True).then_inc(loaded, 16)
                    sp.dma_start(w2[0:rows, n, :], w2_w[HT * n:HT * n + rows]).then_inc(loaded, 16)
                sp.dma_start(b2[:, :], b2_w.partition_broadcast(P)).then_inc(loaded, 16)

                def do(name, i, b):
                    if name == "f_n":
                        if not isinstance(b, int):
                            sp.wait_ge(normed, b * TB)
                        sp.dma_start(h[:, :, 0:P], x[b, 1:1 + S, 0:P].rearrange("(t p) d -> p t d", p=P))\
                            .then_inc(h_in, 16)
                        sp.dma_start(h[:, :, P:DM], x[b, 0:S, P:DM].rearrange("(t p) d -> p t d", p=P))\
                            .then_inc(h_in, 16)
                    elif name == "xr":
                        sp.wait_ge(y_done, b * TB)
                        sp.dma_start(xr[:, :, :], x[b, 1:1 + S].rearrange("(t p) d -> p t d", p=P))\
                            .then_inc(xr_in, 16)
                        if last:
                            sp.dma_start(res[:, :, :], residual[b, 1:1 + S].rearrange("(t p) d -> p t d", p=P))\
                                .then_inc(res_in, 16)
                    elif name == "w2":
                        sp.wait_ge(out_done if last else y_done, b * TB + TB)
                        sp.dma_start(dst[b].rearrange("(t p) d -> p t d", p=P),
                                     (out if last else y)[:, :, :]).then_inc(stored, 16)

                steps(sp, do)
                sp.wait_ge(stored, 16 * NB)

            @block.gpsimd
            def _(pool):
                pool.memset(half[:, :], -0.5).then_inc(half_set, 1)
                pool.wait_ge(half_set, 1)
                pool.wait_ge(loaded, 16 * loads)

                def do(name, i, b):
                    if name == "xr":
                        pool.wait_ge(xr_in, b * 16 + 16)
                        pool.tensor_tensor(xr[:, :, :], xr[:, :, :],
                                           b2[:, :].unsqueeze(1).to_broadcast([P, TB, DM]), ALU.add)\
                            .then_inc(xb_done, 1)
                        if last:
                            pool.wait_ge(res_in, b * 16 + 16)
                            pool.wait_ge(xb_done, b * 2 + 1)
                            pool.tensor_tensor(xr[:, :, :], xr[:, :, :], res[:, :, :], ALU.add)\
                                .then_inc(xb_done, 1)
                    elif name == "f_n":
                        wait_apart(pool, K, var_done, b + 1)
                        pool.tensor_scalar(ve[:, :], mv[:, :, 1], LN_EPS, None, ALU.add).then_inc(ve_done, 1)
                        pool.wait_ge(ve_done, b + 1)
                        pool.tensor_tensor(rs[:, :], ve[:, :], half[:, :], ALU.pow).then_inc(rstd_done, 1)
                    elif name == "f_t":
                        for k in range(KT):
                            pool.wait_ge(hi_done, b * KT + k + 1)
                            pool.tensor_tensor(ht_lo[:, k, :], ht[:, k, :], ht_hi[:, k, :], ALU.subtract)\
                                .then_inc(lo_done, 1)
                    elif name == "w2" and last:
                        wait_apart(pool, K, var2_done, b + 1)
                        pool.tensor_scalar(ve2[:, :], mv2[:, :, 1], LN_EPS, None, ALU.add).then_inc(ve2_done, 1)
                        pool.wait_ge(ve2_done, b + 1)
                        pool.tensor_tensor(rs2[:, :], ve2[:, :], half[:, :], ALU.pow).then_inc(rstd2_done, 1)

                steps(pool, do)

            @block.scalar
            def _(act):
                act.wait_ge(w_loaded, 16)
                for k in range(KT):
                    nc.scalar.activation(w_hi[:, k, :], w_raw[:, k, :], ACT.Copy).then_inc(w_hi_done, 1)
                act.wait_ge(loaded, 16 * loads)

                def do(name, i, b):
                    if name == "f_t":
                        for k in range(KT):
                            act.wait_ge(turned, b * KT + k + 1)
                            nc.scalar.activation(ht[:, k, :], FB[k][:, :], ACT.Identity, bias=bet[:, k:k + 1],
                                                 scale=gam[:, k:k + 1]).then_inc(scaled, 1)
                    elif name == "w1":
                        n, rows = b * NT + i, tile_rows(i)
                        act.wait_ge(ag_full, n + 1)
                        act.wait_ge(hid_done, b * NT + max(i - 1, 0))
                        nc.scalar.activation(gate[0:rows, i % 2, :], AB[i % 2][1][0:rows, :], ACT.Gelu,
                                             bias=b1[0:rows, 1, i:i + 1]).then_inc(gate_done, 1)

                steps(act, do)

            @block.vector
            def _(dve):
                for k in range(KT):
                    dve.wait_ge(w_hi_done, k + 1)
                    dve.tensor_tensor(w_lo[:, k, :], w_raw[:, k, :], w_hi[:, k, :], ALU.subtract)\
                        .then_inc(w_lo_done, 1)
                dve.wait_ge(loaded, 16 * loads)

                def do(name, i, b):
                    if name == "f_n":
                        dve.wait_ge(h_in, b * 32 + 32)
                        for t in range(TB):
                            dve.bn_stats(st[:, t, :], h[:, t, :]).then_inc(stats, 1)
                        for t in range(TB):
                            wait_apart(dve, K, stats, b * TB + t + 1)
                            m = dve.bn_aggr(mv[:, t, :], st[:, t, :])
                        m.then_inc(var_done, 1)
                        dve.wait_ge(rstd_done, b + 1)
                        if not isinstance(b, int):
                            dve.wait_ge(turned, b * KT)
                        for t in range(TB):
                            dve.tensor_scalar(hn[:, t, :], h[:, t, :], mv[:, t, 0:1], rs[:, t:t + 1],
                                              ALU.subtract, ALU.mult).then_inc(normed, 1)
                    elif name == "f_t":
                        for k in range(KT):
                            dve.wait_ge(scaled, b * KT + k + 1)
                            dve.wait_ge(turned, b * KT + k + 1)
                            dve.tensor_copy(ht_hi[:, k, :], ht[:, k, :]).then_inc(hi_done, 1)
                    elif name == "w1":
                        n, rows = b * NT + i, tile_rows(i)
                        dve.wait_ge(gate_done, n + 1)
                        dve.scalar_tensor_tensor(out=hid[0:rows, i, :], in0=AB[i % 2][0][0:rows, :],
                                                 scalar=b1[0:rows, 0, i:i + 1], in1=gate[0:rows, i % 2, :],
                                                 op0=ALU.add, op1=ALU.mult).then_inc(hid_done, 1)
                    elif name == "w2":
                        dve.wait_ge(xb_done, (b + 1) * (2 if last else 1))
                        if not last:
                            dve.wait_ge(stored, b * 16)
                        else:
                            dve.wait_ge(out_done, b * TB)
                        for t in range(TB):
                            dve.wait_ge(w2_full, b * TB + t + 1)
                            dve.tensor_tensor(y[:, t, :], WB[t % 2][:, 0:DM], xr[:, t, :], ALU.add)\
                                .then_inc(y_done, 1)
                        if last:
                            for t in range(TB):
                                dve.wait_ge(y_done, b * TB + t + 1)
                                dve.bn_stats(st2[:, t, :], y[:, t, :]).then_inc(stats2, 1)
                            for t in range(TB):
                                wait_apart(dve, K, stats2, b * TB + t + 1)
                                m = dve.bn_aggr(mv2[:, t, :], st2[:, t, :])
                            m.then_inc(var2_done, 1)
                            dve.wait_ge(rstd2_done, b + 1)
                            dve.wait_ge(stored, b * 16)
                            for t in range(TB):
                                dve.tensor_scalar(out[:, t, :], y[:, t, :], mv2[:, t, 0:1], rs2[:, t:t + 1],
                                                  ALU.subtract, ALU.mult).then_inc(out_done, 1)

                steps(dve, do)

            @block.tensor
            def _(pe):
                def split_mm(o, a_hi, a_lo, r_hi, r_lo, first, last):
                    pe.matmul(o, a_hi, r_hi, start=first, stop=False)
                    pe.matmul(o, a_lo, r_hi, start=False, stop=False)
                    return pe.matmul(o, a_hi, r_lo, start=False, stop=last)

                pe.wait_ge(w_lo_done, 2)
                pe.wait_ge(loaded, 16 * loads)

                def do(name, i, b):
                    if name == "f_t":
                        pe.wait_ge(normed, b * TB + TB)
                        for k in range(KT):
                            if not isinstance(b, int):
                                pe.wait_ge(scaled, b * KT + k - 1)
                            for t in range(TB):
                                m = pe.transpose(FB[k][:, P * t:P * t + P], hn[:, t, P * k:P * k + P],
                                                 K["ident"][:, :])
                            m.then_inc(turned, 1)
                    elif name == "w1":
                        rows = tile_rows(i)
                        if i == 0:
                            pe.wait_ge(lo_done, b * KT + KT)
                        pe.wait_ge(hid_done, b * NT + max(i - 1, 0))
                        for k in range(2):
                            col = slice(HID * k + HT * i, HID * k + HT * i + rows)
                            for f in range(KT):
                                m = split_mm(AB[i % 2][k][0:rows, :], w_hi[:, f, col], w_lo[:, f, col],
                                             ht_hi[:, f, :], ht_lo[:, f, :], f == 0, f == KT - 1)
                        m.then_inc(ag_full, 1)
                    elif name == "w2":
                        pe.wait_ge(hid_done, b * NT + NT)
                        for t in range(TB):
                            pe.wait_ge(y_done, b * TB + max(t - 1, 0))
                            for n in range(NT):
                                rows = tile_rows(n)
                                m = pe.matmul(WB[t % 2][:, 0:DM], hid[0:rows, n, P * t:P * t + P],
                                              w2[0:rows, n, :], start=(n == 0), stop=(n == NT - 1))
                            m.then_inc(w2_full, 1)

                steps(pe, do)


def rotary():
    half = np.arange(0, FD, 2, dtype=np.float32)
    inv_freq = (np.float32(1.0) / np.float32(10000.0) ** (half / np.float32(FD))).astype(np.float32)
    t = np.arange(S, dtype=np.float32)
    freqs = t[:, None] * inv_freq[None, :]
    freqs = np.concatenate([freqs, freqs], -1)
    base = (half + np.float32(0.4 * FD)) / np.float32(1.4 * FD)
    power = (t - np.float32(S // 2)) / np.float32(P // 2)
    scale = base[None, :].astype(np.float64) ** power[:, None].astype(np.float64)
    scale = np.concatenate([scale, scale], -1)
    cos, sin = np.cos(freqs.astype(np.float64)), np.sin(freqs.astype(np.float64))
    return np.stack([np.stack([cos * scale, sin * scale]), np.stack([cos / scale, sin / scale])]).astype(np.float32)


NAMES = ["L0_attn_x", "L0_attn_w_qkv", "L0_attn_b_qkv", "L0_attn_w_out", "L0_attn_b_out", "L0_ffn_wqkv",
         "L0_ffn_q_scale", "L0_ffn_k_scale", "L0_ffn_wo", "L0_ffn_ln_g", "L0_ffn_ln_b", "L0_ffn_w1", "L0_ffn_b1",
         "L0_ffn_w2", "L0_ffn_b2", "rot"]


def program(nc, t, out):
    dram = lambda name, shape: nc.dram_tensor(name, shape, F32, kind="Internal").ap()
    scr = dram("qk_parts", [NB, 2, 4 * P, S])
    after_first = dram("after_first", [NB, S + 1, DM])
    after_attn = [dram(f"after_attn{i}", [NB, S + 1, DM]) for i in range(DEPTH)]
    after_layer = dram("after_layer", [NB, S + 1, DM])
    with ExitStack() as ctx:
        K = constants(nc, ctx)
        zero = ctx.enter_context(nc.sbuf_tensor("zero_row", [NB, DM], F32))
        zero_set = ctx.enter_context(nc.semaphore("zero_set"))
        zero_out = ctx.enter_context(nc.semaphore("zero_out"))
        with nc.Block() as block:
            @block.vector
            def _(dve):
                dve.memset(zero[:, :], 0.0).then_inc(zero_set, 1)

            @block.sync
            def _(sp):
                sp.wait_ge(zero_set, 1)
                for a in after_attn:
                    sp.dma_start(a[:, 0, :], zero[:, :]).then_inc(zero_out, 16)
                sp.wait_ge(zero_out, 16 * DEPTH)

        first_attention(nc, K, scr, t["L0_attn_x"], t["L0_attn_w_qkv"], t["L0_attn_b_qkv"], t["L0_attn_w_out"],
                        t["L0_attn_b_out"], after_first)
        x = after_first
        for i in range(DEPTH):
            local_attention(nc, K, i, x[:, 1:], t["L0_ffn_wqkv"][i], t["L0_ffn_q_scale"][i],
                            t["L0_ffn_k_scale"][i], t["L0_ffn_wo"][i], t["rot"], after_attn[i])
            last = i == DEPTH - 1
            feed_forward(nc, K, i, after_attn[i], t["L0_ffn_ln_g"][i], t["L0_ffn_ln_b"][i], t["L0_ffn_w1"][i],
                         t["L0_ffn_b1"][i], t["L0_ffn_w2"][i], t["L0_ffn_b2"][i], after_first if last else None,
                         out if last else after_layer[:, 1:])
            x = after_layer


def kernel(**inputs):
    import concourse.bacc as bacc
    from concourse.bass_utils import run_bass_kernel_spmd

    nc = bacc.Bacc("TRN2", target_bir_lowering=False, num_devices=1)
    arrays = {f"in_{n}": np.ascontiguousarray(rotary() if n == "rot" else inputs[n]) for n in NAMES}
    t = {n: nc.dram_tensor(f"in_{n}", arrays[f"in_{n}"].shape, F32, kind="ExternalInput").ap() for n in NAMES}
    out = nc.dram_tensor("out", [NB, S, DM], F32, kind="ExternalOutput").ap()
    program(nc, t, out)
    return run_bass_kernel_spmd(nc, [arrays], core_ids=[0]).results[0]["out"]
```

```python
from contextlib import ExitStack

import numpy as np

import concourse.bass as bass
from concourse import mybir

F32 = mybir.dt.float32
F32R = mybir.dt.float32r
BF16 = mybir.dt.bfloat16
ALU = mybir.AluOpType
ACT = mybir.ActivationFunctionType
AX = mybir.AxisListType

P = 128
NEG = -1.0e30
MADE = 15
LN_EPS = 1e-5

NB, S, DM = 8, 512, 256
TB = S // P
KT = DM // P
AH, AD = 16, 16
HP = 4
AG = AH // HP
FH, FD = 8, 64
INNER = FH * FD
HID = 682
NT = 6
HT = 114
DEPTH = 2


def tile_rows(n):
    return min(HT, HID - n * HT)


class Uses:

    def __init__(self, consumers, depth):
        self.c, self.depth = consumers, depth

    def filled(self, b, n):
        return b * len(self.c) + n + 1

    def emptied(self, b, n):
        eng = self.c[n]
        return eng, b * self.c.count(eng) + self.c[:n + 1].count(eng)

    def before(self, b, n):
        if n >= self.depth:
            return [self.emptied(b, n - self.depth)]
        if isinstance(b, int) and b == 0:
            return []
        return [(e, b * self.c.count(e)) for e in sorted(set(self.c))]


def wait_apart(eng, K, sem, value):
    if not isinstance(value, int):
        value = eng.snap(eng.to_reg(value))
        eng.wait_ge(K["made"], MADE)
    eng.wait_ge(sem, value)


def constants(nc, ctx):
    sb = lambda name, shape, dt: ctx.enter_context(nc.sbuf_tensor(name, shape, dt))
    k = {
        "ident": sb("ident", [P, P], F32),
        "identb": sb("identb", [P, P], BF16),
        "causal": sb("causal", [P, P], BF16),
        "window": sb("window", [P, 2, P], BF16),
        "window0": sb("window0", [P, 2, P], BF16),
        "window_t": sb("window_t", [P, 2, P], BF16),
    }
    made = k["made"] = ctx.enter_context(nc.semaphore("const_made"))
    with nc.Block() as block:
        @block.gpsimd
        def _(pool):
            pool.memset(k["ident"][:, :], 0.0).then_inc(made, 1)
            pool.memset(k["identb"][:, :], 0.0).then_inc(made, 1)
            pool.memset(k["causal"][:, :], 0.0).then_inc(made, 1)
            pool.memset(k["window"][:, :, :], 0.0).then_inc(made, 1)
            pool.memset(k["window0"][:, 0, :], 0.0).then_inc(made, 1)
            pool.memset(k["window0"][:, 1, :], NEG).then_inc(made, 1)
            pool.memset(k["window_t"][:, :, :], 0.0).then_inc(made, 1)
            pool.wait_ge(made, 7)
            for m in (k["ident"], k["identb"]):
                pool.affine_select(out=m[:, :], in_=m[:, :], compare_op=ALU.not_equal, fill=1.0, base=0,
                                   pattern=[[-1, P]], channel_multiplier=1).then_inc(made, 1)
            for m in (k["causal"][:, :], k["window"][:, 1, :], k["window0"][:, 0, :]):
                pool.affine_select(out=m, in_=m, compare_op=ALU.is_ge, fill=NEG, base=0,
                                   pattern=[[-1, P]], channel_multiplier=1).then_inc(made, 1)
            pool.affine_select(out=k["window"][:, 0, :], in_=k["window"][:, 0, :], compare_op=ALU.is_ge,
                               fill=NEG, base=0, pattern=[[1, P]], channel_multiplier=-1).then_inc(made, 1)
            pool.affine_select(out=k["window_t"][:, 0, :], in_=k["window_t"][:, 0, :], compare_op=ALU.is_ge,
                               fill=NEG, base=0, pattern=[[1, P]], channel_multiplier=-1).then_inc(made, 1)
            pool.affine_select(out=k["window_t"][:, 1, :], in_=k["window_t"][:, 1, :], compare_op=ALU.is_ge,
                               fill=NEG, base=0, pattern=[[-1, P]], channel_multiplier=1).then_inc(made, 1)
            pool.wait_ge(made, MADE)
    return k


def first_attention(nc, K, scr, x, w_qkv, b_qkv, w_out, b_out, dst):
    with ExitStack() as ctx:
        sb = lambda name, shape, dt=F32: ctx.enter_context(nc.sbuf_tensor("a_" + name, shape, dt))
        ps = lambda name, shape: ctx.enter_context(nc.psum_tensor("a_" + name, shape, F32))
        signals = []

        def sem(name):
            signals.append(nc.alloc_semaphore(name="a_" + name))
            return signals[-1]


        w_hi, w_lo = sb("w_hi", [P, KT, 3 * DM], F32R), sb("w_lo", [P, KT, 3 * DM], F32R)
        wo_hi, wo_lo = sb("wo_hi", [P, AG, DM], F32R), sb("wo_lo", [P, AG, DM], F32R)
        bqk = sb("bqk", [P, 4])
        bv, bo = sb("bv", [P, DM]), sb("bo", [P, DM])
        xin = sb("xin", [P, TB, DM])
        xt_hi, xt_lo = sb("xt_hi", [P, KT, S], F32R), sb("xt_lo", [P, KT, S], F32R)
        part_f = sb("part_f", [P, 2, S])
        qk_hi, qk_lo = sb("qk_hi", [P, 4, S], F32R), sb("qk_lo", [P, 4, S], F32R)
        MROW = 96
        Q, Kk = sb("Q", [P, AH, S], F32R), sb("K", [P, AH, S], F32R)
        V = sb("V", [P, TB, AH, 32])
        negm = sb("negm", [P, TB, AH])
        mrow = sb("mrow", [HP, AG, S], F32R)
        QOFF = [0, 512, 896, 1152]
        PT = sb("PT", [P, 2, HP, 1280])
        room = PT[:, 0].rearrange("p h q -> p (h q)")
        w_raw = room[:, 0:KT * 3 * DM].rearrange("p (k n) -> p k n", k=KT)
        wo = room[:, KT * 3 * DM:KT * 3 * DM + AG * DM].rearrange("p (g n) -> p g n", g=AG)
        NC = S // 32
        ot, on = sb("ot", [P, NC, 32]), sb("on", [P, NC, 32], F32R)
        zn, rc = sb("zn", [P, NC, AD]), sb("rc", [P, NC])
        ztf = sb("ztf", [P, S])
        zt = sb("zt", [P, AG, S], F32R)
        xr = sb("xr", [P, TB, DM])
        y, out = sb("y", [P, TB, DM]), sb("out", [P, TB, DM])
        st, mv = sb("st", [P, TB, 6]), sb("mv", [P, TB, 2])
        ve, rs, half = sb("ve", [P, TB]), sb("rs", [P, TB]), sb("half", [P, TB])

        FB = [ps("f0", [P, S]), ps("f1", [P, S])]
        MX = [ps("x0", [P, S]), ps("x1", [P, S])]
        SC = [ps("c0", [P, S]), ps("c1", [P, S])]
        OB, MB = ps("o", [P, S]), ps("m", [P, S])
        YB = [OB, MB]

        w_loaded, w_split, wo_loaded = sem("w_loaded"), sem("w_split"), sem("wo_loaded")
        wo_split, stacks_set = sem("wo_split"), sem("stacks_set")
        x_in, front_full, front_free = sem("x_in"), sem("front_full"), sem("front_free")
        lo_done, v_done = sem("lo_done"), sem("v_done")
        parts_out = sem("parts_out")
        stacked = [sem(f"stacked{g}") for g in range(AG)]
        mx_full, max_done, sc_full, exp_done = sem("mx_full"), sem("max_done"), sem("sc_full"), sem("exp_done")
        y_full, y_done = sem("y_full"), sem("y_done")
        mt_full, mrow_done = sem("mt_full"), sem("mrow_done")
        m_in = [sem(f"m_in{g}") for g in range(AG)]
        o_full, o_free, z_done = sem("o_full"), sem("o_free"), sem("z_done")
        xr_in, xb_ready = sem("xr_in"), sem("xb_ready")
        v_set = sem("v_set")
        stats, var_done, rstd_a, rstd_done = sem("stats"), sem("var_done"), sem("rstd_a"), sem("rstd_done")
        norm, zn_split, z_turned = sem("norm"), sem("zn_split"), sem("z_turned")
        out_done, stored = sem("out_done"), sem("stored")

        NF = 10
        UNITS = AH * TB
        GU = HP * TB
        AHEAD = GU + 12

        BEHIND = {3: [("f_x", 0)], 5: [("mt", 1), ("f_xe", 0)], 12: [("f_qk", 0)], 14: [("f_qe", 0)],
                  16: [("f_qk", 1)], 18: [("f_qe", 1)], 20: [("pv", 0)], 22: [("z0", 0), ("mt", 2)],
                  24: [("z1", 0)], 25: [("f_load", 0)], 28: [("z2", 0)], 29: [("f_qk", 2)], 30: [("z3", 0)],
                  31: [("f_qe", 2)], 34: [("f_load", 1), ("xr", 0)], 36: [("pv", 1)],
                  38: [("z0", 1), ("mt", 3)], 40: [("z1", 1)], 44: [("z2", 1), ("f_qk", 3)],
                  46: [("z3", 1)], 47: [("f_qe", 3)], 50: [("f_load", 2)], 52: [("pv", 2)],
                  54: [("z0", 2), ("f_mt", 0)], 56: [("z1", 2)], 60: [("z2", 2)], 62: [("z3", 2)]}
        STEPS = []
        for k in range(UNITS):
            u = k + AHEAD
            STEPS += [("sm", u) if u < UNITS else ("f_sm", u - UNITS), ("st", k)] + BEHIND.get(k, [])
        late = [("f_sm", AHEAD - n) for n in (3, 2, 1)]
        STEPS = [s for s in STEPS if s not in late] + late
        STEPS += [("pv", 3), ("f_load", 3), ("z0", 3), ("z1", 3), ("z2", 3), ("f_v", 0), ("z3", 3), ("out", 0)]
        first = [s for s in STEPS if s[0][0] == "f" and s[0] not in ("f_sm", "f_mt")]
        FIRST = first + [("f_sm", u) for u in range(GU)] + [("f_mt", 0)] + [("f_sm", u) for u in range(GU, AHEAD)]

        def steps(eng, do):
            for name, i in FIRST:
                do(name, i, 0)
            with eng.Fori(0, NB - 1) as it:
                for name, i in STEPS:
                    do(name, i, it + 1 if name[0] == "f" else it)
            for name, i in STEPS:
                if name[0] != "f":
                    do(name, i, NB - 1)

        with nc.Block() as block:
            @block.sync
            def _(sp):
                sp.dma_start(xin[:, :, :], x[0].rearrange("(t p) d -> p t d", p=P)).then_inc(x_in, 16)
                sp.dma_start(w_raw[:, :, :], w_qkv.rearrange("(k p) n -> p k n", p=P)).then_inc(w_loaded, 16)
                for m, c in enumerate((0, DM, P, DM + P)):
                    sp.dma_start(bqk[:, m:m + 1], b_qkv[c:c + P].unsqueeze(1),
                                 allow_slow_non_contiguous=True).then_inc(w_loaded, 16)
                sp.dma_start(bv[:, :], b_qkv[2 * DM:].partition_broadcast(P)).then_inc(w_loaded, 16)
                sp.dma_start(bo[:, :], b_out.partition_broadcast(P)).then_inc(w_loaded, 16)
                wo_rows = w_out.rearrange("(g j d) n -> j d g n", j=HP, d=AD)
                for r in range(2 * HP):
                    sp.dma_start(wo[AD * r:AD * r + AD, :, :], wo_rows[r // 2]).then_inc(wo_loaded, 16)

                def do(name, i, b):
                    if name == "f_x":
                        if not isinstance(b, int):
                            sp.wait_ge(front_full, (b - 1) * NF + 2)
                            sp.dma_start(xin[:, :, :], x[b].rearrange("(t p) d -> p t d", p=P)).then_inc(x_in, 16)
                    elif name == "f_qe":
                        sp.wait_ge(front_free, b * NF + 3 + i)
                        sp.dma_start(scr[b, 0, P * i:P * i + P], qk_hi[:, i, :].bitcast(F32)).then_inc(parts_out, 16)
                        sp.wait_ge(lo_done, b * 6 + 3 + i)
                        sp.dma_start(scr[b, 1, P * i:P * i + P], qk_lo[:, i, :].bitcast(F32)).then_inc(parts_out, 16)
                    elif name == "f_load":
                        wait_apart(sp, K, parts_out, b * 128 + 64 * (i // 2 + 1))
                        if i == 0 and isinstance(b, int):
                            sp.wait_ge(stacks_set, 2)
                            sp.wait_ge(v_set, 3)
                        if not isinstance(b, int):
                            sp.wait_ge(sc_full, (b - 1) * UNITS + GU * (i + 1))
                        r0, t0 = 64 * (i % 2), 2 * (i // 2)
                        for t, dst_t, order in ((t0, Q, (0, 0, 1)), (t0 + 1, Kk, (0, 1, 0))):
                            for slot, part in enumerate(order):
                                sp.dma_start(
                                    dst_t[AD * slot:AD * slot + AD, HP * i:HP * i + HP, :].bitcast(F32),
                                    scr[b, part, P * t + r0:P * t + r0 + 64]
                                    .rearrange("(h d) n -> d h n", d=AD)).then_inc(stacked[i], 16)
                    elif name in ("mt", "f_mt"):
                        sp.wait_ge(mrow_done, b * AG + i + 1)
                        for j in range(HP):
                            sp.dma_start(Q[MROW:MROW + 1, HP * i + j, :].bitcast(F32),
                                         mrow[j:j + 1, i, :].bitcast(F32)).then_inc(m_in[i], 16)

                steps(sp, do)

            @block.gpsimd
            def _(pool):
                pool.memset(half[:, :], -0.5).then_inc(rstd_a, 1)
                pool.memset(Kk[:, :, :].bitcast(F32), 0.0).then_inc(stacks_set, 1)
                pool.wait_ge(stacks_set, 1)
                pool.memset(Kk[MROW:MROW + 1, :, :].bitcast(F32), 1.0).then_inc(stacks_set, 1)

                pool.wait_ge(stacks_set, 2)

                def do(name, i, b):
                    if name == "xr":
                        pool.wait_ge(y_done, b * TB)
                        pool.dma_start(xr[:, :, :], x[b].rearrange("(t p) d -> p t d", p=P)).then_inc(xr_in, 16)
                        pool.wait_ge(xr_in, b * 16 + 16)
                        pool.wait_ge(w_loaded, 112)
                        pool.tensor_tensor(xr[:, :, :], xr[:, :, :],
                                           bo[:, :].unsqueeze(1).to_broadcast([P, TB, DM]), ALU.add)\
                            .then_inc(xb_ready, 1)
                    elif name == "f_xe":
                        for h in range(KT):
                            pool.wait_ge(front_free, b * NF + h + 1)
                            pool.tensor_tensor(xt_lo[:, h, :], part_f[:, h, :], xt_hi[:, h, :], ALU.subtract)\
                                .then_inc(lo_done, 1)
                    elif name == "f_qe":
                        pool.wait_ge(front_free, b * NF + 3 + i)
                        pool.wait_ge(parts_out, b * 128)
                        pool.tensor_tensor(qk_lo[:, i, :], part_f[:, i % 2, :], qk_hi[:, i, :], ALU.subtract)\
                            .then_inc(lo_done, 1)
                    elif name == "f_v":
                        pool.wait_ge(front_free, b * NF + NF)
                        vt = V[:, :, :, 0:AD]
                        pool.tensor_tensor(vt, vt, bv[:, :].rearrange("p (h d) -> p h d", d=AD).unsqueeze(1)
                                           .to_broadcast([P, TB, AH, AD]), ALU.add).then_inc(v_done, 1)
                    elif name == "z1" and i < AG - 1:
                        wait_apart(pool, K, norm, b * 8 + 2 * i + 2)
                        pool.tensor_copy(on[:, :, 0:AD], zn[:, :, :]).then_inc(zn_split, 1)
                        pool.wait_ge(zn_split, b * 8 + 2 * i + 1)
                        pool.tensor_tensor(on[:, :, AD:2 * AD], zn[:, :, :], on[:, :, 0:AD], ALU.subtract)\
                            .then_inc(zn_split, 1)
                    elif name == "out":
                        wait_apart(pool, K, var_done, b + 1)
                        pool.tensor_scalar(ve[:, :], mv[:, :, 1], LN_EPS, None, ALU.add).then_inc(rstd_a, 1)
                        pool.wait_ge(rstd_a, b + 2)
                        pool.tensor_tensor(rs[:, :], ve[:, :], half[:, :], ALU.pow).then_inc(rstd_done, 1)
                        wait_apart(pool, K, rstd_done, b + 1)
                        wait_apart(pool, K, stored, b * 16)
                        for t in range(TB):
                            pool.tensor_scalar(out[:, t, :], y[:, t, :], mv[:, t, 0:1], rs[:, t:t + 1],
                                               ALU.subtract, ALU.mult).then_inc(out_done, 1)
                        pool.wait_ge(out_done, b * TB + TB)
                        pool.dma_start(dst[b, 1:1 + S].rearrange("(t p) d -> p t d", p=P),
                                       out[:, :, :]).then_inc(stored, 16)

                steps(pool, do)
                pool.wait_ge(stored, 16 * NB)


            @block.scalar
            def _(act):
                act.wait_ge(w_loaded, 112)
                for kt in range(KT):
                    nc.scalar.activation(w_hi[:, kt, :], w_raw[:, kt, :], ACT.Copy).then_inc(w_split, 1)
                act.wait_ge(wo_loaded, 128)
                nc.scalar.activation(wo_hi[:, :, :], wo[:, :, :], ACT.Copy).then_inc(wo_split, 1)

                def do(name, i, b):
                    if name == "f_xe":
                        for h in range(KT):
                            act.wait_ge(front_full, b * NF + h + 1)
                            if not isinstance(b, int):
                                act.wait_ge(lo_done, b * 6 + h - 1)
                            nc.scalar.activation(xt_hi[:, h, :], FB[h][:, :], ACT.Identity)
                            nc.scalar.activation(part_f[:, h, :], FB[h][:, :], ACT.Identity)\
                                .then_inc(front_free, 1)
                    elif name == "f_qe":
                        act.wait_ge(front_full, b * NF + 3 + i)
                        act.wait_ge(parts_out, b * 128)
                        nc.scalar.activation(qk_hi[:, i, :], FB[i % 2][:, :], ACT.Identity,
                                             bias=bqk[:, i:i + 1])
                        act.wait_ge(lo_done, b * 6 + i + 1)
                        nc.scalar.activation(part_f[:, i % 2, :], FB[i % 2][:, :], ACT.Identity,
                                             bias=bqk[:, i:i + 1]).then_inc(front_free, 1)
                    elif name == "f_v":
                        act.wait_ge(v_set, 2)
                        for t in range(TB):
                            act.wait_ge(front_full, b * NF + 7 + t)
                            nc.scalar.activation(V[:, t, :, 0:AD], FB[t % 2][:, 0:DM]
                                                 .rearrange("p (h d) -> p h d", d=AD), ACT.Identity)\
                                .then_inc(front_free, 1)
                    elif name == "z3":
                        act.wait_ge(z_turned, b * AG + i + 1)
                        if i == 0:
                            act.wait_ge(y_full, b * TB)
                        nc.scalar.activation(zt[:, i, :], ztf[:, :], ACT.Identity).then_inc(z_done, 1)
                    elif name in ("mt", "f_mt"):
                        act.wait_ge(mt_full, b * AG + i + 1)
                        act.wait_ge(m_in[i], b * 64)
                        nc.scalar.activation(mrow[:, i, :], MB[0:HP, :], ACT.Identity).then_inc(mrow_done, 1)
                    elif name == "st":
                        j, h = i % TB, i // TB
                        act.wait_ge(sc_full, b * UNITS + i + 1)
                        q0 = max(P * j - S // 2, 0)
                        nq = S - P * j
                        nc.scalar.activation(PT[:, h // HP % 2, h % HP, QOFF[j]:QOFF[j] + nq],
                                             SC[i % 2][:, q0:q0 + nq], ACT.Exp, scale=AD ** -0.5)\
                            .then_inc(exp_done, 1)

                steps(act, do)

            @block.vector
            def _(dve):
                dve.memset(V[:, :, :, :], 0.0).then_inc(v_set, 1)
                dve.wait_ge(v_set, 1)
                dve.memset(V[:, :, :, AD:AD + 1], 1.0).then_inc(v_set, 1)
                dve.memset(Q[:, :, :].bitcast(F32), 0.0).then_inc(v_set, 1)
                dve.wait_ge(w_split, 2)
                for kt in range(KT):
                    dve.tensor_tensor(w_lo[:, kt, :], w_raw[:, kt, :], w_hi[:, kt, :], ALU.subtract)\
                        .then_inc(w_split, 1)
                dve.wait_ge(wo_split, 1)
                dve.tensor_tensor(wo_lo[:, :, :], wo[:, :, :], wo_hi[:, :, :], ALU.subtract).then_inc(wo_split, 1)

                def do(name, i, b):
                    if name in ("sm", "f_sm"):
                        q, h = i % TB, i // TB
                        dve.wait_ge(mx_full, b * UNITS + i + 1)
                        dve.tensor_reduce(negm[:, q, h:h + 1], MX[i % 2][:, 0:P * (q + 1)], AX.X, ALU.max,
                                          negate=True).then_inc(max_done, 1)
                    elif name == "z0":
                        dve.wait_ge(o_full, b * AG + i + 1)
                        dve.transpose(ot[:, :, :].rearrange("p c r -> p (c r)"), OB[:, :]).then_inc(o_free, 1)
                        dve.wait_ge(o_free, b * AG + i + 1)
                        dve.reciprocal(rc[:, :], ot[:, :, AD]).then_inc(norm, 1)
                    elif name == "z1":
                        dve.wait_ge(norm, b * 8 + 2 * i + 1)
                        dve.wait_ge(z_turned, b * AG + i)
                        dve.tensor_tensor(zn[:, :, :], ot[:, :, 0:AD],
                                          rc[:, :].unsqueeze(2).to_broadcast([P, NC, AD]), ALU.mult)\
                            .then_inc(norm, 1)
                        if i == AG - 1:
                            dve.wait_ge(norm, b * 8 + 2 * i + 2)
                            dve.tensor_copy(on[:, :, 0:AD], zn[:, :, :]).then_inc(zn_split, 1)
                            dve.wait_ge(zn_split, b * 8 + 2 * i + 1)
                            dve.tensor_tensor(on[:, :, AD:2 * AD], zn[:, :, :], on[:, :, 0:AD], ALU.subtract)\
                                .then_inc(zn_split, 1)
                    elif name == "z2":
                        dve.wait_ge(zn_split, b * 8 + 2 * i + 2)
                        dve.wait_ge(z_done, b * AG + i)
                        dve.transpose(ztf[:, :], on[:, :, :].rearrange("p c r -> p (c r)").bitcast(F32))\
                            .then_inc(z_turned, 1)
                    elif name == "out":
                        dve.wait_ge(xb_ready, b + 1)
                        dve.wait_ge(out_done, b * TB)
                        for t in range(TB):
                            dve.wait_ge(y_full, b * TB + t + 1)
                            dve.tensor_tensor(y[:, t, :], YB[t % 2][:, 0:DM], xr[:, t, :], ALU.add)\
                                .then_inc(y_done, 1)
                            dve.wait_ge(y_done, b * TB + t + 1)
                            dve.bn_stats(st[:, t, :], y[:, t, :]).then_inc(stats, 1)
                        for t in range(TB):
                            wait_apart(dve, K, stats, b * TB + t + 1)
                            m = dve.bn_aggr(mv[:, t, :], st[:, t, :])
                        m.then_inc(var_done, 1)

                steps(dve, do)

            @block.tensor
            def _(pe):
                def split_mm(o, a_hi, a_lo, r_hi, r_lo, first, last):
                    pe.matmul(o, a_hi, r_hi, start=first, stop=False)
                    pe.matmul(o, a_lo, r_hi, start=False, stop=False)
                    return pe.matmul(o, a_hi, r_lo, start=False, stop=last)

                def pass_wait(done, b, i):
                    if isinstance(b, int) and b == 0 and i < 2:
                        return
                    pe.wait_ge(done, b * UNITS + max(i - 1, 0))


                def do(name, i, b):
                    if name == "f_x":
                        pe.wait_ge(x_in, b * 16 + 16)
                        for h in range(KT):
                            if not isinstance(b, int):
                                pe.wait_ge(front_free, b * NF + h - 1)
                            for t in range(TB):
                                m = pe.transpose(FB[h][:, P * t:P * t + P], xin[:, t, P * h:P * h + P],
                                                 K["ident"][:, :])
                            m.then_inc(front_full, 1)
                    elif name == "f_qk":
                        col = (0, DM, P, DM + P)[i]
                        pe.wait_ge(w_split, 4)
                        pe.wait_ge(front_free, b * NF + max(1 + i, 2))
                        pe.wait_ge(lo_done, b * 6 + 2)
                        for h in range(KT):
                            m = split_mm(FB[i % 2][:, :], w_hi[:, h, col:col + P], w_lo[:, h, col:col + P],
                                         xt_hi[:, h, :], xt_lo[:, h, :], h == 0, h == KT - 1)
                        m.then_inc(front_full, 1)
                    elif name == "f_v":
                        for t in range(TB):
                            pe.wait_ge(front_free, b * NF + 5 + t)
                            for h in range(KT):
                                tok = slice(P * t, P * t + P)
                                m = split_mm(FB[t % 2][:, 0:DM], xt_hi[:, h, tok], xt_lo[:, h, tok],
                                             w_hi[:, h, 2 * DM:], w_lo[:, h, 2 * DM:], h == 0, h == KT - 1)
                            m.then_inc(front_full, 1)
                    elif name in ("sm", "f_sm"):
                        q, h = i % TB, i // TB
                        if i % GU == 0:
                            pe.wait_ge(stacked[i // GU], b * 96 + 96)
                        pass_wait(max_done, b, i)
                        r, nk = MX[i % 2], max(P * (q + 1), 256)
                        pe.matmul(r[:, 0:nk], Q[0:MROW, h, P * q:P * q + P], Kk[0:MROW, h, 0:nk],
                                  start=True, stop=True)
                        pe.matmul(r[:, P * q:P * q + P], K["identb"][:, :], K["causal"][:, :], start=False,
                                  stop=True, skip_group_check=True).then_inc(mx_full, 1)
                    elif name in ("mt", "f_mt"):
                        pe.wait_ge(max_done, b * UNITS + GU * (i + 1))
                        pe.wait_ge(mrow_done, b * AG + i)
                        if name == "f_mt" and not isinstance(b, int):
                            pe.wait_ge(y_done, (b - 1) * TB)
                        for q in range(TB):
                            m = pe.transpose(MB[0:HP, P * q:P * q + P], negm[:, q, HP * i:HP * i + HP],
                                             K["ident"][:, :])
                        m.then_inc(mt_full, 1)
                    elif name == "st":
                        j, h = i % TB, i // TB
                        if i == 0:
                            pe.wait_ge(wo_split, 2)
                        if i % GU == 0:
                            pe.wait_ge(m_in[i // GU], b * 64 + 64)
                        pass_wait(exp_done, b, i)
                        q0, r = min(P * j, S // 2), SC[i % 2]
                        pe.matmul(r[:, 0:S - q0], Kk[0:MROW + 1, h, P * j:P * j + P], Q[0:MROW + 1, h, q0:S],
                                  start=True, stop=True)
                        pe.matmul(r[:, P * j - q0:P * j - q0 + P], K["identb"][:, :], K["window_t"][:, 0, :],
                                  start=False, stop=True, skip_group_check=True).then_inc(sc_full, 1)
                    elif name == "pv":
                        pe.wait_ge(exp_done, b * UNITS + GU * (i + 1))
                        pe.wait_ge(o_free, b * AG + i)
                        pe.wait_ge(y_done, b * TB)
                        pe.wait_ge(v_done, b + 1)
                        for j in range(TB):
                            for hh in range(HP):
                                m = pe.matmul(OB[32 * hh:32 * hh + 32, P * j:S], V[:, j, HP * i + hh, :],
                                              PT[:, i % 2, hh, QOFF[j]:QOFF[j] + S - P * j],
                                              start=(j == 0), stop=(j == TB - 1), skip_group_check=True)
                        m.then_inc(o_full, 1)
                    elif name == "out":
                        pe.wait_ge(z_done, b * AG + AG)
                        last = isinstance(b, int)
                        pe.wait_ge(mrow_done, b * AG + AG + (0 if last else 1))
                        for t in range(TB):
                            pe.wait_ge(y_done, b * TB + max(t - 1, 0))
                            tok = slice(P * t, P * t + P)
                            for g in range(AG):
                                pe.matmul(YB[t % 2][:, 0:DM], zt[:, g, tok], wo_hi[:, g, :],
                                          start=(g == 0), stop=False)
                                m = pe.matmul(YB[t % 2][:, 0:DM], zt[:, g, tok], wo_lo[:, g, :],
                                              start=False, stop=(g == AG - 1))
                            m.then_inc(y_full, 1)

                steps(pe, do)

        nc.clear_and_free_semaphores(signals)
        nc.all_engine_barrier()


def local_attention(nc, K, lay, x, wqkv, q_scale, k_scale, wo_w, rot, dst):
    with ExitStack() as ctx:
        sb = lambda name, shape, dt=F32: ctx.enter_context(nc.sbuf_tensor(f"l{lay}_" + name, shape, dt))
        ps = lambda name, shape: ctx.enter_context(nc.psum_tensor(f"l{lay}_" + name, shape, F32))
        sem = lambda name: ctx.enter_context(nc.semaphore(f"l{lay}_" + name))

        w_hi, w_lo = sb("w_hi", [P, KT, 3 * INNER], F32R), sb("w_lo", [P, KT, 3 * INNER], F32R)
        wo = sb("wo", [P, INNER // P, DM])
        scales = sb("scales", [P, 2, FD])
        rots = sb("rots", [P, 2, 2, TB, FD])
        xin = sb("xin", [P, TB, DM])
        xt_hi, xt_lo = sb("xt_hi", [P, KT, S + 1], F32R), sb("xt_lo", [P, KT, S + 1], F32R)
        sq = sb("sq", [P, 2, INNER])
        t1, t2 = sb("t1", [P, 2, 2, INNER]), sb("t2", [P, 2, 2, INNER])
        ss, inv, half = sb("ss", [P, 2, 2 * FH]), sb("inv", [P, 2, 2 * FH]), sb("half", [P, 2 * FH])
        qk = sb("qk", [P, TB, 2, INNER])
        Q1, K1 = sb("Q1", [P, FH, S], F32R), sb("K1", [P, FH, S], F32R)
        Q2, K2 = sb("Q2", [P, FH, S], F32R), sb("K2", [P, FH, S], F32R)
        V = sb("V", [P, TB, INNER])
        ones = sb("ones", [P, FD])
        LOW = 32
        negm = sb("negm", [P, TB, 2, 2, 2])
        mrow = sb("mrow", [2 * LOW, 2, S], F32R)
        PT = sb("PT", [P, 2, TB, 2, 2 * P])
        rsum = sb("rsum", [P, INNER // P, S])
        zt = sb("zt", [P, INNER // P, S])
        xr, out = sb("xr", [P, TB, DM]), sb("out", [P, TB, DM])

        FB = [ps("f0", [P, S]), ps("f1", [P, S])]
        MX = [ps("x0", [P, S]), ps("x1", [P, S])]
        SC = [ps("c0", [P, S]), ps("c1", [P, S])]
        OB, SB = ps("o", [P, S]), ps("s", [P, S])
        YB = [OB, SB]

        w_loaded, w_hi_done, w_lo_done, small = sem("w_loaded"), sem("w_hi_done"), sem("w_lo_done"), sem("small")
        q2_set, k2_set = sem("q2_set"), sem("k2_set")
        rots_in, rots_done = sem("rots_in"), sem("rots_done")
        x_in, front_full, hi_done = sem("x_in"), sem("front_full"), sem("hi_done")
        front_free = sem("front_free")
        sq_done, ss_raw, ss_done, inv_done = sem("sq_done"), sem("ss_raw"), sem("ss_done"), sem("inv_done")
        summed, rotated = sem("summed"), sem("rotated")
        stacked = [sem(f"stacked{p}") for p in range(FH // 2)]
        mx_full, max_done, sc_full, exp_done = sem("mx_full"), sem("max_done"), sem("sc_full"), sem("exp_done")
        mt_full, mhi_done, mrow_done = sem("mt_full"), sem("mhi_done"), sem("mrow_done")
        m_in = [sem("m_in0"), sem("m_in1")]
        o_full, o_out, ln_done, rsum_done, z_done = (
            sem("o_full"), sem("o_out"), sem("ln_done"), sem("rsum_done"), sem("z_done"))
        y_full, y_done = sem("y_full"), sem("y_done")
        xr_in, stored = sem("xr_in"), sem("stored")

        NF, QK_AT, T_AT, V_AT = 22, 2, 10, 18
        PAIRS, UNITS = FH // 2, FH // 2 * TB

        sm, fsm, qk_, qe, te = (lambda *us: [("sm", u) for u in us], lambda *us: [("f_sm", u) for u in us],
                                lambda u: [("f_qk", u)], lambda u: [("f_qe", u)],
                                lambda p: [("f_t", p), ("f_te", p)])
        fv = lambda t: [("f_v", t)]
        BEHIND = [sm(8, 9) + [("f_x", 0), ("f_xe", 0)], sm(10, 11) + qk_(0), sm(12) + qe(0) + qk_(1),
                  sm(13) + qe(1) + qk_(2) + [("pv", 0)], sm(14, 15) + [("z", 0)] + qe(2) + qk_(3) + [("mt", 1)],
                  qe(3) + qk_(4), qe(4) + qk_(5), qe(5) + qk_(6), qe(6) + qk_(7) + [("xr", 0)], qe(7),
                  [("pv", 1)], [("z", 1), ("pv", 2)], [("z", 2)] + te(0), te(1), [], te(2) + fsm(0, 1)]
        STEPS = []
        for k in range(UNITS):
            STEPS += [("st", k)] + BEHIND[k]
        STEPS += te(3) + [("pv", 3), ("z", 3)] + fsm(2, 3) + fv(0) + fsm(4) + [("zl", 0)] + fv(1) + fsm(5) + fv(2) \
            + fsm(6) + fv(3) + fsm(7) + [("zn", 0), ("f_mt", 0), ("out", 0)]

        def steps(eng, do):
            for name, i in STEPS:
                if name[0] == "f":
                    do(name, i, 0)
            with eng.Fori(0, NB - 1) as it:
                for name, i in STEPS:
                    do(name, i, it + 1 if name[0] == "f" else it)
            for name, i in STEPS:
                if name[0] != "f":
                    do(name, i, NB - 1)

        raw = qk[:, 0:3, :, :].rearrange("p t w n -> p (t w n)").rearrange("p (k n) -> p k n", k=KT)

        with nc.Block() as block:
            @block.sync
            def _(sp):
                sp.dma_start(xin[:, :, :], x[0].rearrange("(t p) d -> p t d", p=P)).then_inc(x_in, 16)
                sp.dma_start(raw, wqkv.rearrange("(k p) n -> p k n", p=P)).then_inc(w_loaded, 16)
                sp.dma_start(wo[:, :, :], wo_w.rearrange("(k p) n -> p k n", p=P)).then_inc(w_loaded, 16)
                sp.dma_start(scales[:, 0, :], q_scale.partition_broadcast(P)).then_inc(rots_in, 16)
                sp.dma_start(scales[:, 1, :], k_scale.partition_broadcast(P)).then_inc(rots_in, 16)
                for w in range(2):
                    for c in range(2):
                        sp.dma_start(rots[:, w, c, :, :], rot[w, c].rearrange("(t p) d -> p t d", p=P))\
                            .then_inc(rots_in, 16)

                def do(name, i, b):
                    if name == "f_x":
                        if not isinstance(b, int):
                            sp.wait_ge(front_full, (b - 1) * NF + 2)
                            sp.dma_start(xin[:, :, :], x[b].rearrange("(t p) d -> p t d", p=P)).then_inc(x_in, 16)
                    elif name == "f_te":
                        sp.wait_ge(hi_done, b * 10 + 4 + 2 * i)
                        for hh in range(2):
                            h, own, other = 2 * i + hh, slice(FD * hh, FD * hh + FD), slice(FD - FD * hh, P - FD * hh)
                            sp.dma_start(K1[other, h, :].bitcast(F32), K1[own, h, :].bitcast(F32))\
                                .then_inc(stacked[i], 16)
                            sp.dma_start(Q2[own, h, :].bitcast(F32), Q1[own, h, :].bitcast(F32))\
                                .then_inc(stacked[i], 16)
                    elif name in ("mt", "f_mt"):
                        sp.wait_ge(mrow_done, b * 2 + i + 1)
                        for hh in range(2):
                            for part in range(2):
                                r, q = LOW * part + 2 * hh, FD - FD * hh + LOW * part
                                sp.dma_start(Q2[q:q + 1, 4 * i + hh:4 * i + 4:2, :].bitcast(F32),
                                             mrow[r:r + 2, i, :].bitcast(F32)).then_inc(m_in[i], 16)
                    elif name == "xr":
                        sp.wait_ge(y_done, b * TB)
                        sp.dma_start(xr[:, :, :], x[b].rearrange("(t p) d -> p t d", p=P)).then_inc(xr_in, 16)

                steps(sp, do)

            @block.gpsimd
            def _(pool):
                pool.memset(half[:, :], -0.5).then_inc(small, 1)
                pool.memset(ones[:, :], 1.0).then_inc(small, 1)
                pool.memset(xt_hi[:, 1, 0:1].bitcast(F32), 0.0).then_inc(small, 1)
                pool.memset(xt_lo[:, 1, 0:1].bitcast(F32), 0.0).then_inc(small, 1)
                pool.wait_ge(k2_set, 1)
                pool.wait_ge(small, 4)
                for hh in range(2):
                    for low in (0, LOW):
                        r = FD - FD * hh + low
                        pool.memset(K2[r:r + 1, hh:FH:2, :].bitcast(F32), 1.0).then_inc(small, 1)
                pool.wait_ge(small, 8)

                def do(name, i, b):
                    if name == "f_qe" and i % 2 == 1:
                        blk, par = i // 2, i // 2 % 2
                        n = b * TB + blk
                        pool.wait_ge(ss_done, n + 1)
                        pool.tensor_tensor(inv[:, par, :], ss[:, par, :], half[:, :], ALU.pow).then_inc(inv_done, 1)
                        for w in range(2):
                            pool.wait_ge(front_free, b * NF + QK_AT + 2 * blk + w + 1)
                            pool.tensor_tensor(t1[:, par, w, :], t1[:, par, w, :], t2[:, par, w, :], ALU.add)\
                                .then_inc(summed, 1)
                        for w in range(2):
                            if w == 0:
                                pool.wait_ge(inv_done, n + 1)
                            pool.wait_ge(summed, 2 * n + w + 1)
                            pool.tensor_tensor(qk[:, blk, w, :].rearrange("p (h d) -> p h d", d=FD),
                                               t1[:, par, w, :].rearrange("p (h d) -> p h d", d=FD),
                                               inv[:, par, FH * w:FH * w + FH].unsqueeze(2)
                                               .to_broadcast([P, FH, FD]), ALU.mult).then_inc(rotated, 1)
                    elif name == "out":
                        pool.wait_ge(y_done, b * TB + TB)
                        pool.dma_start(dst[b, 1:1 + S].rearrange("(t p) d -> p t d", p=P),
                                       out[:, :, :]).then_inc(stored, 16)

                steps(pool, do)
                pool.wait_ge(stored, 16 * NB)

            @block.scalar
            def _(act):
                act.wait_ge(w_loaded, 32)
                for kt in range(KT):
                    nc.scalar.activation(w_hi[:, kt, :], raw[:, kt, :], ACT.Copy).then_inc(w_hi_done, 1)

                def do(name, i, b):
                    if name == "f_xe":
                        for h in range(KT):
                            act.wait_ge(front_full, b * NF + h + 1)
                            nc.scalar.activation(xt_hi[:, h, h:S + h], FB[h][:, :], ACT.Identity)\
                                .then_inc(hi_done, 1)
                    elif name == "f_qe":
                        w = i % 2
                        act.wait_ge(front_full, b * NF + QK_AT + i + 1)
                        if not (isinstance(b, int) and i < 2):
                            act.wait_ge(ss_raw, b * 8 + i - 1)
                        nc.scalar.activation(sq[:, w, :], FB[w][:, :], ACT.Square).then_inc(sq_done, 1)
                    elif name == "f_te":
                        for w, dst_t in enumerate((Q1, K1)):
                            act.wait_ge(front_full, b * NF + T_AT + 2 * i + w + 1)
                            for hh in range(2):
                                own = slice(FD * hh, FD * hh + FD)
                                m = nc.scalar.activation(dst_t[own, 2 * i + hh, :], FB[w][own, :], ACT.Identity)
                            m.then_inc(hi_done, 1)
                    elif name in ("mt", "f_mt"):
                        act.wait_ge(mt_full, b * 2 + i + 1)
                        act.wait_ge(m_in[i], b * 64)
                        nc.scalar.activation(mrow[0:4, i, :], SB[0:4, :], ACT.Identity).then_inc(mhi_done, 1)
                    elif name == "st":
                        p, j = i // TB, i % TB
                        act.wait_ge(sc_full, b * UNITS + i + 1)
                        nq = P if j == TB - 1 else 2 * P
                        src = SC[i % 2][:, :].rearrange("p (h q) -> p h q", h=2)
                        nc.scalar.activation(PT[:, p % 2, j, :, 0:nq], src[:, :, 2 * P - nq:2 * P], ACT.Exp,
                                             scale=8.0).then_inc(exp_done, 1)
                    elif name == "z":
                        act.wait_ge(o_full, b * PAIRS + i + 1)
                        act.wait_ge(z_done, b * PAIRS)
                        nc.scalar.activation(rsum[:, i, :], SB[:, :], ACT.Identity)
                        act.wait_ge(y_full, b * TB)
                        nc.scalar.activation(zt[:, i, :], OB[:, :], ACT.Identity).then_inc(o_out, 1)
                    elif name == "zl":
                        act.wait_ge(o_out, b * PAIRS + PAIRS)
                        nc.scalar.activation(rsum[:, :, :], rsum[:, :, :], ACT.Ln).then_inc(ln_done, 1)
                        act.wait_ge(ln_done, b + 1)
                        for p in range(PAIRS):
                            nc.scalar.activation(rsum[:, p, :], rsum[:, p, :], ACT.Exp, scale=-1.0)\
                                .then_inc(rsum_done, 1)

                steps(act, do)

            @block.vector
            def _(dve):
                dve.memset(K2[:, :, :].bitcast(F32), 0.0).then_inc(k2_set, 1)
                dve.memset(Q2[:, :, :].bitcast(F32), 0.0).then_inc(q2_set, 1)
                for kt in range(KT):
                    dve.wait_ge(w_hi_done, kt + 1)
                    dve.tensor_tensor(w_lo[:, kt, :], raw[:, kt, :], w_hi[:, kt, :], ALU.subtract)\
                        .then_inc(w_lo_done, 1)
                dve.wait_ge(rots_in, 96)
                H2 = FD // 2
                for w in range(2):
                    sc = scales[:, w:w + 1, :].to_broadcast([P, TB, FD])
                    dve.tensor_tensor(rots[:, w, 0, :, :], rots[:, w, 0, :, :], sc, ALU.mult)\
                        .then_inc(rots_done, 1)
                    dve.scalar_tensor_tensor(out=rots[:, w, 1, :, 0:H2], in0=rots[:, w, 1, :, 0:H2], scalar=-1.0,
                                             in1=sc[:, :, H2:FD], op0=ALU.mult, op1=ALU.mult)\
                        .then_inc(rots_done, 1)
                    dve.tensor_tensor(rots[:, w, 1, :, H2:FD], rots[:, w, 1, :, H2:FD], sc[:, :, 0:H2],
                                      ALU.mult).then_inc(rots_done, 1)
                dve.wait_ge(rots_done, 6)

                def do(name, i, b):
                    if name == "f_xe":
                        for h in range(KT):
                            dve.wait_ge(hi_done, b * 10 + h + 1)
                            dve.tensor_tensor(xt_lo[:, h, h:S + h], FB[h][:, :], xt_hi[:, h, h:S + h],
                                              ALU.subtract).then_inc(front_free, 1)
                    elif name == "f_qe":
                        blk, w, par = i // 2, i % 2, i // 2 % 2
                        if not (isinstance(b, int) and blk < 2):
                            dve.wait_ge(rotated, b * 8 + 2 * blk - 2)
                        f = FB[w][:, :].rearrange("p (h d) -> p h d", d=FD)
                        a = t1[:, par, w, :].rearrange("p (h d) -> p h d", d=FD)
                        c = t2[:, par, w, :].rearrange("p (h d) -> p h d", d=FD)
                        cs = lambda k, lo, hi: rots[:, w, k, blk, lo:hi].unsqueeze(1)\
                            .to_broadcast([P, FH, hi - lo])
                        dve.wait_ge(sq_done, b * 8 + i + 1)
                        dve.tensor_reduce(ss[:, par, FH * w:FH * w + FH],
                                          sq[:, w, :].rearrange("p (h d) -> p h d", d=FD), AX.X, ALU.add)\
                            .then_inc(ss_raw, 1)
                        if w == 1:
                            dve.wait_ge(ss_raw, b * 8 + i + 1)
                            dve.tensor_scalar(ss[:, par, :], ss[:, par, :], 1e-24, None, ALU.max)\
                                .then_inc(ss_done, 1)
                        dve.tensor_tensor(a, f, cs(0, 0, FD), ALU.mult)
                        dve.tensor_tensor(c[:, :, 0:H2], f[:, :, H2:FD], cs(1, 0, H2), ALU.mult)
                        dve.tensor_tensor(c[:, :, H2:FD], f[:, :, 0:H2], cs(1, H2, FD), ALU.mult)\
                            .then_inc(front_free, 1)
                    elif name == "f_te":
                        for w in range(2):
                            dve.wait_ge(hi_done, b * 10 + 3 + 2 * i + w)
                            for hh in range(2):
                                h, own = 2 * i + hh, slice(FD * hh, FD * hh + FD)
                                other = slice(FD - FD * hh, P - FD * hh)
                                if w == 0:
                                    m = dve.tensor_tensor(Q1[other, h, :], FB[0][own, :], Q1[own, h, :],
                                                          ALU.subtract)
                                else:
                                    m = dve.tensor_tensor(K2[own, h, :], FB[1][own, :], K1[own, h, :],
                                                          ALU.subtract)
                            m.then_inc(front_free, 1)
                    elif name == "f_v":
                        dve.wait_ge(front_full, b * NF + V_AT + i + 1)
                        dve.tensor_copy(V[:, i, :], FB[i % 2][:, :]).then_inc(front_free, 1)
                    elif name in ("sm", "f_sm"):
                        p, q = i // TB, i % TB
                        dve.wait_ge(mx_full, b * UNITS + i + 1)
                        dve.tensor_reduce(negm[:, q, p // 2, :, p % 2],
                                          MX[i % 2][:, :].rearrange("p (h k) -> p h k", h=2), AX.X,
                                          ALU.max, negate=True).then_inc(max_done, 1)
                    elif name in ("mt", "f_mt"):
                        dve.wait_ge(mhi_done, b * 2 + i + 1)
                        dve.tensor_tensor(mrow[LOW:LOW + 4, i, :], SB[0:4, :], mrow[0:4, i, :], ALU.subtract)\
                            .then_inc(mrow_done, 1)
                    elif name == "zn":
                        for p in range(PAIRS):
                            dve.wait_ge(rsum_done, b * PAIRS + p + 1)
                            dve.tensor_tensor(zt[:, p, :], zt[:, p, :], rsum[:, p, :], ALU.mult)\
                                .then_inc(z_done, 1)
                    elif name == "out":
                        dve.wait_ge(xr_in, b * 16 + 16)
                        dve.wait_ge(stored, b * 16)
                        for t in range(TB):
                            dve.wait_ge(y_full, b * TB + t + 1)
                            dve.tensor_tensor(out[:, t, :], YB[t % 2][:, 0:DM], xr[:, t, :], ALU.add)\
                                .then_inc(y_done, 1)

                steps(dve, do)

            @block.tensor
            def _(pe):
                def split_mm(o, a_hi, a_lo, r_hi, r_lo, first, last):
                    pe.matmul(o, a_hi, r_hi, start=first, stop=False)
                    pe.matmul(o, a_lo, r_hi, start=False, stop=False)
                    return pe.matmul(o, a_hi, r_lo, start=False, stop=last)

                def front_wait(b, n):
                    if not (isinstance(b, int) and n < 2):
                        pe.wait_ge(front_free, b * NF + n - 1)

                def pass_wait(done, b, i):
                    if isinstance(b, int) and b == 0 and i < 2:
                        return
                    pe.wait_ge(done, b * UNITS + max(i - 1, 0))

                def do(name, i, b):
                    if name == "f_x":
                        pe.wait_ge(x_in, b * 16 + 16)
                        for h in range(KT):
                            front_wait(b, h)
                            for t in range(TB):
                                m = pe.transpose(FB[h][:, P * t:P * t + P], xin[:, t, P * h:P * h + P],
                                                 K["ident"][:, :])
                            m.then_inc(front_full, 1)
                    elif name == "f_qk":
                        w, tok = i % 2, slice(P * (i // 2), P * (i // 2) + P)
                        pe.wait_ge(w_lo_done, 2)
                        pe.wait_ge(small, 4)
                        if i == 0:
                            pe.wait_ge(front_free, b * NF + 2)
                        else:
                            front_wait(b, QK_AT + i)
                        col = slice(INNER * w, INNER * w + INNER)
                        for h in range(KT):
                            m = split_mm(FB[w][:, :], xt_hi[:, h, tok], xt_lo[:, h, tok], w_hi[:, h, col],
                                         w_lo[:, h, col], h == 0, h == KT - 1)
                        m.then_inc(front_full, 1)
                    elif name == "f_t":
                        pe.wait_ge(rotated, b * 8 + 8)
                        for w in range(2):
                            front_wait(b, T_AT + 2 * i + w)
                            for t in range(TB):
                                m = pe.transpose(FB[w][:, P * t:P * t + P], qk[:, t, w, P * i:P * i + P],
                                                 K["ident"][:, :])
                            m.then_inc(front_full, 1)
                    elif name == "f_v":
                        front_wait(b, V_AT + i)
                        tok = slice(P * i, P * i + P)
                        for h in range(KT):
                            m = split_mm(FB[i % 2][:, :], xt_hi[:, h, tok], xt_lo[:, h, tok],
                                         w_hi[:, h, 2 * INNER:], w_lo[:, h, 2 * INNER:], h == 0, h == KT - 1)
                        m.then_inc(front_full, 1)
                    elif name in ("sm", "f_sm"):
                        p, q = i // TB, i % TB
                        if q == 0:
                            pe.wait_ge(small, 8)
                            pe.wait_ge(q2_set, 1)
                            pe.wait_ge(stacked[p], b * 64 + 64)
                            pe.wait_ge(front_free, b * NF + T_AT + 2 * p + 2)
                        pass_wait(max_done, b, i)
                        k0 = P * max(q - 1, 0)
                        r = MX[i % 2][:, :].rearrange("p (h k) -> p h k", h=2)
                        for hh in range(2):
                            h = 2 * p + hh
                            pe.matmul(r[:, hh, :], Q1[:, h, P * q:P * q + P], K1[:, h, k0:k0 + 2 * P],
                                      start=(hh == 0), stop=True, skip_group_check=True)
                        mask = K["window"] if q else K["window0"]
                        pe.matmul(r, K["identb"][:, :],
                                  mask[:, :, :].rearrange("p b k -> p (b k)").unsqueeze(1)
                                  .to_broadcast([P, 2, 2 * P]), start=False, stop=True,
                                  skip_group_check=True).then_inc(mx_full, 1)
                    elif name in ("mt", "f_mt"):
                        pe.wait_ge(max_done, b * UNITS + 8 * i + 8)
                        pe.wait_ge(o_out, b * PAIRS + i)
                        if name == "f_mt" and not isinstance(b, int):
                            pe.wait_ge(y_done, (b - 1) * TB)
                        for q in range(TB):
                            m = pe.transpose(SB[0:4, P * q:P * q + P],
                                             negm[:, q, i].rearrange("p a b -> p (a b)"), K["ident"][:, :])
                        m.then_inc(mt_full, 1)
                    elif name == "st":
                        p, j = i // TB, i % TB
                        if i % 8 == 0:
                            pe.wait_ge(m_in[i // 8], b * 64 + 64)
                        pass_wait(exp_done, b, i)
                        q0 = P * min(j, TB - 2)
                        key, qry = slice(P * j, P * j + P), slice(q0, q0 + 2 * P)
                        o = SC[i % 2][:, :].rearrange("p (h q) -> p h q", h=2)
                        for hh in range(2):
                            h = 2 * p + hh
                            pe.matmul(o[:, hh, :], K1[:, h, key], Q1[:, h, qry], start=(hh == 0), stop=False,
                                      skip_group_check=True)
                            pe.matmul(o[:, hh, :], K2[:, h, key], Q2[:, h, qry], start=False, stop=True,
                                      skip_group_check=True)
                        if j < TB - 1:
                            mask = K["window_t"][:, :, :].rearrange("p b q -> p (b q)")
                        else:
                            o, mask = o[:, :, P:2 * P], K["window_t"][:, 0, :]
                        pe.matmul(o, K["identb"][:, :], mask.unsqueeze(1).to_broadcast([P, 2, mask.shape[1]]),
                                  start=False, stop=True, skip_group_check=True).then_inc(sc_full, 1)
                    elif name == "pv":
                        pe.wait_ge(exp_done, b * UNITS + TB * i + TB)
                        pe.wait_ge(o_out, b * PAIRS + i)
                        pe.wait_ge(mrow_done, b * 2 + (1 if i == 0 else 2))
                        pe.wait_ge(y_done, b * TB)
                        pe.wait_ge(front_free, b * NF + NF)
                        for j in range(TB):
                            nq = P if j == TB - 1 else 2 * P
                            for hh in range(2):
                                h, rows = 2 * i + hh, slice(FD * hh, FD * hh + FD)
                                pe.matmul(OB[rows, P * j:P * j + nq], V[:, j, FD * h:FD * h + FD],
                                          PT[:, i % 2, j, hh, 0:nq], start=(j == 0), stop=(j == TB - 1),
                                          skip_group_check=True)
                            for hh in range(2):
                                rows = slice(FD * hh, FD * hh + FD)
                                m = pe.matmul(SB[rows, P * j:P * j + nq], ones[:, :], PT[:, i % 2, j, hh, 0:nq],
                                              start=(j == 0), stop=(j == TB - 1), skip_group_check=True)
                        m.then_inc(o_full, 1)
                    elif name == "out":
                        pe.wait_ge(z_done, b * PAIRS + PAIRS)
                        pe.wait_ge(mrow_done, b * 2 + (2 if isinstance(b, int) else 3))
                        for t in range(TB):
                            pe.wait_ge(y_done, b * TB + max(t - 1, 0))
                            for p in range(INNER // P):
                                m = pe.matmul(YB[t % 2][:, 0:DM], zt[:, p, P * t:P * t + P], wo[:, p, :],
                                              start=(p == 0), stop=(p == INNER // P - 1))
                            m.then_inc(y_full, 1)

                steps(pe, do)


def feed_forward(nc, K, lay, x, ln_g, ln_b, w1_w, b1_w, w2_w, b2_w, residual, dst):
    with ExitStack() as ctx:
        sb = lambda name, shape, dt=F32: ctx.enter_context(nc.sbuf_tensor(f"m{lay}_" + name, shape, dt))
        ps = lambda name, shape: ctx.enter_context(nc.psum_tensor(f"m{lay}_" + name, shape, F32))
        sem = lambda name: ctx.enter_context(nc.semaphore(f"m{lay}_" + name))
        last = residual is not None
        loads = 3 + 3 * NT

        w_raw = sb("w_raw", [P, KT, 2 * HID])
        w_hi, w_lo = sb("w_hi", [P, KT, 2 * HID], F32R), sb("w_lo", [P, KT, 2 * HID], F32R)
        w2 = sb("w2", [HT, NT, DM])
        b1 = sb("b1", [HT, 2, NT])
        gam, bet = sb("gam", [P, KT]), sb("bet", [P, KT])
        b2 = sb("b2", [P, DM])
        h = sb("h", [P, TB, DM])
        hn = sb("hn", [P, TB, DM])
        st, mv = sb("st", [P, TB, 6]), sb("mv", [P, TB, 2])
        ve, rs, half = sb("ve", [P, TB]), sb("rs", [P, TB]), sb("half", [P, TB])
        ht = sb("ht", [P, KT, S])
        ht_hi, ht_lo = sb("ht_hi", [P, KT, S], F32R), sb("ht_lo", [P, KT, S], F32R)
        gate = sb("gate", [HT, 2, S])
        hid = sb("hid", [HT, NT, S])
        xr = sb("xr", [P, TB, DM])
        res = sb("res", [P, TB, DM])
        y, out = sb("y", [P, TB, DM]), sb("out", [P, TB, DM])
        st2, mv2 = sb("st2", [P, TB, 6]), sb("mv2", [P, TB, 2])
        ve2, rs2 = sb("ve2", [P, TB]), sb("rs2", [P, TB])

        FB = [ps("f0", [P, S]), ps("f1", [P, S])]
        AB = [[ps(f"a{i}", [P, S]), ps(f"g{i}", [P, S])] for i in range(2)]
        WB = [ps("w0", [P, S]), ps("w1", [P, S])]

        w_loaded, loaded, w_hi_done, w_lo_done = sem("w_loaded"), sem("loaded"), sem("w_hi_done"), sem("w_lo_done")
        h_in, stats, var_done, rstd_done = sem("h_in"), sem("stats"), sem("var_done"), sem("rstd_done")
        normed, turned, scaled, hi_done, lo_done = (
            sem("normed"), sem("turned"), sem("scaled"), sem("hi_done"), sem("lo_done"))
        ag_full, gate_done, hid_done = sem("ag_full"), sem("gate_done"), sem("hid_done")
        w2_full, y_done, xr_in, res_in, xb_done, stored = (
            sem("w2_full"), sem("y_done"), sem("xr_in"), sem("res_in"), sem("xb_done"), sem("stored"))
        if last:
            stats2, var2_done, rstd2_done, out_done = (
                sem("stats2"), sem("var2_done"), sem("rstd2_done"), sem("out_done"))

        STEPS = [("xr", 0)] + [("w1", n) for n in range(3)] + [("f_n", 0)] + [("w1", n) for n in range(3, NT)] \
            + [("f_t", 0), ("w2", 0)]

        def steps(eng, do):
            for name, i in STEPS:
                if name[0] == "f":
                    do(name, i, 0)
            with eng.Fori(0, NB - 1) as it:
                for name, i in STEPS:
                    do(name, i, it + 1 if name[0] == "f" else it)
            for name, i in STEPS:
                if name[0] != "f":
                    do(name, i, NB - 1)

        with nc.Block() as block:
            @block.sync
            def _(sp):
                sp.dma_start(w_raw[:, :, :], w1_w.rearrange("(k p) n -> p k n", p=P)).then_inc(w_loaded, 16)
                sp.dma_start(gam[:, :], ln_g.rearrange("(k p) -> p k", p=P),
                             allow_slow_non_contiguous=True).then_inc(loaded, 16)
                sp.dma_start(bet[:, :], ln_b.rearrange("(k p) -> p k", p=P),
                             allow_slow_non_contiguous=True).then_inc(loaded, 16)
                for n in range(NT):
                    rows = tile_rows(n)
                    for k in range(2):
                        sp.dma_start(b1[0:rows, k, n:n + 1],
                                     b1_w[HID * k + HT * n:HID * k + HT * n + rows].unsqueeze(1),
                                     allow_slow_non_contiguous=True).then_inc(loaded, 16)
                    sp.dma_start(w2[0:rows, n, :], w2_w[HT * n:HT * n + rows]).then_inc(loaded, 16)
                sp.dma_start(b2[:, :], b2_w.partition_broadcast(P)).then_inc(loaded, 16)

                def do(name, i, b):
                    if name == "f_n":
                        if not isinstance(b, int):
                            sp.wait_ge(normed, b * TB)
                        sp.dma_start(h[:, :, 0:P], x[b, 1:1 + S, 0:P].rearrange("(t p) d -> p t d", p=P))\
                            .then_inc(h_in, 16)
                        sp.dma_start(h[:, :, P:DM], x[b, 0:S, P:DM].rearrange("(t p) d -> p t d", p=P))\
                            .then_inc(h_in, 16)
                    elif name == "xr":
                        sp.wait_ge(y_done, b * TB)
                        sp.dma_start(xr[:, :, :], x[b, 1:1 + S].rearrange("(t p) d -> p t d", p=P))\
                            .then_inc(xr_in, 16)
                        if last:
                            sp.dma_start(res[:, :, :], residual[b, 1:1 + S].rearrange("(t p) d -> p t d", p=P))\
                                .then_inc(res_in, 16)
                    elif name == "w2":
                        sp.wait_ge(out_done if last else y_done, b * TB + TB)
                        sp.dma_start(dst[b].rearrange("(t p) d -> p t d", p=P),
                                     (out if last else y)[:, :, :]).then_inc(stored, 16)

                steps(sp, do)
                sp.wait_ge(stored, 16 * NB)

            @block.gpsimd
            def _(pool):
                pool.memset(half[:, :], -0.5).then_inc(rstd_done, 1)
                pool.wait_ge(rstd_done, 1)
                pool.wait_ge(loaded, 16 * loads)

                def do(name, i, b):
                    if name == "xr":
                        pool.wait_ge(xr_in, b * 16 + 16)
                        pool.tensor_tensor(xr[:, :, :], xr[:, :, :],
                                           b2[:, :].unsqueeze(1).to_broadcast([P, TB, DM]), ALU.add)\
                            .then_inc(xb_done, 1)
                        if last:
                            pool.wait_ge(res_in, b * 16 + 16)
                            pool.wait_ge(xb_done, b * 2 + 1)
                            pool.tensor_tensor(xr[:, :, :], xr[:, :, :], res[:, :, :], ALU.add)\
                                .then_inc(xb_done, 1)
                    elif name == "f_n":
                        wait_apart(pool, K, var_done, b + 1)
                        pool.tensor_scalar(ve[:, :], mv[:, :, 1], LN_EPS, None, ALU.add).then_inc(rstd_done, 1)
                        pool.wait_ge(rstd_done, 2 * b + 2)
                        pool.tensor_tensor(rs[:, :], ve[:, :], half[:, :], ALU.pow).then_inc(rstd_done, 1)
                    elif name == "f_t":
                        for k in range(KT):
                            pool.wait_ge(hi_done, b * KT + k + 1)
                            pool.tensor_tensor(ht_lo[:, k, :], ht[:, k, :], ht_hi[:, k, :], ALU.subtract)\
                                .then_inc(lo_done, 1)
                    elif name == "w2" and last:
                        wait_apart(pool, K, var2_done, b + 1)
                        pool.tensor_scalar(ve2[:, :], mv2[:, :, 1], LN_EPS, None, ALU.add).then_inc(rstd2_done, 1)
                        pool.wait_ge(rstd2_done, 2 * b + 1)
                        pool.tensor_tensor(rs2[:, :], ve2[:, :], half[:, :], ALU.pow).then_inc(rstd2_done, 1)

                steps(pool, do)

            @block.scalar
            def _(act):
                act.wait_ge(w_loaded, 16)
                for k in range(KT):
                    nc.scalar.activation(w_hi[:, k, :], w_raw[:, k, :], ACT.Copy).then_inc(w_hi_done, 1)
                act.wait_ge(loaded, 16 * loads)

                def do(name, i, b):
                    if name == "f_t":
                        for k in range(KT):
                            act.wait_ge(turned, b * KT + k + 1)
                            nc.scalar.activation(ht[:, k, :], FB[k][:, :], ACT.Identity, bias=bet[:, k:k + 1],
                                                 scale=gam[:, k:k + 1]).then_inc(scaled, 1)
                    elif name == "w1":
                        n, rows = b * NT + i, tile_rows(i)
                        act.wait_ge(ag_full, n + 1)
                        act.wait_ge(hid_done, b * NT + max(i - 1, 0))
                        nc.scalar.activation(gate[0:rows, i % 2, :], AB[i % 2][1][0:rows, :], ACT.Gelu,
                                             bias=b1[0:rows, 1, i:i + 1]).then_inc(gate_done, 1)

                steps(act, do)

            @block.vector
            def _(dve):
                for k in range(KT):
                    dve.wait_ge(w_hi_done, k + 1)
                    dve.tensor_tensor(w_lo[:, k, :], w_raw[:, k, :], w_hi[:, k, :], ALU.subtract)\
                        .then_inc(w_lo_done, 1)
                dve.wait_ge(loaded, 16 * loads)

                def do(name, i, b):
                    if name == "f_n":
                        dve.wait_ge(h_in, b * 32 + 32)
                        for t in range(TB):
                            dve.bn_stats(st[:, t, :], h[:, t, :]).then_inc(stats, 1)
                        for t in range(TB):
                            wait_apart(dve, K, stats, b * TB + t + 1)
                            m = dve.bn_aggr(mv[:, t, :], st[:, t, :])
                        m.then_inc(var_done, 1)
                        dve.wait_ge(rstd_done, 2 * b + 3)
                        if not isinstance(b, int):
                            dve.wait_ge(turned, b * KT)
                        for t in range(TB):
                            dve.tensor_scalar(hn[:, t, :], h[:, t, :], mv[:, t, 0:1], rs[:, t:t + 1],
                                              ALU.subtract, ALU.mult).then_inc(normed, 1)
                    elif name == "f_t":
                        for k in range(KT):
                            dve.wait_ge(scaled, b * KT + k + 1)
                            dve.wait_ge(turned, b * KT + k + 1)
                            dve.tensor_copy(ht_hi[:, k, :], ht[:, k, :]).then_inc(hi_done, 1)
                    elif name == "w1":
                        n, rows = b * NT + i, tile_rows(i)
                        dve.wait_ge(gate_done, n + 1)
                        dve.scalar_tensor_tensor(out=hid[0:rows, i, :], in0=AB[i % 2][0][0:rows, :],
                                                 scalar=b1[0:rows, 0, i:i + 1], in1=gate[0:rows, i % 2, :],
                                                 op0=ALU.add, op1=ALU.mult).then_inc(hid_done, 1)
                    elif name == "w2":
                        dve.wait_ge(xb_done, (b + 1) * (2 if last else 1))
                        if not last:
                            dve.wait_ge(stored, b * 16)
                        else:
                            dve.wait_ge(out_done, b * TB)
                        for t in range(TB):
                            dve.wait_ge(w2_full, b * TB + t + 1)
                            dve.tensor_tensor(y[:, t, :], WB[t % 2][:, 0:DM], xr[:, t, :], ALU.add)\
                                .then_inc(y_done, 1)
                        if last:
                            for t in range(TB):
                                dve.wait_ge(y_done, b * TB + t + 1)
                                dve.bn_stats(st2[:, t, :], y[:, t, :]).then_inc(stats2, 1)
                            for t in range(TB):
                                wait_apart(dve, K, stats2, b * TB + t + 1)
                                m = dve.bn_aggr(mv2[:, t, :], st2[:, t, :])
                            m.then_inc(var2_done, 1)
                            dve.wait_ge(rstd2_done, 2 * b + 2)
                            dve.wait_ge(stored, b * 16)
                            for t in range(TB):
                                dve.tensor_scalar(out[:, t, :], y[:, t, :], mv2[:, t, 0:1], rs2[:, t:t + 1],
                                                  ALU.subtract, ALU.mult).then_inc(out_done, 1)

                steps(dve, do)

            @block.tensor
            def _(pe):
                def split_mm(o, a_hi, a_lo, r_hi, r_lo, first, last):
                    pe.matmul(o, a_hi, r_hi, start=first, stop=False)
                    pe.matmul(o, a_lo, r_hi, start=False, stop=False)
                    return pe.matmul(o, a_hi, r_lo, start=False, stop=last)

                pe.wait_ge(w_lo_done, 2)
                pe.wait_ge(loaded, 16 * loads)

                def do(name, i, b):
                    if name == "f_t":
                        pe.wait_ge(normed, b * TB + TB)
                        for k in range(KT):
                            if not isinstance(b, int):
                                pe.wait_ge(scaled, b * KT + k - 1)
                            for t in range(TB):
                                m = pe.transpose(FB[k][:, P * t:P * t + P], hn[:, t, P * k:P * k + P],
                                                 K["ident"][:, :])
                            m.then_inc(turned, 1)
                    elif name == "w1":
                        rows = tile_rows(i)
                        if i == 0:
                            pe.wait_ge(lo_done, b * KT + KT)
                        pe.wait_ge(hid_done, b * NT + max(i - 1, 0))
                        for k in range(2):
                            col = slice(HID * k + HT * i, HID * k + HT * i + rows)
                            for f in range(KT):
                                m = split_mm(AB[i % 2][k][0:rows, :], w_hi[:, f, col], w_lo[:, f, col],
                                             ht_hi[:, f, :], ht_lo[:, f, :], f == 0, f == KT - 1)
                        m.then_inc(ag_full, 1)
                    elif name == "w2":
                        pe.wait_ge(hid_done, b * NT + NT)
                        for t in range(TB):
                            pe.wait_ge(y_done, b * TB + max(t - 1, 0))
                            for n in range(NT):
                                rows = tile_rows(n)
                                m = pe.matmul(WB[t % 2][:, 0:DM], hid[0:rows, n, P * t:P * t + P],
                                              w2[0:rows, n, :], start=(n == 0), stop=(n == NT - 1))
                            m.then_inc(w2_full, 1)

                steps(pe, do)


def rotary():
    half = np.arange(0, FD, 2, dtype=np.float32)
    inv_freq = (np.float32(1.0) / np.float32(10000.0) ** (half / np.float32(FD))).astype(np.float32)
    t = np.arange(S, dtype=np.float32)
    freqs = t[:, None] * inv_freq[None, :]
    freqs = np.concatenate([freqs, freqs], -1)
    base = (half + np.float32(0.4 * FD)) / np.float32(1.4 * FD)
    power = (t - np.float32(S // 2)) / np.float32(P // 2)
    scale = base[None, :].astype(np.float64) ** power[:, None].astype(np.float64)
    scale = np.concatenate([scale, scale], -1)
    cos, sin = np.cos(freqs.astype(np.float64)), np.sin(freqs.astype(np.float64))
    return np.stack([np.stack([cos * scale, sin * scale]), np.stack([cos / scale, sin / scale])]).astype(np.float32)


NAMES = ["L0_attn_x", "L0_attn_w_qkv", "L0_attn_b_qkv", "L0_attn_w_out", "L0_attn_b_out", "L0_ffn_wqkv",
         "L0_ffn_q_scale", "L0_ffn_k_scale", "L0_ffn_wo", "L0_ffn_ln_g", "L0_ffn_ln_b", "L0_ffn_w1", "L0_ffn_b1",
         "L0_ffn_w2", "L0_ffn_b2", "rot"]


def program(nc, t, out):
    dram = lambda name, shape: nc.dram_tensor(name, shape, F32, kind="Internal").ap()
    scr = dram("qk_parts", [NB, 2, 4 * P, S])
    after_first = dram("after_first", [NB, S + 1, DM])
    after_attn = [dram(f"after_attn{i}", [NB, S + 1, DM]) for i in range(DEPTH)]
    after_layer = dram("after_layer", [NB, S + 1, DM])
    with ExitStack() as ctx:
        K = constants(nc, ctx)
        zero = ctx.enter_context(nc.sbuf_tensor("zero_row", [NB, DM], F32))
        zero_set = ctx.enter_context(nc.semaphore("zero_set"))
        zero_out = ctx.enter_context(nc.semaphore("zero_out"))
        with nc.Block() as block:
            @block.vector
            def _(dve):
                dve.memset(zero[:, :], 0.0).then_inc(zero_set, 1)

            @block.sync
            def _(sp):
                sp.wait_ge(zero_set, 1)
                for a in after_attn:
                    sp.dma_start(a[:, 0, :], zero[:, :]).then_inc(zero_out, 16)
                sp.wait_ge(zero_out, 16 * DEPTH)

        first_attention(nc, K, scr, t["L0_attn_x"], t["L0_attn_w_qkv"], t["L0_attn_b_qkv"], t["L0_attn_w_out"],
                        t["L0_attn_b_out"], after_first)
        x = after_first
        for i in range(DEPTH):
            local_attention(nc, K, i, x[:, 1:], t["L0_ffn_wqkv"][i], t["L0_ffn_q_scale"][i],
                            t["L0_ffn_k_scale"][i], t["L0_ffn_wo"][i], t["rot"], after_attn[i])
            last = i == DEPTH - 1
            feed_forward(nc, K, i, after_attn[i], t["L0_ffn_ln_g"][i], t["L0_ffn_ln_b"][i], t["L0_ffn_w1"][i],
                         t["L0_ffn_b1"][i], t["L0_ffn_w2"][i], t["L0_ffn_b2"][i], after_first if last else None,
                         out if last else after_layer[:, 1:])
            x = after_layer


def kernel(**inputs):
    import concourse.bacc as bacc
    from concourse.bass_utils import run_bass_kernel_spmd

    nc = bacc.Bacc("TRN2", target_bir_lowering=False, num_devices=1)
    arrays = {f"in_{n}": np.ascontiguousarray(rotary() if n == "rot" else inputs[n]) for n in NAMES}
    t = {n: nc.dram_tensor(f"in_{n}", arrays[f"in_{n}"].shape, F32, kind="ExternalInput").ap() for n in NAMES}
    out = nc.dram_tensor("out", [NB, S, DM], F32, kind="ExternalOutput").ap()
    program(nc, t, out)
    return run_bass_kernel_spmd(nc, [arrays], core_ids=[0]).results[0]["out"]
```

```python
from contextlib import ExitStack

import numpy as np

import concourse.bass as bass
from concourse import mybir

F32 = mybir.dt.float32
F32R = mybir.dt.float32r
BF16 = mybir.dt.bfloat16
ALU = mybir.AluOpType
ACT = mybir.ActivationFunctionType
AX = mybir.AxisListType

P = 128
NEG = -1.0e30
MADE = 15
LN_EPS = 1e-5

NB, S, DM = 8, 512, 256
TB = S // P
KT = DM // P
AH, AD = 16, 16
HP = 4
AG = AH // HP
FH, FD = 8, 64
INNER = FH * FD
HID = 682
NT = 6
HT = 114
DEPTH = 2


def tile_rows(n):
    return min(HT, HID - n * HT)


class Uses:

    def __init__(self, consumers, depth):
        self.c, self.depth = consumers, depth

    def filled(self, b, n):
        return b * len(self.c) + n + 1

    def emptied(self, b, n):
        eng = self.c[n]
        return eng, b * self.c.count(eng) + self.c[:n + 1].count(eng)

    def before(self, b, n):
        if n >= self.depth:
            return [self.emptied(b, n - self.depth)]
        if isinstance(b, int) and b == 0:
            return []
        return [(e, b * self.c.count(e)) for e in sorted(set(self.c))]


def wait_apart(eng, K, sem, value):
    if not isinstance(value, int):
        value = eng.snap(eng.to_reg(value))
        eng.wait_ge(K["made"], MADE)
    eng.wait_ge(sem, value)


def constants(nc, ctx):
    sb = lambda name, shape, dt: ctx.enter_context(nc.sbuf_tensor(name, shape, dt))
    k = {
        "ident": sb("ident", [P, P], F32),
        "identb": sb("identb", [P, P], BF16),
        "causal": sb("causal", [P, P], BF16),
        "window": sb("window", [P, 2, P], BF16),
        "window0": sb("window0", [P, 2, P], BF16),
        "window_t": sb("window_t", [P, 2, P], BF16),
    }
    made = k["made"] = ctx.enter_context(nc.semaphore("const_made"))
    with nc.Block() as block:
        @block.gpsimd
        def _(pool):
            pool.memset(k["ident"][:, :], 0.0).then_inc(made, 1)
            pool.memset(k["identb"][:, :], 0.0).then_inc(made, 1)
            pool.memset(k["causal"][:, :], 0.0).then_inc(made, 1)
            pool.memset(k["window"][:, :, :], 0.0).then_inc(made, 1)
            pool.memset(k["window0"][:, 0, :], 0.0).then_inc(made, 1)
            pool.memset(k["window0"][:, 1, :], NEG).then_inc(made, 1)
            pool.memset(k["window_t"][:, :, :], 0.0).then_inc(made, 1)
            pool.wait_ge(made, 7)
            for m in (k["ident"], k["identb"]):
                pool.affine_select(out=m[:, :], in_=m[:, :], compare_op=ALU.not_equal, fill=1.0, base=0,
                                   pattern=[[-1, P]], channel_multiplier=1).then_inc(made, 1)
            for m in (k["causal"][:, :], k["window"][:, 1, :], k["window0"][:, 0, :]):
                pool.affine_select(out=m, in_=m, compare_op=ALU.is_ge, fill=NEG, base=0,
                                   pattern=[[-1, P]], channel_multiplier=1).then_inc(made, 1)
            pool.affine_select(out=k["window"][:, 0, :], in_=k["window"][:, 0, :], compare_op=ALU.is_ge,
                               fill=NEG, base=0, pattern=[[1, P]], channel_multiplier=-1).then_inc(made, 1)
            pool.affine_select(out=k["window_t"][:, 0, :], in_=k["window_t"][:, 0, :], compare_op=ALU.is_ge,
                               fill=NEG, base=0, pattern=[[1, P]], channel_multiplier=-1).then_inc(made, 1)
            pool.affine_select(out=k["window_t"][:, 1, :], in_=k["window_t"][:, 1, :], compare_op=ALU.is_ge,
                               fill=NEG, base=0, pattern=[[-1, P]], channel_multiplier=1).then_inc(made, 1)
            pool.wait_ge(made, MADE)
    return k


def first_attention(nc, K, scr, x, w_qkv, b_qkv, w_out, b_out, dst):
    with ExitStack() as ctx:
        sb = lambda name, shape, dt=F32: ctx.enter_context(nc.sbuf_tensor("a_" + name, shape, dt))
        ps = lambda name, shape: ctx.enter_context(nc.psum_tensor("a_" + name, shape, F32))
        signals = []

        def sem(name):
            signals.append(nc.alloc_semaphore(name="a_" + name))
            return signals[-1]


        w_hi, w_lo = sb("w_hi", [P, KT, 3 * DM], F32R), sb("w_lo", [P, KT, 3 * DM], F32R)
        wo_hi, wo_lo = sb("wo_hi", [P, AG, DM], F32R), sb("wo_lo", [P, AG, DM], F32R)
        bqk = sb("bqk", [P, 4])
        bv, bo = sb("bv", [P, DM]), sb("bo", [P, DM])
        xin = sb("xin", [P, TB, DM])
        xt_hi, xt_lo = sb("xt_hi", [P, KT, S], F32R), sb("xt_lo", [P, KT, S], F32R)
        part_f = sb("part_f", [P, 2, S])
        qk_hi, qk_lo = sb("qk_hi", [P, 4, S], F32R), sb("qk_lo", [P, 4, S], F32R)
        MROW = 96
        Q, Kk = sb("Q", [P, AH, S], F32R), sb("K", [P, AH, S], F32R)
        V = sb("V", [P, TB, AH, 32])
        negm = sb("negm", [P, TB, AH])
        mrow = sb("mrow", [HP, AG, S], F32R)
        QOFF = [0, 512, 896, 1152]
        PT = sb("PT", [P, 2, HP, 1280])
        room = PT[:, 0].rearrange("p h q -> p (h q)")
        w_raw = room[:, 0:KT * 3 * DM].rearrange("p (k n) -> p k n", k=KT)
        wo = room[:, KT * 3 * DM:KT * 3 * DM + AG * DM].rearrange("p (g n) -> p g n", g=AG)
        NC = S // 32
        ot, on = sb("ot", [P, NC, 32]), sb("on", [P, NC, 32], F32R)
        zn, rc = sb("zn", [P, NC, AD]), sb("rc", [P, NC])
        ztf = sb("ztf", [P, S])
        zt = sb("zt", [P, AG, S], F32R)
        xr = sb("xr", [P, TB, DM])
        y, out = sb("y", [P, TB, DM]), sb("out", [P, TB, DM])
        st, mv = sb("st", [P, TB, 6]), sb("mv", [P, TB, 2])
        ve, rs, half = sb("ve", [P, TB]), sb("rs", [P, TB]), sb("half", [P, TB])

        FB = [ps("f0", [P, S]), ps("f1", [P, S])]
        MX = [ps("x0", [P, S]), ps("x1", [P, S])]
        SC = [ps("c0", [P, S]), ps("c1", [P, S])]
        OB, MB = ps("o", [P, S]), ps("m", [P, S])
        YB = [OB, MB]

        w_loaded, w_split, wo_loaded = sem("w_loaded"), sem("w_split"), sem("wo_loaded")
        wo_split, stacks_set = sem("wo_split"), sem("stacks_set")
        x_in, front_full, front_free = sem("x_in"), sem("front_full"), sem("front_free")
        lo_done, v_done, xhi_done = sem("lo_done"), sem("v_done"), sem("xhi_done")
        parts_out = sem("parts_out")
        stacked = [sem(f"stacked{g}") for g in range(AG)]
        mx_full, max_done, sc_full, exp_done = sem("mx_full"), sem("max_done"), sem("sc_full"), sem("exp_done")
        y_full, y_done = sem("y_full"), sem("y_done")
        mt_full, mrow_done = sem("mt_full"), sem("mrow_done")
        m_in = [sem(f"m_in{g}") for g in range(AG)]
        o_full, o_free, z_done = sem("o_full"), sem("o_free"), sem("z_done")
        xr_in, xb_ready = sem("xr_in"), sem("xb_ready")
        v_set = sem("v_set")
        stats, var_done, rstd_a, rstd_done = sem("stats"), sem("var_done"), sem("rstd_a"), sem("rstd_done")
        norm, zn_split, z_turned = sem("norm"), sem("zn_split"), sem("z_turned")
        out_done, stored = sem("out_done"), sem("stored")

        NF = 10
        UNITS = AH * TB
        GU = HP * TB

        STEPS = [s.rsplit(":", 1) for s in """
            sm:41 st:13 sm:42 st:14 f_x:0 f_xe:0 sm:43 st:15 sm:44 st:16 f_qk:0 sm:45 st:17 f_qe:0
            sm:46 st:18 sm:47 st:19 f_qk:1 sm:48 st:20 sm:49 pv:0 f_qe:1 st:21 mt:2 z0:0 sm:50 st:22
            z1:0 sm:51 st:23 sm:52 st:24 sm:53 f_load:0 st:25 sm:54 st:26 z2:0 sm:55 st:27 sm:56 st:28
            z3:0 sm:57 st:29 sm:58 st:30 sm:59 st:31 sm:60 st:32 sm:61 st:33 f_qk:2 f_load:1 sm:62
            st:34 f_qe:2 xr:0 sm:63 st:35 f_sm:0 st:36 pv:1 f_sm:1 st:37 f_sm:2 mt:3 st:38 z0:1 f_sm:3
            st:39 f_sm:4 st:40 z1:1 f_sm:5 st:41 f_sm:6 st:42 f_sm:7 f_qk:3 st:43 f_qe:3 f_sm:8 st:44
            z2:1 f_sm:9 st:45 f_sm:10 st:46 z3:1 f_sm:11 st:47 f_sm:12 st:48 f_sm:13 st:49 f_sm:14
            f_load:2 st:50 f_sm:15 st:51 st:52 pv:2 f_sm:16 f_sm:17 st:53 f_mt:0 f_sm:18 st:54 z0:2
            f_sm:19 st:55 z1:2 f_sm:20 st:56 f_sm:21 st:57 f_sm:22 st:58 f_sm:23 st:59 f_sm:24 st:60
            z2:2 f_sm:25 st:61 f_sm:26 z3:2 f_sm:27 st:62 st:63 f_sm:28 f_st:0 pv:3 f_sm:29 f_st:1
            f_load:3 z0:3 f_sm:30 f_st:2 f_v:0 z1:3 f_sm:31 f_st:3 f_v:1 f_sm:32 f_st:4 f_mt:1 f_sm:33
            f_st:5 z2:3 f_sm:34 f_st:6 f_v:2 z3:3 f_sm:35 f_st:7 f_v:3 f_sm:36 f_st:8 f_sm:37 out:0
            f_st:9 f_sm:38 out:1 f_st:10 f_sm:39 out:2 f_sm:40 out:3 f_st:11 f_st:12 end:0""".split()]
        STEPS = [(name, int(i)) for name, i in STEPS]
        FIRST = [s for s in STEPS if s[0][0] == "f"]

        def steps(eng, do):
            for name, i in FIRST:
                do(name, i, 0)
            with eng.Fori(0, NB - 1) as it:
                for name, i in STEPS:
                    do(name, i, it + 1 if name[0] == "f" else it)
            for name, i in STEPS:
                if name[0] != "f":
                    do(name, i, NB - 1)

        with nc.Block() as block:
            @block.sync
            def _(sp):
                sp.dma_start(xin[:, :, :], x[0].rearrange("(t p) d -> p t d", p=P)).then_inc(x_in, 16)
                sp.dma_start(w_raw[:, :, :], w_qkv.rearrange("(k p) n -> p k n", p=P)).then_inc(w_loaded, 16)
                for m, c in enumerate((0, DM, P, DM + P)):
                    sp.dma_start(bqk[:, m:m + 1], b_qkv[c:c + P].unsqueeze(1),
                                 allow_slow_non_contiguous=True).then_inc(w_loaded, 16)
                sp.dma_start(bv[:, :], b_qkv[2 * DM:].partition_broadcast(P)).then_inc(w_loaded, 16)
                sp.dma_start(bo[:, :], b_out.partition_broadcast(P)).then_inc(w_loaded, 16)
                wo_rows = w_out.rearrange("(g j d) n -> j d g n", j=HP, d=AD)
                for r in range(2 * HP):
                    sp.dma_start(wo[AD * r:AD * r + AD, :, :], wo_rows[r // 2]).then_inc(wo_loaded, 16)

                def do(name, i, b):
                    if name == "f_x":
                        if not isinstance(b, int):
                            sp.wait_ge(front_full, (b - 1) * NF + 2)
                            sp.dma_start(xin[:, :, :], x[b].rearrange("(t p) d -> p t d", p=P)).then_inc(x_in, 16)
                    elif name == "f_qe":
                        sp.wait_ge(front_free, b * NF + 3 + i)
                        sp.dma_start(scr[b, 0, P * i:P * i + P], qk_hi[:, i, :].bitcast(F32)).then_inc(parts_out, 16)
                        sp.wait_ge(lo_done, b * 4 + 1 + i)
                        sp.dma_start(scr[b, 1, P * i:P * i + P], qk_lo[:, i, :].bitcast(F32)).then_inc(parts_out, 16)
                    elif name == "f_load":
                        wait_apart(sp, K, parts_out, b * 128 + 64 * (i // 2 + 1))
                        if i == 0 and isinstance(b, int):
                            sp.wait_ge(stacks_set, 2)
                            sp.wait_ge(v_set, 3)
                        if not isinstance(b, int):
                            sp.wait_ge(sc_full, (b - 1) * UNITS + GU * (i + 1))
                        r0, t0 = 64 * (i % 2), 2 * (i // 2)
                        for t, dst_t, order in ((t0, Q, (0, 0, 1)), (t0 + 1, Kk, (0, 1, 0))):
                            for slot, part in enumerate(order):
                                sp.dma_start(
                                    dst_t[AD * slot:AD * slot + AD, HP * i:HP * i + HP, :].bitcast(F32),
                                    scr[b, part, P * t + r0:P * t + r0 + 64]
                                    .rearrange("(h d) n -> d h n", d=AD)).then_inc(stacked[i], 16)
                    elif name in ("mt", "f_mt"):
                        sp.wait_ge(mrow_done, b * AG + i + 1)
                        for j in range(HP):
                            sp.dma_start(Q[MROW:MROW + 1, HP * i + j, :].bitcast(F32),
                                         mrow[j:j + 1, i, :].bitcast(F32)).then_inc(m_in[i], 16)

                steps(sp, do)

            @block.gpsimd
            def _(pool):
                pool.memset(half[:, :], -0.5).then_inc(rstd_a, 1)
                pool.memset(Kk[:, :, :].bitcast(F32), 0.0).then_inc(stacks_set, 1)
                pool.wait_ge(stacks_set, 1)
                pool.memset(Kk[MROW:MROW + 1, :, :].bitcast(F32), 1.0).then_inc(stacks_set, 1)

                pool.wait_ge(stacks_set, 2)

                def do(name, i, b):
                    if name == "xr":
                        pool.wait_ge(y_done, b * TB)
                        pool.dma_start(xr[:, :, :], x[b].rearrange("(t p) d -> p t d", p=P)).then_inc(xr_in, 16)
                        pool.wait_ge(xr_in, b * 16 + 16)
                        pool.wait_ge(w_loaded, 112)
                        pool.tensor_tensor(xr[:, :, :], xr[:, :, :],
                                           bo[:, :].unsqueeze(1).to_broadcast([P, TB, DM]), ALU.add)\
                            .then_inc(xb_ready, 1)
                    elif name == "f_qe":
                        pool.wait_ge(front_free, b * NF + 3 + i)
                        pool.wait_ge(parts_out, b * 128)
                        pool.tensor_tensor(qk_lo[:, i, :], part_f[:, i % 2, :], qk_hi[:, i, :], ALU.subtract)\
                            .then_inc(lo_done, 1)
                    elif name == "f_v" and i == TB - 1:
                        pool.wait_ge(front_free, b * NF + NF)
                        vt = V[:, :, :, 0:AD]
                        pool.tensor_tensor(vt, vt, bv[:, :].rearrange("p (h d) -> p h d", d=AD).unsqueeze(1)
                                           .to_broadcast([P, TB, AH, AD]), ALU.add).then_inc(v_done, 1)
                    elif name == "z1" and i < AG - 1:
                        wait_apart(pool, K, norm, b * 8 + 2 * i + 2)
                        pool.tensor_copy(on[:, :, 0:AD], zn[:, :, :]).then_inc(zn_split, 1)
                        pool.wait_ge(zn_split, b * 8 + 2 * i + 1)
                        pool.tensor_tensor(on[:, :, AD:2 * AD], zn[:, :, :], on[:, :, 0:AD], ALU.subtract)\
                            .then_inc(zn_split, 1)
                    elif name == "out" and i == TB - 1:
                        wait_apart(pool, K, var_done, b + 1)
                        pool.tensor_scalar(ve[:, :], mv[:, :, 1], LN_EPS, None, ALU.add).then_inc(rstd_a, 1)
                        pool.wait_ge(rstd_a, b + 2)
                        pool.tensor_tensor(rs[:, :], ve[:, :], half[:, :], ALU.pow).then_inc(rstd_done, 1)
                    elif name == "end":
                        wait_apart(pool, K, rstd_done, b + 1)
                        wait_apart(pool, K, stored, b * 16)
                        for t in range(TB):
                            pool.tensor_scalar(out[:, t, :], y[:, t, :], mv[:, t, 0:1], rs[:, t:t + 1],
                                               ALU.subtract, ALU.mult).then_inc(out_done, 1)
                        pool.wait_ge(out_done, b * TB + TB)
                        pool.dma_start(dst[b, 1:1 + S].rearrange("(t p) d -> p t d", p=P),
                                       out[:, :, :]).then_inc(stored, 16)

                steps(pool, do)
                pool.wait_ge(stored, 16 * NB)


            @block.scalar
            def _(act):
                act.wait_ge(w_loaded, 112)
                for kt in range(KT):
                    nc.scalar.activation(w_hi[:, kt, :], w_raw[:, kt, :], ACT.Copy).then_inc(w_split, 1)
                act.wait_ge(wo_loaded, 128)
                nc.scalar.activation(wo_hi[:, :, :], wo[:, :, :], ACT.Copy).then_inc(wo_split, 1)

                def do(name, i, b):
                    if name == "f_xe":
                        for h in range(KT):
                            act.wait_ge(front_full, b * NF + h + 1)
                            nc.scalar.activation(xt_hi[:, h, :], FB[h][:, :], ACT.Identity)\
                                .then_inc(xhi_done, 1)
                    elif name == "f_qe":
                        act.wait_ge(front_full, b * NF + 3 + i)
                        act.wait_ge(parts_out, b * 128)
                        nc.scalar.activation(qk_hi[:, i, :], FB[i % 2][:, :], ACT.Identity,
                                             bias=bqk[:, i:i + 1])
                        act.wait_ge(lo_done, b * 4 + max(i - 1, 0))
                        nc.scalar.activation(part_f[:, i % 2, :], FB[i % 2][:, :], ACT.Identity,
                                             bias=bqk[:, i:i + 1]).then_inc(front_free, 1)
                    elif name == "f_v":
                        act.wait_ge(v_set, 2)
                        act.wait_ge(front_full, b * NF + 7 + i)
                        nc.scalar.activation(V[:, i, :, 0:AD], FB[i % 2][:, 0:DM]
                                             .rearrange("p (h d) -> p h d", d=AD), ACT.Identity)\
                            .then_inc(front_free, 1)
                    elif name == "z3":
                        act.wait_ge(z_turned, b * AG + i + 1)
                        if i == 0:
                            act.wait_ge(y_full, b * TB)
                        nc.scalar.activation(zt[:, i, :], ztf[:, :], ACT.Identity).then_inc(z_done, 1)
                    elif name in ("mt", "f_mt"):
                        act.wait_ge(mt_full, b * AG + i + 1)
                        act.wait_ge(m_in[i], b * 64)
                        nc.scalar.activation(mrow[:, i, :], MB[0:HP, :], ACT.Identity).then_inc(mrow_done, 1)
                    elif name in ("st", "f_st"):
                        j, h = i % TB, i // TB
                        act.wait_ge(sc_full, b * UNITS + i + 1)
                        q0 = max(P * j - S // 2, 0)
                        nq = S - P * j
                        nc.scalar.activation(PT[:, h // HP % 2, h % HP, QOFF[j]:QOFF[j] + nq],
                                             SC[i % 2][:, q0:q0 + nq], ACT.Exp, scale=AD ** -0.5)\
                            .then_inc(exp_done, 1)

                steps(act, do)

            @block.vector
            def _(dve):
                dve.memset(V[:, :, :, :], 0.0).then_inc(v_set, 1)
                dve.wait_ge(v_set, 1)
                dve.memset(V[:, :, :, AD:AD + 1], 1.0).then_inc(v_set, 1)
                dve.memset(Q[:, :, :].bitcast(F32), 0.0).then_inc(v_set, 1)
                dve.wait_ge(w_split, 2)
                for kt in range(KT):
                    dve.tensor_tensor(w_lo[:, kt, :], w_raw[:, kt, :], w_hi[:, kt, :], ALU.subtract)\
                        .then_inc(w_split, 1)
                dve.wait_ge(wo_split, 1)
                dve.tensor_tensor(wo_lo[:, :, :], wo[:, :, :], wo_hi[:, :, :], ALU.subtract).then_inc(wo_split, 1)

                def do(name, i, b):
                    if name == "f_xe":
                        for h in range(KT):
                            dve.wait_ge(xhi_done, b * KT + h + 1)
                            dve.tensor_tensor(xt_lo[:, h, :], FB[h][:, :], xt_hi[:, h, :], ALU.subtract)\
                                .then_inc(front_free, 1)
                    elif name in ("sm", "f_sm"):
                        q, h = i % TB, i // TB
                        dve.wait_ge(mx_full, b * UNITS + i + 1)
                        dve.tensor_reduce(negm[:, q, h:h + 1], MX[i % 2][:, 0:P * (q + 1)], AX.X, ALU.max,
                                          negate=True).then_inc(max_done, 1)
                    elif name == "z0":
                        dve.wait_ge(o_full, b * AG + i + 1)
                        dve.transpose(ot[:, :, :].rearrange("p c r -> p (c r)"), OB[:, :]).then_inc(o_free, 1)
                        dve.wait_ge(o_free, b * AG + i + 1)
                        dve.reciprocal(rc[:, :], ot[:, :, AD]).then_inc(norm, 1)
                    elif name == "z1":
                        dve.wait_ge(norm, b * 8 + 2 * i + 1)
                        dve.wait_ge(z_turned, b * AG + i)
                        dve.tensor_tensor(zn[:, :, :], ot[:, :, 0:AD],
                                          rc[:, :].unsqueeze(2).to_broadcast([P, NC, AD]), ALU.mult)\
                            .then_inc(norm, 1)
                        if i == AG - 1:
                            dve.wait_ge(norm, b * 8 + 2 * i + 2)
                            dve.tensor_copy(on[:, :, 0:AD], zn[:, :, :]).then_inc(zn_split, 1)
                            dve.wait_ge(zn_split, b * 8 + 2 * i + 1)
                            dve.tensor_tensor(on[:, :, AD:2 * AD], zn[:, :, :], on[:, :, 0:AD], ALU.subtract)\
                                .then_inc(zn_split, 1)
                    elif name == "z2":
                        dve.wait_ge(zn_split, b * 8 + 2 * i + 2)
                        dve.wait_ge(z_done, b * AG + i)
                        dve.transpose(ztf[:, :], on[:, :, :].rearrange("p c r -> p (c r)").bitcast(F32))\
                            .then_inc(z_turned, 1)
                    elif name == "out":
                        if i == 0:
                            dve.wait_ge(xb_ready, b + 1)
                            dve.wait_ge(out_done, b * TB)
                        dve.wait_ge(y_full, b * TB + i + 1)
                        dve.tensor_tensor(y[:, i, :], YB[i % 2][:, 0:DM], xr[:, i, :], ALU.add)\
                            .then_inc(y_done, 1)
                        dve.wait_ge(y_done, b * TB + i + 1)
                        dve.bn_stats(st[:, i, :], y[:, i, :]).then_inc(stats, 1)
                        if i == TB - 1:
                            for t in range(TB):
                                wait_apart(dve, K, stats, b * TB + t + 1)
                                m = dve.bn_aggr(mv[:, t, :], st[:, t, :])
                            m.then_inc(var_done, 1)

                steps(dve, do)

            @block.tensor
            def _(pe):
                def split_mm(o, a_hi, a_lo, r_hi, r_lo, first, last):
                    pe.matmul(o, a_hi, r_hi, start=first, stop=False)
                    pe.matmul(o, a_lo, r_hi, start=False, stop=False)
                    return pe.matmul(o, a_hi, r_lo, start=False, stop=last)

                def pass_wait(done, b, i):
                    if isinstance(b, int) and b == 0 and i < 2:
                        return
                    pe.wait_ge(done, b * UNITS + max(i - 1, 0))


                def do(name, i, b):
                    if name == "f_x":
                        pe.wait_ge(x_in, b * 16 + 16)
                        for h in range(KT):
                            if not isinstance(b, int):
                                pe.wait_ge(front_free, b * NF + h - 1)
                            for t in range(TB):
                                m = pe.transpose(FB[h][:, P * t:P * t + P], xin[:, t, P * h:P * h + P],
                                                 K["ident"][:, :])
                            m.then_inc(front_full, 1)
                    elif name == "f_qk":
                        col = (0, DM, P, DM + P)[i]
                        pe.wait_ge(w_split, 4)
                        pe.wait_ge(front_free, b * NF + max(1 + i, 2))
                        for h in range(KT):
                            m = split_mm(FB[i % 2][:, :], w_hi[:, h, col:col + P], w_lo[:, h, col:col + P],
                                         xt_hi[:, h, :], xt_lo[:, h, :], h == 0, h == KT - 1)
                        m.then_inc(front_full, 1)
                    elif name == "f_v":
                        pe.wait_ge(front_free, b * NF + 5 + i)
                        for h in range(KT):
                            tok = slice(P * i, P * i + P)
                            m = split_mm(FB[i % 2][:, 0:DM], xt_hi[:, h, tok], xt_lo[:, h, tok],
                                         w_hi[:, h, 2 * DM:], w_lo[:, h, 2 * DM:], h == 0, h == KT - 1)
                        m.then_inc(front_full, 1)
                    elif name in ("sm", "f_sm"):
                        q, h = i % TB, i // TB
                        if i % GU == 0:
                            pe.wait_ge(stacked[i // GU], b * 96 + 96)
                        pass_wait(max_done, b, i)
                        r, nk = MX[i % 2], max(P * (q + 1), 256)
                        pe.matmul(r[:, 0:nk], Q[0:MROW, h, P * q:P * q + P], Kk[0:MROW, h, 0:nk],
                                  start=True, stop=True)
                        pe.matmul(r[:, P * q:P * q + P], K["identb"][:, :], K["causal"][:, :], start=False,
                                  stop=True, skip_group_check=True).then_inc(mx_full, 1)
                    elif name in ("mt", "f_mt"):
                        pe.wait_ge(max_done, b * UNITS + GU * (i + 1))
                        pe.wait_ge(mrow_done, b * AG + i)
                        for q in range(TB):
                            m = pe.transpose(MB[0:HP, P * q:P * q + P], negm[:, q, HP * i:HP * i + HP],
                                             K["ident"][:, :])
                        m.then_inc(mt_full, 1)
                    elif name in ("st", "f_st"):
                        j, h = i % TB, i // TB
                        if i == 0:
                            pe.wait_ge(wo_split, 2)
                        if i % GU == 0:
                            pe.wait_ge(m_in[i // GU], b * 64 + 64)
                        pass_wait(exp_done, b, i)
                        q0, r = min(P * j, S // 2), SC[i % 2]
                        pe.matmul(r[:, 0:S - q0], Kk[0:MROW + 1, h, P * j:P * j + P], Q[0:MROW + 1, h, q0:S],
                                  start=True, stop=True)
                        pe.matmul(r[:, P * j - q0:P * j - q0 + P], K["identb"][:, :], K["window_t"][:, 0, :],
                                  start=False, stop=True, skip_group_check=True).then_inc(sc_full, 1)
                    elif name == "pv":
                        pe.wait_ge(exp_done, b * UNITS + GU * (i + 1))
                        pe.wait_ge(o_free, b * AG + i)
                        pe.wait_ge(y_done, b * TB)
                        pe.wait_ge(v_done, b + 1)
                        for j in range(TB):
                            for hh in range(HP):
                                m = pe.matmul(OB[32 * hh:32 * hh + 32, P * j:S], V[:, j, HP * i + hh, :],
                                              PT[:, i % 2, hh, QOFF[j]:QOFF[j] + S - P * j],
                                              start=(j == 0), stop=(j == TB - 1), skip_group_check=True)
                        m.then_inc(o_full, 1)
                    elif name == "out":
                        if i == 0:
                            pe.wait_ge(z_done, b * AG + AG)
                            pe.wait_ge(mrow_done, b * AG + AG + (0 if isinstance(b, int) else 2))
                        pe.wait_ge(y_done, b * TB + max(i - 1, 0))
                        tok = slice(P * i, P * i + P)
                        for g in range(AG):
                            pe.matmul(YB[i % 2][:, 0:DM], zt[:, g, tok], wo_hi[:, g, :],
                                      start=(g == 0), stop=False)
                            m = pe.matmul(YB[i % 2][:, 0:DM], zt[:, g, tok], wo_lo[:, g, :],
                                          start=False, stop=(g == AG - 1))
                        m.then_inc(y_full, 1)

                steps(pe, do)

        nc.clear_and_free_semaphores(signals)
        nc.all_engine_barrier()


def local_attention(nc, K, lay, x, wqkv, q_scale, k_scale, wo_w, rot, dst):
    with ExitStack() as ctx:
        sb = lambda name, shape, dt=F32: ctx.enter_context(nc.sbuf_tensor(f"l{lay}_" + name, shape, dt))
        ps = lambda name, shape: ctx.enter_context(nc.psum_tensor(f"l{lay}_" + name, shape, F32))
        sem = lambda name: ctx.enter_context(nc.semaphore(f"l{lay}_" + name))

        w_hi, w_lo = sb("w_hi", [P, KT, 3 * INNER], F32R), sb("w_lo", [P, KT, 3 * INNER], F32R)
        wo = sb("wo", [P, INNER // P, DM])
        scales = sb("scales", [P, 2, FD])
        rots = sb("rots", [P, 2, 2, TB, FD])
        xin = sb("xin", [P, TB, DM])
        xt_hi, xt_lo = sb("xt_hi", [P, KT, S + 1], F32R), sb("xt_lo", [P, KT, S + 1], F32R)
        sq = sb("sq", [P, 2, INNER])
        t1, t2 = sb("t1", [P, 2, 2, INNER]), sb("t2", [P, 2, 2, INNER])
        ss, inv, half = sb("ss", [P, 2, 2 * FH]), sb("inv", [P, 2, 2 * FH]), sb("half", [P, 2 * FH])
        qk = sb("qk", [P, TB, 2, INNER])
        Q1, K1 = sb("Q1", [P, FH, S], F32R), sb("K1", [P, FH, S], F32R)
        Q2, K2 = sb("Q2", [P, FH, S], F32R), sb("K2", [P, FH, S], F32R)
        V = sb("V", [P, TB, INNER])
        ones = sb("ones", [P, FD])
        LOW = 32
        negm = sb("negm", [P, TB, 2, 2, 2])
        mrow = sb("mrow", [2 * LOW, 2, S], F32R)
        PT = sb("PT", [P, 2, TB, 2, 2 * P])
        rsum = sb("rsum", [P, INNER // P, S])
        zt = sb("zt", [P, INNER // P, S])
        xr, out = sb("xr", [P, TB, DM]), sb("out", [P, TB, DM])

        FB = [ps("f0", [P, S]), ps("f1", [P, S])]
        MX = [ps("x0", [P, S]), ps("x1", [P, S])]
        SC = [ps("c0", [P, S]), ps("c1", [P, S])]
        OB, SB = ps("o", [P, S]), ps("s", [P, S])
        YB = [OB, SB]

        w_loaded, w_hi_done, w_lo_done, small = sem("w_loaded"), sem("w_hi_done"), sem("w_lo_done"), sem("small")
        q2_set, k2_set = sem("q2_set"), sem("k2_set")
        rots_in, rots_done = sem("rots_in"), sem("rots_done")
        x_in, front_full, hi_done = sem("x_in"), sem("front_full"), sem("hi_done")
        front_free = sem("front_free")
        sq_done, ss_raw, ss_done, inv_done = sem("sq_done"), sem("ss_raw"), sem("ss_done"), sem("inv_done")
        summed, rotated = sem("summed"), sem("rotated")
        stacked = [sem(f"stacked{p}") for p in range(FH // 2)]
        mx_full, max_done, sc_full, exp_done = sem("mx_full"), sem("max_done"), sem("sc_full"), sem("exp_done")
        mt_full, mhi_done, mrow_done = sem("mt_full"), sem("mhi_done"), sem("mrow_done")
        m_in = [sem("m_in0"), sem("m_in1")]
        o_full, o_out, ln_done, rsum_done, z_done = (
            sem("o_full"), sem("o_out"), sem("ln_done"), sem("rsum_done"), sem("z_done"))
        y_full, y_done = sem("y_full"), sem("y_done")
        xr_in, stored = sem("xr_in"), sem("stored")

        NF, QK_AT, T_AT, V_AT = 22, 2, 10, 18
        PAIRS, UNITS = FH // 2, FH // 2 * TB

        STEPS = [s.rsplit(":", 1) for s in """
            sm:8 st:0 sm:9 f_x:0 f_xe:0 st:1 sm:10 sm:11 f_qk:0 f_qe:0 st:2 sm:12 f_qk:1 f_qe:1 st:3
            sm:13 f_qk:2 st:4 sm:14 pv:0 f_qe:2 sm:15 z:0 f_qk:3 f_qe:3 mt:1 st:5 f_qe:4 f_qk:4 st:6
            f_qe:5 f_qk:5 st:7 f_qe:6 f_qk:6 st:8 f_qk:7 f_qe:7 xr:0 st:9 st:10 st:11 pv:1 st:12 z:1
            pv:2 z:2 f_t:0 f_te:0 st:13 f_t:1 f_te:1 st:14 f_t:2 f_te:2 f_sm:0 st:15 f_sm:1 f_t:3
            f_te:3 pv:3 z:3 f_sm:2 f_v:0 f_sm:3 f_sm:4 f_sm:5 zl:0 f_sm:6 f_v:1 f_sm:7 zn:0 f_v:2
            f_mt:0 f_v:3 out:0""".split()]
        STEPS = [(name, int(i)) for name, i in STEPS]

        def steps(eng, do):
            for name, i in STEPS:
                if name[0] == "f":
                    do(name, i, 0)
            with eng.Fori(0, NB - 1) as it:
                for name, i in STEPS:
                    do(name, i, it + 1 if name[0] == "f" else it)
            for name, i in STEPS:
                if name[0] != "f":
                    do(name, i, NB - 1)

        raw = qk[:, 0:3, :, :].rearrange("p t w n -> p (t w n)").rearrange("p (k n) -> p k n", k=KT)

        with nc.Block() as block:
            @block.sync
            def _(sp):
                sp.dma_start(xin[:, :, :], x[0].rearrange("(t p) d -> p t d", p=P)).then_inc(x_in, 16)
                sp.dma_start(raw, wqkv.rearrange("(k p) n -> p k n", p=P)).then_inc(w_loaded, 16)
                sp.dma_start(wo[:, :, :], wo_w.rearrange("(k p) n -> p k n", p=P)).then_inc(w_loaded, 16)
                sp.dma_start(scales[:, 0, :], q_scale.partition_broadcast(P)).then_inc(rots_in, 16)
                sp.dma_start(scales[:, 1, :], k_scale.partition_broadcast(P)).then_inc(rots_in, 16)
                for w in range(2):
                    for c in range(2):
                        sp.dma_start(rots[:, w, c, :, :], rot[w, c].rearrange("(t p) d -> p t d", p=P))\
                            .then_inc(rots_in, 16)

                def do(name, i, b):
                    if name == "f_x":
                        if not isinstance(b, int):
                            sp.wait_ge(front_full, (b - 1) * NF + 2)
                            sp.dma_start(xin[:, :, :], x[b].rearrange("(t p) d -> p t d", p=P)).then_inc(x_in, 16)
                    elif name == "f_te":
                        sp.wait_ge(hi_done, b * 10 + 4 + 2 * i)
                        for hh in range(2):
                            h, own, other = 2 * i + hh, slice(FD * hh, FD * hh + FD), slice(FD - FD * hh, P - FD * hh)
                            sp.dma_start(K1[other, h, :].bitcast(F32), K1[own, h, :].bitcast(F32))\
                                .then_inc(stacked[i], 16)
                            sp.dma_start(Q2[own, h, :].bitcast(F32), Q1[own, h, :].bitcast(F32))\
                                .then_inc(stacked[i], 16)
                    elif name in ("mt", "f_mt"):
                        sp.wait_ge(mrow_done, b * 2 + i + 1)
                        for hh in range(2):
                            for part in range(2):
                                r, q = LOW * part + 2 * hh, FD - FD * hh + LOW * part
                                sp.dma_start(Q2[q:q + 1, 4 * i + hh:4 * i + 4:2, :].bitcast(F32),
                                             mrow[r:r + 2, i, :].bitcast(F32)).then_inc(m_in[i], 16)
                    elif name == "xr":
                        sp.wait_ge(y_done, b * TB)
                        sp.dma_start(xr[:, :, :], x[b].rearrange("(t p) d -> p t d", p=P)).then_inc(xr_in, 16)

                steps(sp, do)

            @block.gpsimd
            def _(pool):
                pool.memset(half[:, :], -0.5).then_inc(small, 1)
                pool.memset(ones[:, :], 1.0).then_inc(small, 1)
                pool.memset(xt_hi[:, 1, 0:1].bitcast(F32), 0.0).then_inc(small, 1)
                pool.memset(xt_lo[:, 1, 0:1].bitcast(F32), 0.0).then_inc(small, 1)
                pool.wait_ge(k2_set, 1)
                pool.wait_ge(small, 4)
                for hh in range(2):
                    for low in (0, LOW):
                        r = FD - FD * hh + low
                        pool.memset(K2[r:r + 1, hh:FH:2, :].bitcast(F32), 1.0).then_inc(small, 1)
                pool.wait_ge(small, 8)

                def do(name, i, b):
                    if name == "f_qe":
                        blk, w, par = i // 2, i % 2, i // 2 % 2
                        n = b * TB + blk
                        if w == 1:
                            pool.wait_ge(ss_done, n + 1)
                            pool.tensor_tensor(inv[:, par, :], ss[:, par, :], half[:, :], ALU.pow)\
                                .then_inc(inv_done, 1)
                        pool.wait_ge(front_free, b * NF + QK_AT + i + 1)
                        pool.tensor_tensor(t1[:, par, w, :], t1[:, par, w, :], t2[:, par, w, :], ALU.add)\
                            .then_inc(summed, 1)
                        for w in range(2 * w):
                            if w == 0:
                                pool.wait_ge(inv_done, n + 1)
                            pool.wait_ge(summed, 2 * n + w + 1)
                            pool.tensor_tensor(qk[:, blk, w, :].rearrange("p (h d) -> p h d", d=FD),
                                               t1[:, par, w, :].rearrange("p (h d) -> p h d", d=FD),
                                               inv[:, par, FH * w:FH * w + FH].unsqueeze(2)
                                               .to_broadcast([P, FH, FD]), ALU.mult).then_inc(rotated, 1)

                    elif name == "out":
                        pool.wait_ge(y_done, b * TB + TB)
                        pool.dma_start(dst[b, 1:1 + S].rearrange("(t p) d -> p t d", p=P),
                                       out[:, :, :]).then_inc(stored, 16)

                steps(pool, do)
                pool.wait_ge(stored, 16 * NB)

            @block.scalar
            def _(act):
                act.wait_ge(w_loaded, 32)
                for kt in range(KT):
                    nc.scalar.activation(w_hi[:, kt, :], raw[:, kt, :], ACT.Copy).then_inc(w_hi_done, 1)

                def do(name, i, b):
                    if name == "f_xe":
                        for h in range(KT):
                            act.wait_ge(front_full, b * NF + h + 1)
                            nc.scalar.activation(xt_hi[:, h, h:S + h], FB[h][:, :], ACT.Identity)\
                                .then_inc(hi_done, 1)
                    elif name == "f_qe":
                        w = i % 2
                        act.wait_ge(front_full, b * NF + QK_AT + i + 1)
                        if not (isinstance(b, int) and i < 2):
                            act.wait_ge(ss_raw, b * 8 + i - 1)
                        nc.scalar.activation(sq[:, w, :], FB[w][:, :], ACT.Square).then_inc(sq_done, 1)
                    elif name == "f_te":
                        for w, dst_t in enumerate((Q1, K1)):
                            act.wait_ge(front_full, b * NF + T_AT + 2 * i + w + 1)
                            for hh in range(2):
                                own = slice(FD * hh, FD * hh + FD)
                                m = nc.scalar.activation(dst_t[own, 2 * i + hh, :], FB[w][own, :], ACT.Identity)
                            m.then_inc(hi_done, 1)
                    elif name in ("mt", "f_mt"):
                        act.wait_ge(mt_full, b * 2 + i + 1)
                        act.wait_ge(m_in[i], b * 64)
                        nc.scalar.activation(mrow[0:4, i, :], SB[0:4, :], ACT.Identity).then_inc(mhi_done, 1)
                    elif name == "st":
                        p, j = i // TB, i % TB
                        act.wait_ge(sc_full, b * UNITS + i + 1)
                        nq = P if j == TB - 1 else 2 * P
                        src = SC[i % 2][:, :].rearrange("p (h q) -> p h q", h=2)
                        nc.scalar.activation(PT[:, p % 2, j, :, 0:nq], src[:, :, 2 * P - nq:2 * P], ACT.Exp,
                                             scale=8.0).then_inc(exp_done, 1)
                    elif name == "z":
                        act.wait_ge(o_full, b * PAIRS + i + 1)
                        act.wait_ge(z_done, b * PAIRS)
                        nc.scalar.activation(rsum[:, i, :], SB[:, :], ACT.Identity)
                        act.wait_ge(y_full, b * TB)
                        nc.scalar.activation(zt[:, i, :], OB[:, :], ACT.Identity).then_inc(o_out, 1)
                    elif name == "zl":
                        act.wait_ge(o_out, b * PAIRS + PAIRS)
                        nc.scalar.activation(rsum[:, :, :], rsum[:, :, :], ACT.Ln).then_inc(ln_done, 1)
                        act.wait_ge(ln_done, b + 1)
                        for p in range(PAIRS):
                            nc.scalar.activation(rsum[:, p, :], rsum[:, p, :], ACT.Exp, scale=-1.0)\
                                .then_inc(rsum_done, 1)

                steps(act, do)

            @block.vector
            def _(dve):
                dve.memset(K2[:, :, :].bitcast(F32), 0.0).then_inc(k2_set, 1)
                dve.memset(Q2[:, :, :].bitcast(F32), 0.0).then_inc(q2_set, 1)
                for kt in range(KT):
                    dve.wait_ge(w_hi_done, kt + 1)
                    dve.tensor_tensor(w_lo[:, kt, :], raw[:, kt, :], w_hi[:, kt, :], ALU.subtract)\
                        .then_inc(w_lo_done, 1)
                dve.wait_ge(rots_in, 96)
                H2 = FD // 2
                for w in range(2):
                    sc = scales[:, w:w + 1, :].to_broadcast([P, TB, FD])
                    dve.tensor_tensor(rots[:, w, 0, :, :], rots[:, w, 0, :, :], sc, ALU.mult)\
                        .then_inc(rots_done, 1)
                    dve.scalar_tensor_tensor(out=rots[:, w, 1, :, 0:H2], in0=rots[:, w, 1, :, 0:H2], scalar=-1.0,
                                             in1=sc[:, :, H2:FD], op0=ALU.mult, op1=ALU.mult)\
                        .then_inc(rots_done, 1)
                    dve.tensor_tensor(rots[:, w, 1, :, H2:FD], rots[:, w, 1, :, H2:FD], sc[:, :, 0:H2],
                                      ALU.mult).then_inc(rots_done, 1)
                dve.wait_ge(rots_done, 6)

                def do(name, i, b):
                    if name == "f_xe":
                        for h in range(KT):
                            dve.wait_ge(hi_done, b * 10 + h + 1)
                            dve.tensor_tensor(xt_lo[:, h, h:S + h], FB[h][:, :], xt_hi[:, h, h:S + h],
                                              ALU.subtract).then_inc(front_free, 1)
                    elif name == "f_qe":
                        blk, w, par = i // 2, i % 2, i // 2 % 2
                        if not (isinstance(b, int) and blk < 2):
                            dve.wait_ge(rotated, b * 8 + 2 * blk - 2)
                        f = FB[w][:, :].rearrange("p (h d) -> p h d", d=FD)
                        a = t1[:, par, w, :].rearrange("p (h d) -> p h d", d=FD)
                        c = t2[:, par, w, :].rearrange("p (h d) -> p h d", d=FD)
                        cs = lambda k, lo, hi: rots[:, w, k, blk, lo:hi].unsqueeze(1)\
                            .to_broadcast([P, FH, hi - lo])
                        dve.wait_ge(sq_done, b * 8 + i + 1)
                        dve.tensor_reduce(ss[:, par, FH * w:FH * w + FH],
                                          sq[:, w, :].rearrange("p (h d) -> p h d", d=FD), AX.X, ALU.add)\
                            .then_inc(ss_raw, 1)
                        if w == 1:
                            dve.wait_ge(ss_raw, b * 8 + i + 1)
                            dve.tensor_scalar(ss[:, par, :], ss[:, par, :], 1e-24, None, ALU.max)\
                                .then_inc(ss_done, 1)
                        dve.tensor_tensor(a, f, cs(0, 0, FD), ALU.mult)
                        dve.tensor_tensor(c[:, :, 0:H2], f[:, :, H2:FD], cs(1, 0, H2), ALU.mult)
                        dve.tensor_tensor(c[:, :, H2:FD], f[:, :, 0:H2], cs(1, H2, FD), ALU.mult)\
                            .then_inc(front_free, 1)
                    elif name == "f_te":
                        for w in range(2):
                            dve.wait_ge(hi_done, b * 10 + 3 + 2 * i + w)
                            for hh in range(2):
                                h, own = 2 * i + hh, slice(FD * hh, FD * hh + FD)
                                other = slice(FD - FD * hh, P - FD * hh)
                                if w == 0:
                                    m = dve.tensor_tensor(Q1[other, h, :], FB[0][own, :], Q1[own, h, :],
                                                          ALU.subtract)
                                else:
                                    m = dve.tensor_tensor(K2[own, h, :], FB[1][own, :], K1[own, h, :],
                                                          ALU.subtract)
                            m.then_inc(front_free, 1)
                    elif name == "f_v":
                        dve.wait_ge(front_full, b * NF + V_AT + i + 1)
                        dve.tensor_copy(V[:, i, :], FB[i % 2][:, :]).then_inc(front_free, 1)
                    elif name in ("sm", "f_sm"):
                        p, q = i // TB, i % TB
                        dve.wait_ge(mx_full, b * UNITS + i + 1)
                        dve.tensor_reduce(negm[:, q, p // 2, :, p % 2],
                                          MX[i % 2][:, :].rearrange("p (h k) -> p h k", h=2), AX.X,
                                          ALU.max, negate=True).then_inc(max_done, 1)
                    elif name in ("mt", "f_mt"):
                        dve.wait_ge(mhi_done, b * 2 + i + 1)
                        dve.tensor_tensor(mrow[LOW:LOW + 4, i, :], SB[0:4, :], mrow[0:4, i, :], ALU.subtract)\
                            .then_inc(mrow_done, 1)
                    elif name == "zn":
                        for p in range(PAIRS):
                            dve.wait_ge(rsum_done, b * PAIRS + p + 1)
                            dve.tensor_tensor(zt[:, p, :], zt[:, p, :], rsum[:, p, :], ALU.mult)\
                                .then_inc(z_done, 1)
                    elif name == "out":
                        dve.wait_ge(xr_in, b * 16 + 16)
                        dve.wait_ge(stored, b * 16)
                        for t in range(TB):
                            dve.wait_ge(y_full, b * TB + t + 1)
                            dve.tensor_tensor(out[:, t, :], YB[t % 2][:, 0:DM], xr[:, t, :], ALU.add)\
                                .then_inc(y_done, 1)

                steps(dve, do)

            @block.tensor
            def _(pe):
                def split_mm(o, a_hi, a_lo, r_hi, r_lo, first, last):
                    pe.matmul(o, a_hi, r_hi, start=first, stop=False)
                    pe.matmul(o, a_lo, r_hi, start=False, stop=False)
                    return pe.matmul(o, a_hi, r_lo, start=False, stop=last)

                def front_wait(b, n):
                    if not (isinstance(b, int) and n < 2):
                        pe.wait_ge(front_free, b * NF + n - 1)

                def pass_wait(done, b, i):
                    if isinstance(b, int) and b == 0 and i < 2:
                        return
                    pe.wait_ge(done, b * UNITS + max(i - 1, 0))

                def do(name, i, b):
                    if name == "f_x":
                        pe.wait_ge(x_in, b * 16 + 16)
                        for h in range(KT):
                            front_wait(b, h)
                            for t in range(TB):
                                m = pe.transpose(FB[h][:, P * t:P * t + P], xin[:, t, P * h:P * h + P],
                                                 K["ident"][:, :])
                            m.then_inc(front_full, 1)
                    elif name == "f_qk":
                        w, tok = i % 2, slice(P * (i // 2), P * (i // 2) + P)
                        pe.wait_ge(w_lo_done, 2)
                        pe.wait_ge(small, 4)
                        if i == 0:
                            pe.wait_ge(front_free, b * NF + 2)
                        else:
                            front_wait(b, QK_AT + i)
                        col = slice(INNER * w, INNER * w + INNER)
                        for h in range(KT):
                            m = split_mm(FB[w][:, :], xt_hi[:, h, tok], xt_lo[:, h, tok], w_hi[:, h, col],
                                         w_lo[:, h, col], h == 0, h == KT - 1)
                        m.then_inc(front_full, 1)
                    elif name == "f_t":
                        pe.wait_ge(rotated, b * 8 + 8)
                        for w in range(2):
                            front_wait(b, T_AT + 2 * i + w)
                            for t in range(TB):
                                m = pe.transpose(FB[w][:, P * t:P * t + P], qk[:, t, w, P * i:P * i + P],
                                                 K["ident"][:, :])
                            m.then_inc(front_full, 1)
                    elif name == "f_v":
                        front_wait(b, V_AT + i)
                        tok = slice(P * i, P * i + P)
                        for h in range(KT):
                            m = split_mm(FB[i % 2][:, :], xt_hi[:, h, tok], xt_lo[:, h, tok],
                                         w_hi[:, h, 2 * INNER:], w_lo[:, h, 2 * INNER:], h == 0, h == KT - 1)
                        m.then_inc(front_full, 1)
                    elif name in ("sm", "f_sm"):
                        p, q = i // TB, i % TB
                        if q == 0:
                            pe.wait_ge(small, 8)
                            pe.wait_ge(q2_set, 1)
                            pe.wait_ge(stacked[p], b * 64 + 64)
                            pe.wait_ge(front_free, b * NF + T_AT + 2 * p + 2)
                        pass_wait(max_done, b, i)
                        k0 = P * max(q - 1, 0)
                        r = MX[i % 2][:, :].rearrange("p (h k) -> p h k", h=2)
                        for hh in range(2):
                            h = 2 * p + hh
                            pe.matmul(r[:, hh, :], Q1[:, h, P * q:P * q + P], K1[:, h, k0:k0 + 2 * P],
                                      start=(hh == 0), stop=True, skip_group_check=True)
                        mask = K["window"] if q else K["window0"]
                        pe.matmul(r, K["identb"][:, :],
                                  mask[:, :, :].rearrange("p b k -> p (b k)").unsqueeze(1)
                                  .to_broadcast([P, 2, 2 * P]), start=False, stop=True,
                                  skip_group_check=True).then_inc(mx_full, 1)
                    elif name in ("mt", "f_mt"):
                        pe.wait_ge(max_done, b * UNITS + 8 * i + 8)
                        pe.wait_ge(o_out, b * PAIRS + i)
                        if name == "f_mt" and not isinstance(b, int):
                            pe.wait_ge(y_done, (b - 1) * TB)
                        for q in range(TB):
                            m = pe.transpose(SB[0:4, P * q:P * q + P],
                                             negm[:, q, i].rearrange("p a b -> p (a b)"), K["ident"][:, :])
                        m.then_inc(mt_full, 1)
                    elif name == "st":
                        p, j = i // TB, i % TB
                        if i % 8 == 0:
                            pe.wait_ge(m_in[i // 8], b * 64 + 64)
                        pass_wait(exp_done, b, i)
                        q0 = P * min(j, TB - 2)
                        key, qry = slice(P * j, P * j + P), slice(q0, q0 + 2 * P)
                        o = SC[i % 2][:, :].rearrange("p (h q) -> p h q", h=2)
                        for hh in range(2):
                            h = 2 * p + hh
                            pe.matmul(o[:, hh, :], K1[:, h, key], Q1[:, h, qry], start=(hh == 0), stop=False,
                                      skip_group_check=True)
                            pe.matmul(o[:, hh, :], K2[:, h, key], Q2[:, h, qry], start=False, stop=True,
                                      skip_group_check=True)
                        if j < TB - 1:
                            mask = K["window_t"][:, :, :].rearrange("p b q -> p (b q)")
                        else:
                            o, mask = o[:, :, P:2 * P], K["window_t"][:, 0, :]
                        pe.matmul(o, K["identb"][:, :], mask.unsqueeze(1).to_broadcast([P, 2, mask.shape[1]]),
                                  start=False, stop=True, skip_group_check=True).then_inc(sc_full, 1)
                    elif name == "pv":
                        pe.wait_ge(exp_done, b * UNITS + TB * i + TB)
                        pe.wait_ge(o_out, b * PAIRS + i)
                        pe.wait_ge(mrow_done, b * 2 + (1 if i == 0 else 2))
                        pe.wait_ge(y_done, b * TB)
                        pe.wait_ge(front_free, b * NF + NF)
                        for j in range(TB):
                            nq = P if j == TB - 1 else 2 * P
                            for hh in range(2):
                                h, rows = 2 * i + hh, slice(FD * hh, FD * hh + FD)
                                pe.matmul(OB[rows, P * j:P * j + nq], V[:, j, FD * h:FD * h + FD],
                                          PT[:, i % 2, j, hh, 0:nq], start=(j == 0), stop=(j == TB - 1),
                                          skip_group_check=True)
                            for hh in range(2):
                                rows = slice(FD * hh, FD * hh + FD)
                                m = pe.matmul(SB[rows, P * j:P * j + nq], ones[:, :], PT[:, i % 2, j, hh, 0:nq],
                                              start=(j == 0), stop=(j == TB - 1), skip_group_check=True)
                        m.then_inc(o_full, 1)
                    elif name == "out":
                        pe.wait_ge(z_done, b * PAIRS + PAIRS)
                        pe.wait_ge(mrow_done, b * 2 + (2 if isinstance(b, int) else 3))
                        for t in range(TB):
                            pe.wait_ge(y_done, b * TB + max(t - 1, 0))
                            for p in range(INNER // P):
                                m = pe.matmul(YB[t % 2][:, 0:DM], zt[:, p, P * t:P * t + P], wo[:, p, :],
                                              start=(p == 0), stop=(p == INNER // P - 1))
                            m.then_inc(y_full, 1)

                steps(pe, do)


def feed_forward(nc, K, lay, x, ln_g, ln_b, w1_w, b1_w, w2_w, b2_w, residual, dst):
    with ExitStack() as ctx:
        sb = lambda name, shape, dt=F32: ctx.enter_context(nc.sbuf_tensor(f"m{lay}_" + name, shape, dt))
        ps = lambda name, shape: ctx.enter_context(nc.psum_tensor(f"m{lay}_" + name, shape, F32))
        sem = lambda name: ctx.enter_context(nc.semaphore(f"m{lay}_" + name))
        last = residual is not None
        loads = 6
        w2_loads = 3

        w_raw = sb("w_raw", [P, KT, 2 * HID])
        w_hi, w_lo = sb("w_hi", [P, KT, 2 * HID], F32R), sb("w_lo", [P, KT, 2 * HID], F32R)
        w2 = sb("w2", [HT, NT, DM])
        w2_hi, w2_lo = sb("w2_hi", [HT, NT, DM], F32R), sb("w2_lo", [HT, NT, DM], F32R)
        b1 = sb("b1", [HT, 2, NT])
        gam, bet = sb("gam", [P, KT]), sb("bet", [P, KT])
        b2 = sb("b2", [P, DM])
        h = sb("h", [P, TB, DM])
        hn = sb("hn", [P, TB, DM])
        st, mv = sb("st", [P, TB, 6]), sb("mv", [P, TB, 2])
        ve, rs, half = sb("ve", [P, TB]), sb("rs", [P, TB]), sb("half", [P, TB])
        ht = sb("ht", [P, KT, S])
        ht_hi, ht_lo = sb("ht_hi", [P, KT, S], F32R), sb("ht_lo", [P, KT, S], F32R)
        gate = sb("gate", [HT, 2, S])
        hid = sb("hid", [HT, 2, S])
        hid_hi, hid_lo = sb("hid_hi", [HT, NT, S], F32R), sb("hid_lo", [HT, NT, S], F32R)
        xr = sb("xr", [P, TB, DM])
        res = sb("res", [P, TB, DM])
        y, out = sb("y", [P, TB, DM]), sb("out", [P, TB, DM])
        st2, mv2 = sb("st2", [P, TB, 6]), sb("mv2", [P, TB, 2])
        ve2, rs2 = sb("ve2", [P, TB]), sb("rs2", [P, TB])

        FB = [ps("f0", [P, S]), ps("f1", [P, S])]
        AB = [[ps(f"a{i}", [P, S]), ps(f"g{i}", [P, S])] for i in range(2)]
        WB = [ps("w0", [P, S]), ps("w1", [P, S])]

        w_loaded, loaded, w_hi_done, w_lo_done = sem("w_loaded"), sem("loaded"), sem("w_hi_done"), sem("w_lo_done")
        h_in, stats, var_done, rstd_done = sem("h_in"), sem("stats"), sem("var_done"), sem("rstd_done")
        normed, turned, scaled, hi_done, lo_done = (
            sem("normed"), sem("turned"), sem("scaled"), sem("hi_done"), sem("lo_done"))
        ag_full, gate_done, hid_done = sem("ag_full"), sem("gate_done"), sem("hid_done")
        upper_done, lower_done, last_lower = sem("upper_done"), sem("lower_done"), sem("last_lower")
        w2_loaded, w2_split = sem("w2_loaded"), sem("w2_split")
        w2_full, y_done, xr_in, res_in, xb_done, stored = (
            sem("w2_full"), sem("y_done"), sem("xr_in"), sem("res_in"), sem("xb_done"), sem("stored"))
        if last:
            res_done = sem("res_done")
            stats2, var2_done, rstd2_done, out_done = (
                sem("stats2"), sem("var2_done"), sem("rstd2_done"), sem("out_done"))

        STEPS = [("f_in", 0), ("w1", 3), ("h", 2), ("f_n", 0), ("xr", 0), ("w1", 4), ("h", 3), ("f_m", 0), ("w1", 5), ("h", 4),
                 ("f_t", 0), ("h", 5), ("w2", 0), ("f_w1", 0), ("f_w1", 1), ("f_h", 0), ("fin", 0), ("f_w1", 2),
                 ("f_h", 1)]
        FIRST = [s for s in STEPS if s[0][0] == "f" and s[0] != "fin"]
        FIRST.insert(3, ("w", 0))

        def steps(eng, do):
            for name, i in FIRST:
                do(name, i, 0)
            with eng.Fori(0, NB - 1) as it:
                for name, i in STEPS:
                    do(name, i, it + 1 if (name, i) in FIRST else it)
            for name, i in STEPS:
                if (name, i) not in FIRST:
                    do(name, i, NB - 1)

        with nc.Block() as block:
            @block.sync
            def _(sp):
                def load_h(b):
                    sp.dma_start(h[:, :, 0:P], x[b, 1:1 + S, 0:P].rearrange("(t p) d -> p t d", p=P))\
                        .then_inc(h_in, 16)
                    sp.dma_start(h[:, :, P:DM], x[b, 0:S, P:DM].rearrange("(t p) d -> p t d", p=P))\
                        .then_inc(h_in, 16)

                load_h(0)
                sp.dma_start(w_raw[:, :, :], w1_w.rearrange("(k p) n -> p k n", p=P)).then_inc(w_loaded, 16)
                sp.dma_start(gam[:, :], ln_g.rearrange("(k p) -> p k", p=P),
                             allow_slow_non_contiguous=True).then_inc(loaded, 16)
                sp.dma_start(bet[:, :], ln_b.rearrange("(k p) -> p k", p=P),
                             allow_slow_non_contiguous=True).then_inc(loaded, 16)
                full = HT * (NT - 1)
                for k in range(2):
                    sp.dma_start(b1[:, k, 0:NT - 1], b1_w[HID * k:HID * k + full].rearrange("(n p) -> p n", p=HT),
                                 allow_slow_non_contiguous=True).then_inc(loaded, 16)
                    sp.dma_start(b1[0:HID - full, k, NT - 1:NT], b1_w[HID * k + full:HID * k + HID].unsqueeze(1),
                                 allow_slow_non_contiguous=True).then_inc(loaded, 16)
                sp.dma_start(w2[:, 0:NT - 1, :], w2_w[0:full].rearrange("(n p) d -> p n d", p=HT))\
                    .then_inc(w2_loaded, 16)
                sp.dma_start(w2[0:HID - full, NT - 1, :], w2_w[full:HID]).then_inc(w2_loaded, 16)
                sp.dma_start(b2[:, :], b2_w.partition_broadcast(P)).then_inc(w2_loaded, 16)

                def do(name, i, b):
                    if name == "f_in":
                        if not isinstance(b, int):
                            sp.wait_ge(normed, b * TB)
                            load_h(b)
                    elif name == "xr":
                        sp.wait_ge(y_done, b * TB)
                        sp.dma_start(xr[:, :, :], x[b, 1:1 + S].rearrange("(t p) d -> p t d", p=P))\
                            .then_inc(xr_in, 16)
                        if last:
                            sp.dma_start(res[:, :, :], residual[b, 1:1 + S].rearrange("(t p) d -> p t d", p=P))\
                                .then_inc(res_in, 16)

                steps(sp, do)

            @block.gpsimd
            def _(pool):
                pool.memset(half[:, :], -0.5).then_inc(rstd_done, 1)
                pool.wait_ge(rstd_done, 1)

                def do(name, i, b):
                    if name == "xr":
                        pool.wait_ge(w2_loaded, 16 * w2_loads)
                        if last:
                            pool.wait_ge(res_done, b + 1)
                        else:
                            pool.wait_ge(xr_in, b * 16 + 16)
                        pool.tensor_tensor(xr[:, :, :], xr[:, :, :],
                                           b2[:, :].unsqueeze(1).to_broadcast([P, TB, DM]), ALU.add)\
                            .then_inc(xb_done, 1)
                    elif name == "f_n":
                        wait_apart(pool, K, var_done, b + 1)
                        pool.tensor_scalar(ve[:, :], mv[:, :, 1], LN_EPS, None, ALU.add).then_inc(rstd_done, 1)
                        pool.wait_ge(rstd_done, 2 * b + 2)
                        pool.tensor_tensor(rs[:, :], ve[:, :], half[:, :], ALU.pow).then_inc(rstd_done, 1)
                    elif name == "f_t":
                        for k in range(KT):
                            pool.wait_ge(hi_done, b * KT + k + 1)
                            pool.tensor_tensor(ht_lo[:, k, :], ht[:, k, :], ht_hi[:, k, :], ALU.subtract)\
                                .then_inc(lo_done, 1)
                    elif name in ("h", "f_h") and i < NT - 1:
                        rows = tile_rows(i)
                        pool.wait_ge(upper_done, b * NT + i + 1)
                        pool.tensor_tensor(hid_lo[0:rows, i, :], hid[0:rows, i % 2, :], hid_hi[0:rows, i, :],
                                           ALU.subtract).then_inc(lower_done, 1)
                    elif name == "w2" and last:
                        wait_apart(pool, K, var2_done, b + 1)
                        pool.tensor_scalar(ve2[:, :], mv2[:, :, 1], LN_EPS, None, ALU.add).then_inc(rstd2_done, 1)
                        pool.wait_ge(rstd2_done, 2 * b + 1)
                        pool.tensor_tensor(rs2[:, :], ve2[:, :], half[:, :], ALU.pow).then_inc(rstd2_done, 1)

                    if name == "fin":
                        wait_apart(pool, K, out_done if last else y_done, b * TB + TB)
                        pool.dma_start(dst[b].rearrange("(t p) d -> p t d", p=P),
                                       (out if last else y)[:, :, :]).then_inc(stored, 16)

                steps(pool, do)
                pool.wait_ge(stored, 16 * NB)

            @block.scalar
            def _(act):
                def do(name, i, b):
                    if name == "w":
                        act.wait_ge(w_loaded, 16)
                        for k in range(KT):
                            nc.scalar.activation(w_hi[:, k, :], w_raw[:, k, :], ACT.Copy).then_inc(w_hi_done, 1)
                        act.wait_ge(w2_loaded, 16 * w2_loads)
                        nc.scalar.activation(w2_hi[:, 0:NT - 1, :], w2[:, 0:NT - 1, :], ACT.Copy)
                        nc.scalar.activation(w2_hi[0:tile_rows(NT - 1), NT - 1, :], w2[0:tile_rows(NT - 1), NT - 1, :],
                                             ACT.Copy).then_inc(w2_split, 1)
                    elif name == "f_t":
                        act.wait_ge(loaded, 16 * loads)
                        for k in range(KT):
                            act.wait_ge(turned, b * KT + k + 1)
                            nc.scalar.activation(ht[:, k, :], FB[k][:, :], ACT.Identity, bias=bet[:, k:k + 1],
                                                 scale=gam[:, k:k + 1]).then_inc(scaled, 1)
                    elif name in ("w1", "f_w1"):
                        n, rows = b * NT + i, tile_rows(i)
                        act.wait_ge(ag_full, n + 1)
                        act.wait_ge(hid_done, b * NT + max(i - 1, 0))
                        nc.scalar.activation(gate[0:rows, i % 2, :], AB[i % 2][1][0:rows, :], ACT.Gelu,
                                             bias=b1[0:rows, 1, i:i + 1]).then_inc(gate_done, 1)
                    elif name in ("h", "f_h"):
                        rows = tile_rows(i)
                        act.wait_ge(hid_done, b * NT + i + 1)
                        act.wait_ge(w2_full, b * TB)
                        nc.scalar.activation(hid_hi[0:rows, i, :], hid[0:rows, i % 2, :], ACT.Identity)\
                            .then_inc(upper_done, 1)

                steps(act, do)

            @block.vector
            def _(dve):
                def do(name, i, b):
                    if name == "w":
                        for k in range(KT):
                            dve.wait_ge(w_hi_done, k + 1)
                            dve.tensor_tensor(w_lo[:, k, :], w_raw[:, k, :], w_hi[:, k, :], ALU.subtract)\
                                .then_inc(w_lo_done, 1)
                        dve.wait_ge(w2_split, 1)
                        dve.tensor_tensor(w2_lo[:, 0:NT - 1, :], w2[:, 0:NT - 1, :], w2_hi[:, 0:NT - 1, :], ALU.subtract)\
                            .then_inc(w2_split, 1)
                        r = slice(0, tile_rows(NT - 1))
                        dve.tensor_tensor(w2_lo[r, NT - 1, :], w2[r, NT - 1, :], w2_hi[r, NT - 1, :], ALU.subtract)\
                            .then_inc(w2_split, 1)
                    elif name == "f_n":
                        dve.wait_ge(h_in, b * 32 + 32)
                        for t in range(TB):
                            dve.bn_stats(st[:, t, :], h[:, t, :]).then_inc(stats, 1)
                        for t in range(TB):
                            wait_apart(dve, K, stats, b * TB + t + 1)
                            m = dve.bn_aggr(mv[:, t, :], st[:, t, :])
                        m.then_inc(var_done, 1)
                    elif name == "f_m":
                        dve.wait_ge(rstd_done, 2 * b + 3)
                        if not isinstance(b, int):
                            dve.wait_ge(turned, b * KT)
                        for t in range(TB):
                            dve.tensor_scalar(hn[:, t, :], h[:, t, :], mv[:, t, 0:1], rs[:, t:t + 1],
                                              ALU.subtract, ALU.mult).then_inc(normed, 1)
                    elif name == "f_t":
                        for k in range(KT):
                            dve.wait_ge(scaled, b * KT + k + 1)
                            dve.wait_ge(turned, b * KT + k + 1)
                            dve.tensor_copy(ht_hi[:, k, :], ht[:, k, :]).then_inc(hi_done, 1)
                    elif name in ("w1", "f_w1"):
                        n, rows = b * NT + i, tile_rows(i)
                        dve.wait_ge(loaded, 16 * loads)
                        dve.wait_ge(gate_done, n + 1)
                        if not (isinstance(b, int) and b == 0 and i < 2):
                            dve.wait_ge(lower_done, b * (NT - 1) + max(i - 1, 0))
                        dve.scalar_tensor_tensor(out=hid[0:rows, i % 2, :], in0=AB[i % 2][0][0:rows, :],
                                                 scalar=b1[0:rows, 0, i:i + 1], in1=gate[0:rows, i % 2, :],
                                                 op0=ALU.add, op1=ALU.mult).then_inc(hid_done, 1)
                    elif name in ("h", "f_h") and i == NT - 1:
                        rows = tile_rows(i)
                        dve.wait_ge(upper_done, b * NT + i + 1)
                        dve.tensor_tensor(hid_lo[0:rows, i, :], hid[0:rows, i % 2, :], hid_hi[0:rows, i, :],
                                          ALU.subtract).then_inc(last_lower, 1)
                    elif name == "w2":
                        dve.wait_ge(xb_done, b + 1)
                        if not last:
                            dve.wait_ge(stored, b * 16)
                        else:
                            dve.wait_ge(out_done, b * TB)
                        for t in range(TB):
                            dve.wait_ge(w2_full, b * TB + t + 1)
                            dve.tensor_tensor(y[:, t, :], WB[t % 2][:, 0:DM], xr[:, t, :], ALU.add)\
                                .then_inc(y_done, 1)
                        if last:
                            for t in range(TB):
                                dve.wait_ge(y_done, b * TB + t + 1)
                                dve.bn_stats(st2[:, t, :], y[:, t, :]).then_inc(stats2, 1)
                            for t in range(TB):
                                wait_apart(dve, K, stats2, b * TB + t + 1)
                                m = dve.bn_aggr(mv2[:, t, :], st2[:, t, :])
                            m.then_inc(var2_done, 1)
                    elif name == "fin" and last:
                        dve.wait_ge(rstd2_done, 2 * b + 2)
                        dve.wait_ge(stored, b * 16)
                        for t in range(TB):
                            dve.tensor_scalar(out[:, t, :], y[:, t, :], mv2[:, t, 0:1], rs2[:, t:t + 1],
                                              ALU.subtract, ALU.mult).then_inc(out_done, 1)
                    elif name == "xr" and last:
                        dve.wait_ge(xr_in, b * 16 + 16)
                        dve.wait_ge(res_in, b * 16 + 16)
                        dve.tensor_tensor(xr[:, :, :], xr[:, :, :], res[:, :, :], ALU.add).then_inc(res_done, 1)

                steps(dve, do)

            @block.tensor
            def _(pe):
                def split_mm(o, a_hi, a_lo, r_hi, r_lo, first, last):
                    pe.matmul(o, a_hi, r_hi, start=first, stop=False)
                    pe.matmul(o, a_lo, r_hi, start=False, stop=False)
                    return pe.matmul(o, a_hi, r_lo, start=False, stop=last)

                def do(name, i, b):
                    if name == "f_t":
                        pe.wait_ge(normed, b * TB + TB)
                        for k in range(KT):
                            if not isinstance(b, int):
                                pe.wait_ge(scaled, b * KT + k - 1)
                            for t in range(TB):
                                m = pe.transpose(FB[k][:, P * t:P * t + P], hn[:, t, P * k:P * k + P],
                                                 K["ident"][:, :])
                            m.then_inc(turned, 1)
                    elif name in ("w1", "f_w1"):
                        rows = tile_rows(i)
                        if i == 0:
                            pe.wait_ge(w_lo_done, 2)
                            pe.wait_ge(lo_done, b * KT + KT)
                        pe.wait_ge(hid_done, b * NT + max(i - 1, 0))
                        for k in range(2):
                            col = slice(HID * k + HT * i, HID * k + HT * i + rows)
                            for f in range(KT):
                                m = split_mm(AB[i % 2][k][0:rows, :], w_hi[:, f, col], w_lo[:, f, col],
                                             ht_hi[:, f, :], ht_lo[:, f, :], f == 0, f == KT - 1)
                        m.then_inc(ag_full, 1)
                    elif name == "w2":
                        pe.wait_ge(w2_split, 3)
                        for t in range(TB):
                            pe.wait_ge(y_done, b * TB + max(t - 1, 0))
                            tok = slice(P * t, P * t + P)
                            for n in range(NT):
                                if t == 0 and n < NT - 1:
                                    pe.wait_ge(lower_done, b * (NT - 1) + n + 1)
                                elif t == 0:
                                    pe.wait_ge(last_lower, b + 1)
                                r = slice(0, tile_rows(n))
                                m = split_mm(WB[t % 2][:, 0:DM], hid_hi[r, n, tok], hid_lo[r, n, tok],
                                             w2_hi[r, n, :], w2_lo[r, n, :], n == 0, n == NT - 1)
                            m.then_inc(w2_full, 1)

                steps(pe, do)


def rotary():
    half = np.arange(0, FD, 2, dtype=np.float32)
    inv_freq = (np.float32(1.0) / np.float32(10000.0) ** (half / np.float32(FD))).astype(np.float32)
    t = np.arange(S, dtype=np.float32)
    freqs = t[:, None] * inv_freq[None, :]
    freqs = np.concatenate([freqs, freqs], -1)
    base = (half + np.float32(0.4 * FD)) / np.float32(1.4 * FD)
    power = (t - np.float32(S // 2)) / np.float32(P // 2)
    scale = base[None, :].astype(np.float64) ** power[:, None].astype(np.float64)
    scale = np.concatenate([scale, scale], -1)
    cos, sin = np.cos(freqs.astype(np.float64)), np.sin(freqs.astype(np.float64))
    return np.stack([np.stack([cos * scale, sin * scale]), np.stack([cos / scale, sin / scale])]).astype(np.float32)


NAMES = ["L0_attn_x", "L0_attn_w_qkv", "L0_attn_b_qkv", "L0_attn_w_out", "L0_attn_b_out", "L0_ffn_wqkv",
         "L0_ffn_q_scale", "L0_ffn_k_scale", "L0_ffn_wo", "L0_ffn_ln_g", "L0_ffn_ln_b", "L0_ffn_w1", "L0_ffn_b1",
         "L0_ffn_w2", "L0_ffn_b2", "rot"]


def program(nc, t, out):
    dram = lambda name, shape: nc.dram_tensor(name, shape, F32, kind="Internal").ap()
    scr = dram("qk_parts", [NB, 2, 4 * P, S])
    after_first = dram("after_first", [NB, S + 1, DM])
    after_attn = [dram(f"after_attn{i}", [NB, S + 1, DM]) for i in range(DEPTH)]
    after_layer = dram("after_layer", [NB, S + 1, DM])
    with ExitStack() as ctx:
        K = constants(nc, ctx)
        zero = ctx.enter_context(nc.sbuf_tensor("zero_row", [NB, DM], F32))
        zero_set = ctx.enter_context(nc.semaphore("zero_set"))
        zero_out = ctx.enter_context(nc.semaphore("zero_out"))
        with nc.Block() as block:
            @block.vector
            def _(dve):
                dve.memset(zero[:, :], 0.0).then_inc(zero_set, 1)

            @block.sync
            def _(sp):
                sp.wait_ge(zero_set, 1)
                for a in after_attn:
                    sp.dma_start(a[:, 0, :], zero[:, :]).then_inc(zero_out, 16)
                sp.wait_ge(zero_out, 16 * DEPTH)

        first_attention(nc, K, scr, t["L0_attn_x"], t["L0_attn_w_qkv"], t["L0_attn_b_qkv"], t["L0_attn_w_out"],
                        t["L0_attn_b_out"], after_first)
        x = after_first
        for i in range(DEPTH):
            local_attention(nc, K, i, x[:, 1:], t["L0_ffn_wqkv"][i], t["L0_ffn_q_scale"][i],
                            t["L0_ffn_k_scale"][i], t["L0_ffn_wo"][i], t["rot"], after_attn[i])
            last = i == DEPTH - 1
            feed_forward(nc, K, i, after_attn[i], t["L0_ffn_ln_g"][i], t["L0_ffn_ln_b"][i], t["L0_ffn_w1"][i],
                         t["L0_ffn_b1"][i], t["L0_ffn_w2"][i], t["L0_ffn_b2"][i], after_first if last else None,
                         out if last else after_layer[:, 1:])
            x = after_layer


def kernel(**inputs):
    import concourse.bacc as bacc
    from concourse.bass_utils import run_bass_kernel_spmd

    nc = bacc.Bacc("TRN2", target_bir_lowering=False, num_devices=1)
    arrays = {f"in_{n}": np.ascontiguousarray(rotary() if n == "rot" else inputs[n]) for n in NAMES}
    t = {n: nc.dram_tensor(f"in_{n}", arrays[f"in_{n}"].shape, F32, kind="ExternalInput").ap() for n in NAMES}
    out = nc.dram_tensor("out", [NB, S, DM], F32, kind="ExternalOutput").ap()
    program(nc, t, out)
    return run_bass_kernel_spmd(nc, [arrays], core_ids=[0]).results[0]["out"]
```
